# Optimizing a Trainium2 kernel written in Bass

```python
import numpy as np
import jax
import jax.numpy as jnp

def _softmax(x, axis=-1):
    return jax.nn.softmax(x, axis=axis)

def _gelu(x):
    return jax.nn.gelu(x, approximate=True)

def _silu(x):
    return jax.nn.silu(x)

def _sigmoid(x):
    return jax.nn.sigmoid(x)

def _layernorm(x, axis=-1, eps=1e-05):
    m = jnp.mean(x, axis=axis, keepdims=True)
    v = jnp.var(x, axis=axis, keepdims=True)
    return (x - m) / jnp.sqrt(v + eps)

def _scatter_add(tgt, idx, src, axis=0):
    return tgt.at[idx].add(src)

def _segment_sum(src, seg, n):
    return jax.ops.segment_sum(src, seg, n)
kernel_name = 'mk_audio_tower_d1_tok_audfeat512_r4_549df8'

def setup_inputs(seed: int=0):
    np.random.seed(seed)
    _w = jnp.asarray

    def _rec_inputs():
        import jax
        import jax.numpy as jnp
        _rk = jax.random.key(seed)
        x = -0.000153849 + 1.00027 * jax.random.normal(jax.random.fold_in(_rk, 1), (32, 1024, 48), jnp.float32)
        return x
    x = _rec_inputs()

    def _L0_tok_setup():
        import jax, jax.numpy as jnp
        import numpy as np
        HIDDEN = 128
        PATCH_T = 8
        MAX_CHANNELS = 64
        PER_CHANNEL_DIM = 8

        def sinusoidal_1d(T, D, dtype=jnp.float32):
            pos = jnp.arange(T, dtype=jnp.float32)[:, None]
            i = jnp.arange(D // 2, dtype=jnp.float32)[None, :]
            inv_freq = jnp.exp(-(2.0 * i / D) * jnp.log(10000.0))
            ang = pos * inv_freq
            pe = jnp.stack([jnp.sin(ang), jnp.cos(ang)], axis=-1).reshape(T, D)
            return pe.astype(dtype)
        key = jax.random.key(seed)
        k1, k2, k3, k4, k5 = jax.random.split(key, 5)
        B, T_raw, C = (32, 1024, 48)
        series = jax.random.normal(k1, (B, T_raw, C), dtype=jnp.float32)
        chan_w = 0.02 * jax.random.normal(k2, (MAX_CHANNELS, PER_CHANNEL_DIM), dtype=jnp.float32)
        chan_b = 0.02 * jax.random.normal(k3, (MAX_CHANNELS, PER_CHANNEL_DIM), dtype=jnp.float32)
        conv_w = 0.02 * jax.random.normal(k4, (HIDDEN, MAX_CHANNELS * PER_CHANNEL_DIM, PATCH_T), dtype=jnp.float32)
        marker = 0.02 * jax.random.normal(k5, (HIDDEN,), dtype=jnp.float32)
        return {'series': series, 'chan_w': chan_w, 'chan_b': chan_b, 'conv_w': conv_w, 'marker': marker}
    _L0_tok_all = _L0_tok_setup()
    _L0_tok_in = {k: v for k, v in _L0_tok_all.items() if k in ('chan_w', 'chan_b', 'conv_w', 'marker')}
    del _L0_tok_all

    def _L0_attn_setup():
        import jax, jax.numpy as jnp
        import numpy as np
        B, L, C = (4, 512, 128)
        H = 8
        HD = C // H

        def _rope_tables(seq_len, dim, dtype):
            inv_freq = 1.0 / 10000.0 ** (jnp.arange(0, dim, 2, dtype=jnp.float32) / dim)
            pos = jnp.arange(seq_len, dtype=jnp.float32)
            sinusoid = pos[:, None] * inv_freq[None, :]
            sin = jnp.sin(sinusoid).astype(dtype)[None, :, None, :]
            cos = jnp.cos(sinusoid).astype(dtype)[None, :, None, :]
            return (cos, sin)

        def _rotate_half(x):
            x1, x2 = jnp.split(x, 2, axis=-1)
            return jnp.concatenate([-x2, x1], axis=-1)
        key = jax.random.key(seed)
        ks = jax.random.split(key, 5)
        s = 0.02
        return {'x': jax.random.normal(ks[0], (B, L, C), dtype=jnp.float32), 'qkv_w': jax.random.normal(ks[1], (3 * C, C), dtype=jnp.float32) * s, 'qkv_b': jax.random.normal(ks[2], (3 * C,), dtype=jnp.float32) * s, 'out_w': jax.random.normal(ks[3], (C, C), dtype=jnp.float32) * s, 'out_b': jax.random.normal(ks[4], (C,), dtype=jnp.float32) * s}
    _L0_attn_all = _L0_attn_setup()
    _L0_attn_in = {k: v for k, v in _L0_attn_all.items() if k in ('qkv_w', 'qkv_b', 'out_w', 'out_b')}
    del _L0_attn_all

    def _L0_ffn_setup():
        import jax, jax.numpy as jnp
        import numpy as np
        B, T, D = (4, 512, 128)
        E, H, K = (8, 128, 2)
        key = jax.random.key(seed)
        ks = jax.random.split(key, 8)
        s_in = 1.0 / np.sqrt(D)
        s_h = 1.0 / np.sqrt(H)
        return {'x': jax.random.normal(ks[0], (B, T, D), dtype=jnp.float32), 'Wg': jax.random.uniform(ks[1], (D, E), jnp.float32, -s_in, s_in), 'bg': jax.random.uniform(ks[2], (E,), jnp.float32, -s_in, s_in), 'W1': jax.random.uniform(ks[3], (E, D, H), jnp.float32, -s_in, s_in), 'b1': jax.random.uniform(ks[4], (E, H), jnp.float32, -s_in, s_in), 'W2': jax.random.uniform(ks[5], (E, H, H), jnp.float32, -s_h, s_h), 'b2': jax.random.uniform(ks[6], (E, H), jnp.float32, -s_h, s_h)}
    _L0_ffn_all = _L0_ffn_setup()
    _L0_ffn_in = {k: v for k, v in _L0_ffn_all.items() if k in ('Wg', 'bg', 'W1', 'b1', 'W2', 'b2')}
    del _L0_ffn_all
    return {'x': x, 'L0_tok_chan_w': _L0_tok_in['chan_w'], 'L0_tok_chan_b': _L0_tok_in['chan_b'], 'L0_tok_conv_w': _L0_tok_in['conv_w'], 'L0_tok_marker': _L0_tok_in['marker'], 'L0_attn_qkv_w': _L0_attn_in['qkv_w'], 'L0_attn_qkv_b': _L0_attn_in['qkv_b'], 'L0_attn_out_w': _L0_attn_in['out_w'], 'L0_attn_out_b': _L0_attn_in['out_b'], 'L0_ffn_Wg': _L0_ffn_in['Wg'], 'L0_ffn_bg': _L0_ffn_in['bg'], 'L0_ffn_W1': _L0_ffn_in['W1'], 'L0_ffn_b1': _L0_ffn_in['b1'], 'L0_ffn_W2': _L0_ffn_in['W2'], 'L0_ffn_b2': _L0_ffn_in['b2']}

def reference(x, L0_tok_chan_w, L0_tok_chan_b, L0_tok_conv_w, L0_tok_marker, L0_attn_qkv_w, L0_attn_qkv_b, L0_attn_out_w, L0_attn_out_b, L0_ffn_Wg, L0_ffn_bg, L0_ffn_W1, L0_ffn_b1, L0_ffn_W2, L0_ffn_b2):
    import jax
    import jax.numpy as jnp

    def _L0_tok_ref(series, chan_w, chan_b, conv_w, marker):
        import jax, jax.numpy as jnp
        import numpy as np
        HIDDEN = 128
        PATCH_T = 8
        MAX_CHANNELS = 64
        PER_CHANNEL_DIM = 8

        def sinusoidal_1d(T, D, dtype=jnp.float32):
            pos = jnp.arange(T, dtype=jnp.float32)[:, None]
            i = jnp.arange(D // 2, dtype=jnp.float32)[None, :]
            inv_freq = jnp.exp(-(2.0 * i / D) * jnp.log(10000.0))
            ang = pos * inv_freq
            pe = jnp.stack([jnp.sin(ang), jnp.cos(ang)], axis=-1).reshape(T, D)
            return pe.astype(dtype)
        B, T_raw, C = series.shape
        if C < MAX_CHANNELS:
            series = jnp.pad(series, ((0, 0), (0, 0), (0, MAX_CHANNELS - C)))
        emb = series[..., None] * chan_w[None, None] + chan_b[None, None]
        if C < MAX_CHANNELS:
            mask = (jnp.arange(MAX_CHANNELS) < C).astype(emb.dtype)
            emb = emb * mask[None, None, :, None]
        flat = emb.reshape(B, T_raw, MAX_CHANNELS * PER_CHANNEL_DIM)
        if T_raw % PATCH_T != 0:
            pad_t = PATCH_T - T_raw % PATCH_T
            flat = jnp.pad(flat, ((0, 0), (0, pad_t), (0, 0)))
        T_pad = flat.shape[1]
        T_token = T_pad // PATCH_T
        patches = flat.reshape(B, T_token, PATCH_T, MAX_CHANNELS * PER_CHANNEL_DIM)
        z = jnp.einsum('btpc,ocp->bto', patches, conv_w)
        z = z + sinusoidal_1d(T_token, HIDDEN, z.dtype)[None]
        mark = jnp.broadcast_to(marker.astype(z.dtype), (B, 1, HIDDEN))
        return jnp.concatenate([mark, z], axis=1)

    def _L0_attn_ref(x, qkv_w, qkv_b, out_w, out_b):
        import jax, jax.numpy as jnp
        import numpy as np
        B, L, C = (4, 512, 128)
        H = 8
        HD = C // H

        def _rope_tables(seq_len, dim, dtype):
            inv_freq = 1.0 / 10000.0 ** (jnp.arange(0, dim, 2, dtype=jnp.float32) / dim)
            pos = jnp.arange(seq_len, dtype=jnp.float32)
            sinusoid = pos[:, None] * inv_freq[None, :]
            sin = jnp.sin(sinusoid).astype(dtype)[None, :, None, :]
            cos = jnp.cos(sinusoid).astype(dtype)[None, :, None, :]
            return (cos, sin)

        def _rotate_half(x):
            x1, x2 = jnp.split(x, 2, axis=-1)
            return jnp.concatenate([-x2, x1], axis=-1)
        b, l, c = x.shape
        hd = c // H
        qkv = x @ qkv_w.T + qkv_b
        q, k, v = jnp.split(qkv, 3, axis=-1)
        q = q.reshape(b, l, H, hd)
        k = k.reshape(b, l, H, hd)
        v = v.reshape(b, l, H, hd)
        cos, sin = _rope_tables(l, hd, x.dtype)
        q1, q2 = (q[..., :hd // 2], q[..., hd // 2:])
        k1, k2 = (k[..., :hd // 2], k[..., hd // 2:])
        q1r = q1 * cos + _rotate_half(q1) * sin
        k1r = k1 * cos + _rotate_half(k1) * sin
        q2r = q2 * cos + _rotate_half(q2) * sin
        k2r = k2 * cos + _rotate_half(k2) * sin
        q = jnp.concatenate([q1r, q2r], axis=-1)
        k = jnp.concatenate([k1r, k2r], axis=-1)
        scale = 1.0 / jnp.sqrt(jnp.asarray(hd, dtype=x.dtype))
        scores = jnp.einsum('bqhd,bkhd->bhqk', q, k) * scale
        weights = jax.nn.softmax(scores, axis=-1)
        attn = jnp.einsum('bhqk,bkhd->bqhd', weights, v).reshape(b, l, c)
        return attn @ out_w.T + out_b

    def _L0_ffn_ref(x, Wg, bg, W1, b1, W2, b2):
        import jax, jax.numpy as jnp
        import numpy as np
        B, T, D = (4, 512, 128)
        E, H, K = (8, 128, 2)
        Bx, Tx, Dx = x.shape
        xf = x.reshape(-1, Dx)
        logits = xf @ Wg + bg
        topk_scores, topk_idx = jax.lax.top_k(logits, K)
        topk_w = jax.nn.softmax(topk_scores, axis=-1)
        h = jax.nn.gelu(jnp.einsum('nd,edh->neh', xf, W1) + b1, approximate=False)
        y = jnp.einsum('neh,ehf->nef', h, W2) + b2
        sel = jnp.take_along_axis(y, topk_idx[:, :, None], axis=1)
        out = jnp.sum(topk_w[:, :, None] * sel, axis=1)
        return out.reshape(Bx, Tx, -1)
    h = _L0_tok_ref(x, L0_tok_chan_w, L0_tok_chan_b, L0_tok_conv_w, L0_tok_marker)
    h = h + _L0_attn_ref(_layernorm(h, axis=-1), L0_attn_qkv_w, L0_attn_qkv_b, L0_attn_out_w, L0_attn_out_b)
    h = h + _L0_ffn_ref(_layernorm(h, axis=-1), L0_ffn_Wg, L0_ffn_bg, L0_ffn_W1, L0_ffn_b1, L0_ffn_W2, L0_ffn_b2)
    return h

_drawn_inputs = setup_inputs


def setup_inputs(seed=0):
    import zlib

    import numpy as np

    out = dict(_drawn_inputs(seed))
    spreads = {}
    factors = {'L0_tok_marker': 15.528, 'L0_attn_qkv_b': 4.154, 'L0_ffn_b1': 3.086}
    for name, (base, spread) in spreads.items():
        noise = np.random.default_rng([zlib.crc32(name.encode()), seed]).standard_normal(out[name].shape)
        drawn = base * np.exp(spread * noise) if base else spread * noise
        out[name] = jnp.asarray(drawn.astype(out[name].dtype))
    for name, factor in factors.items():
        out[name] = (out[name] * factor).astype(out[name].dtype)
    return out
```

```python
from contextlib import ExitStack

import numpy as np

import concourse.bass as bass
from concourse import mybir

ALU = mybir.AluOpType
ACT = mybir.ActivationFunctionType
F32 = mybir.dt.float32
F32R = mybir.dt.float32r
AX = mybir.AxisListType

P = 128
BATCH, T_RAW, CHANS = 32, 1024, 48
PATCH, PER_CHAN, MAX_CHANS = 8, 8, 64
TOKENS = T_RAW // PATCH
HID = 128
HEADS, HD = 8, 16
EXPERTS = 8
KCH = PATCH * CHANS // P
GB = 4
GROUPS = BATCH // GB
GT = GB * TOKENS
TILES = BATCH + 1
MT = BATCH
EPS = 1e-5
SCALE = HD ** -0.5
XSLOTS = 4

COLS = {}


def _columns():
    at = 0
    for name, n in (("wg", EXPERTS), ("pe", HID), ("cos", TOKENS), ("sin", TOKENS), ("ident", P), ("headmask", HEADS),
                    ("headrows", P), ("rank", EXPERTS), ("cw", KCH * PER_CHAN), ("cb", KCH * PER_CHAN),
                    ("marker", HID), ("bias", 5), ("ob", HID), ("bg", EXPERTS),
                    ("b1", EXPERTS), ("parity", 2), ("low_key", 1), ("hide_high", 1)):
        COLS[name] = (at, n)
        at += n
    return at


NCOLS = _columns()


def audio_tower_kernel(nc, xt, convw, consts, wqkv, wo, w1, w2, b2bd, out):
    parts_dram = nc.dram_tensor("parts_dram", [GROUPS, 2, HEADS, 2, HD, GT], F32).ap()
    ctx = ExitStack()
    with ctx:
        def sb(name, shape, dt=F32):
            return ctx.enter_context(nc.sbuf_tensor(name, shape, dt))

        def sem(name):
            return ctx.enter_context(nc.semaphore(name))

        cst = sb("cst", [P, NCOLS])

        def const(name):
            at, n = COLS[name]
            return cst[:, at:at + n]

        conv_sb = sb("conv_sb", [P, KCH, PER_CHAN, HID])
        weff = sb("weff", [P, KCH, HID])
        cbw = sb("cbw", [P, KCH, HID])
        ones = sb("ones", [P, P])
        pe_bias = sb("pe_bias", [P, HID])
        x_sb = sb("x_sb", [P, XSLOTS, KCH, GT])
        h = sb("h", [P, TILES, HID])
        stats = sb("stats", [P, TILES, 6])
        ln_tmp = sb("ln_tmp", [P, 6, TILES])
        rstd = sb("rstd", [P, TILES])
        shift = sb("shift", [P, TILES])
        wqkv_sb = sb("wqkv_sb", [P, 5, HID])
        wo_sb = sb("wo_sb", [P, HID])
        ident_r = sb("ident_r", [P, 3, P], F32R)
        xn = sb("xn", [P, 2, GB, HID])
        xnT = sb("xnT", [P, 2, GT])
        xnT_m = sb("xnT_m", [P, 1])
        rope_a = sb("rope_a", [P, 2, GB, TOKENS])
        rope_b = sb("rope_b", [P, 2, GB, TOKENS])
        q32 = sb("q32", [P, 2, GB, TOKENS])
        k_all = sb("k_all", [P, BATCH, TOKENS])
        v_all = sb("v_all", [P, BATCH, HID])
        split = sb("split", [P, 4, GT], F32R)
        q_stack = [sb(f"q_stack{s}", [P, HEADS, GB, TOKENS], F32R) for s in range(2)]
        KB = HEADS // 2 * GB
        k_zeros = [sb(f"k_stack{s}", [P, KB + 2, TOKENS], F32R) for s in range(2)]
        k_stack = [t[:, 1:KB + 1, :].rearrange("p (r b) t -> p r b t", b=GB) for t in k_zeros]
        v_fix = sb("v_fix", [P, 2, GB, HID])
        smk_sb = sb("smk_sb", [P, 2, GB, HEADS])
        negmax = sb("negmax", [P, 2, HEADS])
        negm = [sb(f"negm{s}", [P, P], F32R) for s in range(2)]
        probs = sb("probs", [P, 2, HEADS, TOKENS])
        pmk = sb("pmk", [P, 2, TOKENS])
        pmk_hid = sb("pmk_hid", [P, 2, TOKENS], F32R)
        pmk_parts = sb("pmk_parts", [P, 2, TOKENS], F32R)
        attT = sb("attT", [P, 2, GB, 2, TOKENS])
        wo_head = sb("wo_head", [P, 2, HID])
        obias = sb("obias", [P, HID])
        qm = sb("qm", [P, 2])
        km_pad = sb("km_pad", [P, P])
        qm_shift = sb("qm_shift", [P, 2 * 120 + HEADS])
        vm_heads, bv_wide = cbw[:, 0, :], cbw[:, 1, :]
        qm_tiled = cbw[:, 2, :].rearrange("p (a h) -> p a h", h=HEADS)
        vm_row = sb("vm_row", [1, HID])
        vm_hid = sb("vm_hid", [P, HID], F32R)
        vm_parts = sb("vm_parts", [P, HID], F32R)
        one_parts = sb("one_parts", [P, HID], F32R)
        mq = sb("mq", [P, 2, 4])
        pmm = sb("pmm", [1, 2, P])
        attT_m = sb("attT_m", [P, BATCH])
        conv_flat = conv_sb[:, :, :, :].rearrange("p a b c -> p (a b c)")
        w1_sb = conv_flat[:, 0:EXPERTS * HID].rearrange("p (e n) -> p e n", e=EXPERTS)
        w2_sb = conv_flat[:, EXPERTS * HID:2 * EXPERTS * HID].rearrange("p (e n) -> p e n", e=EXPERTS)
        b2_sb = conv_flat[:, 2 * EXPERTS * HID:(2 * EXPERTS + GB) * HID].rearrange("p (b n) -> p b n", b=GB)
        rec = x_sb[:, XSLOTS - 1, 0, :].rearrange("p (s n) -> p s n", s=2)
        x_flat = x_sb[:, :, :, :].rearrange("p a b c -> p (a b c)")
        x2T = x_flat[:, 0:TILES * P]
        pmq = x_flat[:, 0:2 * (P + 1)].rearrange("p (a n) -> p a n", a=2)
        pmqT = x_flat[:, 3 * P:5 * P].rearrange("p (a n) -> p a n", a=2)
        mq_sel = x_flat[:, 5 * P:5 * P + BATCH * HEADS].rearrange("p (b h) -> p b h", b=BATCH)
        TE = TILES * EXPERTS
        at = TILES * P
        logits = x_flat[:, at:at + TE].rearrange("p (n e) -> p n e", n=TILES)
        gate = x_flat[:, at + TE:at + 2 * TE].rearrange("p (n e) -> p n e", n=TILES)
        gt = x_flat[:, at + 2 * TE:at + 6 * TE].rearrange("p (a n e) -> p a n e", a=4, n=TILES)
        gs = x_flat[:, at + 6 * TE:at + 7 * TE].rearrange("p (a n) -> p a n", a=8)
        hid = probs[:, :, :, :].rearrange("p a b c -> p a (b c)")[:, :, 0:GT]
        wgrp = pe_bias[:, 0:2 * GB * EXPERTS].rearrange("p (s n) -> p s n", s=2)
        wgrpT = sb("wgrpT", [P, P])

        banks = ctx.enter_context(nc.psum_tensor("banks", [P, 8, 512], F32))

        def bank(n, k=1):
            return banks[:, n:n + k, :].rearrange("p a b -> p (a b)")

        consts_in = sem("consts_in")
        conv_in = sem("conv_in")
        weights_in = sem("weights_in")
        ffn_in = sem("ffn_in")
        x_in = [sem(f"x_in{s}") for s in range(XSLOTS)]
        memsets_done = sem("memsets_done")
        pool_memsets = sem("pool_memsets")
        dve_chain = sem("dve_chain")
        pool_chain = sem("pool_chain")
        pool_held = sem("pool_held")
        sp_held = sem("sp_held")
        act_chain = sem("act_chain")
        bias_sum = sem("bias_sum")
        setup_xn = sem("setup_xn")
        stats_done = sem("stats_done")
        rope_summed = sem("rope_summed")
        rope_high = sem("rope_high")
        row_max = sem("row_max")
        pe_bias_done = sem("pe_bias_done")
        weff_done = sem("weff_done")
        tok_done = sem("tok_done")
        h_done = sem("h_done")
        var_done = sem("var_done")
        std_done = sem("std_done")
        rstd_done = sem("rstd_done")
        xn_done = sem("xn_done")
        ready = {k: sem(f"{k}_ready") for k in ("xnT", "q", "qp", "k", "kp", "v", "smk", "out")}
        taken = {k: sem(f"{k}_taken") for k in ("xnT", "q", "qp", "k", "kp", "v", "smk", "out")}
        setup_ready = sem("setup_ready")
        setup_taken = sem("setup_taken")
        marker_set = sem("marker_set")
        ident_r_done = sem("ident_r_done")
        q_split = sem("q_split")
        k_split = sem("k_split")
        v_kept = sem("v_kept")
        pmk_split = sem("pmk_split")
        rec_done = sem("rec_done")
        h_biased = sem("h_biased")
        parts_out = [sem(f"parts_out{s}") for s in range(2)]
        q_stacked = [sem(f"q_stacked{s}") for s in range(2)]
        k_stacked = [sem(f"k_stacked{s}") for s in range(2)]
        max_scored = sem("max_scored")
        negm_done = sem("negm_done")
        scored = sem("scored")
        exp_done = sem("exp_done")
        pv_done = sem("pv_done")
        norm_done = sem("norm_done")
        mq_step = sem("mq_step")
        mq_max = sem("mq_max")
        mq_exp = sem("mq_exp")
        mq_norm = sem("mq_norm")
        mq_copied = sem("mq_copied")
        mq_att = sem("mq_att")
        x2n_done = sem("x2n_done")
        x2t_ready = sem("x2t_ready")
        x2t_taken = sem("x2t_taken")
        x2_kept = sem("x2_kept")
        logits_ready = sem("logits_ready")
        logits_taken = sem("logits_taken")
        gap_done = sem("gap_done")
        gap_exp = sem("gap_exp")
        gate_done = sem("gate_done")
        wgrp_done = sem("wgrp_done")
        wT_ready = sem("wT_ready")
        wT_taken = sem("wT_taken")
        b2_ready = sem("b2_ready")
        b2_taken = sem("b2_taken")
        hid_ready = sem("hid_ready")
        gelu_done = sem("gelu_done")
        y_ready = sem("y_ready")
        y_taken = sem("y_taken")
        stored = sem("stored")

        H = P // 2
        NQ, NK = 8, 4

        block = ctx.enter_context(nc.Block())

        def groups(eng, step):
            step(0, 0)
            with eng.Fori(1, GROUPS - 2, 2) as g:
                step(g, 1)
                step(g + 1, 0)
            step(GROUPS - 1, 1)

        @block.sync
        def _(sp):
            sp.dma_start(cst[:, :], consts).then_inc(consts_in, 16)
            sp.dma_start(conv_sb[:, :, :, :], convw).then_inc(conv_in, 16)
            for g in range(XSLOTS):
                sp.dma_start(x_sb[:, g, :, :], xt[g]).then_inc(x_in[g], 16)
            sp.dma_start(wqkv_sb[:, :, :], wqkv).then_inc(weights_in, 16)
            sp.dma_start(wo_sb[:, :], wo).then_inc(weights_in, 16)
            for g in range(XSLOTS, GROUPS):
                sp.wait_ge(tok_done, g - XSLOTS + 1)
                sp.dma_start(x_sb[:, g - XSLOTS, :, :], xt[g]).then_inc(x_in[g - XSLOTS], 16)
            sp.wait_ge(weff_done, 2)
            sp.dma_start(w1_sb[:, :, :], w1).then_inc(ffn_in, 16)
            sp.dma_start(w2_sb[:, :, :], w2).then_inc(ffn_in, 16)
            sp.dma_start(b2_sb[:, :, :], b2bd).then_inc(ffn_in, 16)
            sp.wait_ge(pool_memsets, 2)

            def put(which, g):
                for part in range(2):
                    dst = parts_dram[bass.ds(g, 1), which].rearrange("g h a d n -> g a h d n")[0, part]
                    sp.dma_start(dst, split[:, 2 * which + part, :].bitcast(F32)).then_inc(parts_out[which], 16)

            def stack_q(g, s):
                for e in range(2):
                    for j in range(4):
                        row = P // 2 * e + HD * j
                        src = parts_dram[bass.ds(g, 1), 0].rearrange(
                            "g (r e) a d n -> g e a d r n", e=2)[0, e, j // 2]
                        dst = q_stack[s][row:row + HD, e:HEADS:2, :, :].rearrange("p r b t -> p r (b t)")
                        sp.dma_start(dst.bitcast(F32), src).then_inc(q_stacked[s], 16)

            def stack_k(g, s):
                for e in range(2):
                    src = parts_dram[bass.ds(g, 1), 1].rearrange("g (r e) a d n -> g e (a d) r n", e=2)[0, e]
                    for j in range(2):
                        row = P // 2 * e + 2 * HD * j
                        dst = k_stack[s][row:row + 2 * HD, :, :, :].rearrange("p r b t -> p r (b t)")
                        sp.dma_start(dst.bitcast(F32), src).then_inc(k_stacked[s], 16)

            def hold(signal, value):
                sp.wait_ge(signal, value)
                if not isinstance(value, int):
                    sp.sem_inc(sp_held, 1)

            def stage_a(g, s, prev):
                hold(q_split, g + 1)
                put(0, g)
                hold(k_split, g + 1)
                put(1, g)
                if prev:
                    hold(scored, (g - 1) * GB)
                hold(parts_out[0], (g + 1) * 32)
                stack_q(g, s)
                hold(parts_out[1], (g + 1) * 32)
                stack_k(g, s)

            stage_a(0, 0, False)
            stage_a(1, 1, False)
            with sp.Fori(2, GROUPS - 1, 2) as g:
                stage_a(g, 0, True)
                stage_a(g + 1, 1, True)

            def store(g):
                sp.wait_ge(y_taken, (g + 1) * EXPERTS)
                sp.dma_start(out[bass.ds(g * GB, GB), 1:TOKENS + 1, :].rearrange("b t c -> t b c"),
                             h[:, bass.ds(g * GB, GB), :]).then_inc(stored, 16)
            with sp.Fori(0, GROUPS, 1) as g:
                store(g)
            sp.wait_ge(y_taken, (GROUPS + 1) * EXPERTS)
            sp.dma_start(out[:, 0, :], h[0:BATCH, MT, :]).then_inc(stored, 16)
            sp.wait_ge(stored, 16 * (GROUPS + 1))

        @block.gpsimd
        def _(pool):
            def hold(signal, value):
                pool.wait_ge(signal, value)
                if not isinstance(value, int):
                    pool.sem_inc(pool_held, 1)

            for s in range(2):
                pool.memset(q_stack[s][:, :, :, :].bitcast(F32), 0.0).then_inc(pool_memsets, 1)
            def stage_a(g, s, first):
                hold(xn_done, g + 1)
                if first:
                    pool.wait_ge(marker_set, 1)
                pool.tensor_tensor(h[:, bass.ds(g * GB, GB), :], h[:, bass.ds(g * GB, GB), :],
                                   obias[:, :].rearrange("p (a n) -> p a n", a=1).to_broadcast([P, GB, HID]),
                                   ALU.add).then_inc(h_biased, 1)
                for which, halves in ((0, ("q", "qp")), (1, ("k", "kp"))):
                    x32 = q32[:, s] if which == 0 else k_all[:, bass.ds(g * GB, GB), :]
                    done = q_split if which == 0 else k_split
                    hi = split[:, 2 * which, :].rearrange("p (b t) -> p b t", b=GB)
                    lo = split[:, 2 * which + 1, :].rearrange("p (b t) -> p b t", b=GB)
                    hold(taken[halves[0]], g + 1)
                    hold(taken[halves[1]], g + 1)
                    if not isinstance(g, int) or g >= 2:
                        if which == 0:
                            hold(scored, (g - 1) * GB)
                    pool.tensor_tensor(x32, rope_a[:, which], rope_b[:, which],
                                       ALU.add).then_inc(rope_summed, 1)
                    hold(rope_summed, 2 * g + which + 1)
                    if not isinstance(g, int) or g >= 1:
                        hold(parts_out[which], g * 32)
                    pool.tensor_copy(hi, x32).then_inc(rope_high, 1)
                    hold(rope_high, 2 * g + which + 1)
                    pool.tensor_tensor(lo, x32, hi, ALU.subtract).then_inc(done, 1)
                hold(taken["v"], g + 1)
                pool.tensor_copy(v_all[:, bass.ds(g * GB, GB), :], v_fix[:, s]).then_inc(v_kept, 1)

            stage_a(0, 0, True)
            stage_a(1, 1, False)
            with pool.Fori(2, GROUPS - 1, 2) as g:
                stage_a(g, 0, False)
                stage_a(g + 1, 1, False)
            def keep(g, s):
                hold(x2t_taken, g + 1)
                pool.tensor_copy(x2T[:, bass.ds(g * GT, GT)], xnT[:, s, :]).then_inc(x2_kept, 1)
            with pool.Fori(0, GROUPS - 1, 2) as g:
                keep(g, 0)
                keep(g + 1, 1)
            pool.wait_ge(x2t_taken, GROUPS + 1)
            pool.tensor_copy(x2T[:, GROUPS * GT:], xnT[:, 0, 0:P]).then_inc(x2_kept, 1)
            pool.wait_ge(gate_done, 1)

            def regroup(g, s):
                if not isinstance(g, int):
                    hold(wT_ready, g - 1)
                pool.tensor_copy(wgrp[:, s, :].rearrange("p (b e) -> p b e", b=GB),
                                 gate[:, bass.ds(g * GB, GB), :]).then_inc(wgrp_done, 1)
            regroup(0, 0)
            regroup(1, 1)
            with pool.Fori(2, GROUPS - 1, 2) as g:
                regroup(g, 0)
                regroup(g + 1, 1)

        @block.scalar
        def _(act):
            act.wait_ge(consts_in, 16)
            act.wait_ge(memsets_done, 1)
            nc.scalar.copy(ident_r[:, 1, :], const("ident")).then_inc(ident_r_done, 1)

            def root(n):
                act.wait_ge(var_done, n)
                nc.scalar.activation(ln_tmp[:, 5, :], ln_tmp[:, 4, :], ACT.Sqrt).then_inc(std_done, 1)

            root(1)

            def take_xnT(g, s):
                act.wait_ge(ready["xnT"], g + 1)
                nc.scalar.copy(xnT[:, s, :], bank(6)).then_inc(taken["xnT"], 1)

            def take_v(g, s):
                act.wait_ge(ready["v"], g + 1)
                if not isinstance(g, int) or g >= 2:
                    act.wait_ge(v_kept, g - 1)
                nc.scalar.copy(v_fix[:, s], bank(7).rearrange("p (b n) -> p b n", b=GB)).then_inc(taken["v"], 1)

            def take_smk(g, s):
                act.wait_ge(ready["smk"], g + 1)
                nc.scalar.copy(smk_sb[:, s], bank(7).rearrange("p (b n) -> p b n", b=GB)[:, :, 0:HEADS]
                               ).then_inc(taken["smk"], 1)

            def exps(n, b, late):
                act.wait_ge(scored, n + 1)
                if late:
                    act.wait_ge(pv_done, n - 1)
                nc.scalar.activation(probs[:, b % 2].rearrange("p h t -> p (h t)"), bank(2, 2),
                                     ACT.Exp, scale=SCALE)
                mk = bank(4 + b % 2)[:, 256:384]
                nc.scalar.activation(pmk[:, b % 2, :], mk, ACT.Exp, scale=SCALE)
                at, _ = COLS["hide_high"]
                nc.scalar.activation(pmk_hid[:, b % 2, :], mk, ACT.Exp, bias=cst[:, at:at + 1],
                                     scale=SCALE).then_inc(exp_done, 1)

            def step(g, s):
                last = isinstance(g, int) and g == GROUPS - 1
                for b in range(GB):
                    if b == 0 and not last:
                        take_xnT(g + 1, 1 - s)
                    exps(g * GB + b, b, not isinstance(g, int) or g * GB + b >= 2)
                    if b == 1 and not last:
                        take_v(g + 1, 1 - s)
                    if b == 2 and not last:
                        take_smk(g + 1, 1 - s)

            take_xnT(0, 0)
            take_v(0, 0)
            take_smk(0, 0)
            groups(act, step)

            for half in range(2):
                act.wait_ge(mq_max, half + 1)
                nc.scalar.activation(pmq[:, half, :], bank(6 + half)[:, 0:P + 1], ACT.Exp,
                                     bias=mq[:, half, 1:2], scale=SCALE,
                                     accum_out=mq[:, half, 2:3]).then_inc(mq_exp, 1)
            root(2)

            def take_x2(g, s):
                act.wait_ge(x2t_ready, g + 1)
                if not isinstance(g, int) or g >= 2:
                    act.wait_ge(x2_kept, g - 1)
                    act.wait_ge(logits_ready, g - 1)
                nc.scalar.copy(xnT[:, s, :], bank(s)).then_inc(x2t_taken, 1)
            take_x2(0, 0)
            take_x2(1, 1)
            with act.Fori(2, GROUPS - 1, 2) as g:
                take_x2(g, 0)
                take_x2(g + 1, 1)
            act.wait_ge(x2t_ready, GROUPS + 1)
            act.wait_ge(x2_kept, GROUPS - 1)
            act.wait_ge(logits_ready, GROUPS - 1)
            nc.scalar.copy(xnT[:, 0, 0:P], bank(0)[:, 0:P]).then_inc(x2t_taken, 1)
            act.wait_ge(gap_done, 1)
            nc.scalar.activation(gs[:, 3, :], gs[:, 2, :], ACT.Exp).then_inc(gap_exp, 1)

            def gelu(n, e, cols, late):
                act.wait_ge(hid_ready, n + 1)
                if late:
                    act.wait_ge(y_ready, n - 1)
                at, _ = COLS["b1"]
                nc.scalar.activation(hid[:, e % 2, 0:cols], bank(e % 2)[:, 0:cols], ACT.Gelu,
                                     bias=cst[:, at + e:at + e + 1]).then_inc(gelu_done, 1)

            def experts(g, first=False):
                for e in range(EXPERTS):
                    gelu(g * EXPERTS + e, e, GT, not first or e >= 2)
                    if e == 1:
                        act.wait_ge(wT_ready, g + 1)
                        if not first:
                            act.wait_ge(b2_ready, g)
                        nc.scalar.copy(wgrpT[0:GB * EXPERTS, :],
                                       bank(5)[0:GB * EXPERTS, 0:P]).then_inc(wT_taken, 1)
            experts(0, True)
            with act.Fori(1, GROUPS, 1) as g:
                experts(g)
            for e in range(EXPERTS):
                gelu(GROUPS * EXPERTS + e, e, BATCH, True)
                if e == 1:
                    act.wait_ge(wT_ready, GROUPS + 1)
                    act.wait_ge(b2_ready, GROUPS)
                    nc.scalar.copy(wgrpT[0:EXPERTS, 0:BATCH],
                                   bank(5)[0:EXPERTS, 0:BATCH]).then_inc(wT_taken, 1)

        @block.vector
        def _(dve):
            v = nc.vector
            links = [0]

            def link(ins):
                links[0] += 1
                ins.then_inc(dve_chain, 1)
                dve.wait_ge(dve_chain, links[0])

            v.memset(ones[:, :], 1.0).then_inc(h_done, 1)
            v.memset(km_pad[:, :], 0.0).then_inc(taken["out"], 1)
            v.memset(qm_shift[:, :], 0.0).then_inc(h_done, 1)
            v.memset(wgrpT[:, :], 0.0)
            for s in range(2):
                v.memset(negm[s][:, :].bitcast(F32), 0.0)
                v.memset(k_zeros[s][:, 0:KB + 2:KB + 1, :].bitcast(F32), 0.0)
            v.memset(ident_r[:, 0:3:2, :].bitcast(F32), 0.0)
            v.memset(h[:, MT, :], 0.0).then_inc(memsets_done, 1)
            dve.wait_ge(memsets_done, 1)
            dve.wait_ge(consts_in, 16)
            dve.wait_ge(conv_in, 16)
            for table, acc in (("cb", cbw), ("cw", weff)):
                at, _ = COLS[table]
                for d in range(PER_CHAN):
                    for j in range(KCH):
                        c = at + j * PER_CHAN + d
                        w = cst[:, c:c + 1]
                        if d == 0:
                            ins = v.tensor_scalar(acc[:, j, :], conv_sb[:, j, d, :], w, None, ALU.mult)
                        else:
                            ins = v.scalar_tensor_tensor(out=acc[:, j, :], in0=conv_sb[:, j, d, :], scalar=w,
                                                         in1=acc[:, j, :], op0=ALU.mult, op1=ALU.add)
                    if d < PER_CHAN - 1:
                        link(ins)
                ins.then_inc(weff_done, 1)
            dve.wait_ge(bias_sum, 1)
            v.tensor_tensor(pe_bias[:, :], bank(2)[:, 0:HID], const("pe"), ALU.add).then_inc(pe_bias_done, 1)
            dve.wait_ge(pe_bias_done, 1)
            at, _ = COLS["marker"]
            link(v.tensor_copy(h[0:BATCH, MT, :], cst[0:BATCH, at:at + HID]))
            link(v.bn_stats(stats[:, MT, :], h[:, MT, :]))

            def grp(t, g):
                return t[:, bass.ds(g * GB, GB), :]

            def tok(g, s):
                dve.wait_ge(tok_done, g + 1)
                v.tensor_tensor(grp(h, g), bank(s).rearrange("p (b n) -> p b n", b=GB),
                                pe_bias[:, :].rearrange("p (a n) -> p a n", a=1).to_broadcast([P, GB, HID]),
                                ALU.add).then_inc(h_done, 1)
                dve.wait_ge(h_done, g + 3)
                for b in range(GB):
                    ins = v.bn_stats(stats[:, bass.ds(g * GB + b, 1), :].rearrange("p a n -> p (a n)"),
                               h[:, bass.ds(g * GB + b, 1), :].rearrange("p a n -> p (a n)"))
                ins.then_inc(stats_done, 1)
            with dve.Fori(0, GROUPS - 1, 2) as g:
                tok(g, 0)
                tok(g + 1, 1)

            norms = [0]

            def layernorm_scales():
                me, se, mo, so = (stats[:, :, c] for c in (1, 2, 4, 5))
                t = [ln_tmp[:, c, :] for c in range(6)]
                v.tensor_tensor(t[0], me, mo, ALU.add)
                v.tensor_tensor(t[1], me, mo, ALU.subtract)
                link(v.tensor_tensor(t[2], se, so, ALU.add))
                link(v.tensor_tensor(t[3], t[1], t[1], ALU.mult))
                link(v.scalar_tensor_tensor(out=t[1], in0=t[3], scalar=float(HID) / 4, in1=t[2],
                                            op0=ALU.mult, op1=ALU.add))
                v.tensor_scalar(t[4], t[1], 1.0 / HID, EPS, ALU.mult, ALU.add).then_inc(var_done, 1)
                norms[0] += 1
                dve.wait_ge(std_done, norms[0])
                link(v.reciprocal(rstd[:, :], t[5]))
                link(v.scalar_tensor_tensor(out=shift[:, :], in0=t[0], scalar=-0.5, in1=rstd[:, :],
                                            op0=ALU.mult, op1=ALU.mult))

            dve.wait_ge(stats_done, GROUPS)
            layernorm_scales()

            def normalize(dst, n):
                return v.tensor_scalar(dst, h[:, bass.ds(n, 1), :].rearrange("p a n -> p (a n)"),
                                       rstd[:, bass.ds(n, 1)], shift[:, bass.ds(n, 1)], ALU.mult, ALU.add)

            normalize(xn[:, 1, 0, :], MT).then_inc(setup_xn, 1)
            dve.wait_ge(setup_ready, 1)
            v.tensor_copy(xnT_m[:, :], bank(3)[:, 0:1]).then_inc(setup_taken, 1)
            bias_at, _ = COLS["bias"]
            v.tensor_scalar(bv_wide[:, :], ones[:, :], cst[:, bias_at + 4:bias_at + 5], None,
                            ALU.mult).then_inc(setup_taken, 1)
            dve.wait_ge(setup_ready, 2)
            v.tensor_tensor(qm[:, 0:1], bank(3)[:, 0:1], cst[:, bias_at:bias_at + 1], ALU.add)
            link(v.tensor_tensor(qm[:, 1:2], bank(3)[:, 1:2], cst[:, bias_at + 2:bias_at + 3], ALU.add))
            v.tensor_scalar(km_pad[:, :].rearrange("p (a n) -> p a n", a=4)[:, :, 0:HEADS],
                            const("headmask").rearrange("p (a h) -> p a h", a=1).to_broadcast([P, 4, HEADS]),
                            qm[:, 1:2], None, ALU.mult)
            v.tensor_scalar(qm_shift[:, 120:120 + HEADS], const("headmask"), qm[:, 0:1], None, ALU.mult)
            v.tensor_scalar(qm_tiled[:, :, :],
                            const("headmask").rearrange("p (a h) -> p a h", a=1).to_broadcast([P, 16, HEADS]),
                            qm[:, 0:1], None, ALU.mult)
            v.tensor_copy(vm_row[:, :], bank(3)[0:1, 128:256])
            at, _ = COLS["low_key"]
            low_key = cst[:, at:at + 1]
            link(v.tensor_tensor(vm_heads[:, :], bank(3)[:, 128:256], const("headrows"), ALU.mult))
            v.scalar_tensor_tensor(out=one_parts[:, :], in0=const("headrows"), scalar=low_key,
                                   in1=const("headrows"), op0=ALU.mult, op1=ALU.subtract)
            link(v.tensor_scalar(vm_hid[:, :], vm_heads[:, :], low_key, None, ALU.mult))
            v.tensor_tensor(vm_parts[:, :], vm_hid[:, :], vm_heads[:, :], ALU.subtract)
            at, _ = COLS["parity"]
            for e in range(2):
                v.tensor_scalar(wo_head[:, e, :], wo_sb[:, :], cst[:, at + e:at + e + 1], None, ALU.mult)
            v.tensor_tensor(obias[:, :], bank(3)[:, 256:384], const("ob"), ALU.add).then_inc(marker_set, 1)
            dve.wait_ge(marker_set, 1)
            v.tensor_tensor(h[0:BATCH, MT, :], h[0:BATCH, MT, :], obias[0:BATCH, :], ALU.add)

            def make_xn(g, s):
                if not isinstance(g, int) or g >= 2:
                    dve.wait_ge(ready["xnT"], g - 1)
                for b in range(GB):
                    ins = normalize(xn[:, s, b, :], g * GB + b)
                ins.then_inc(xn_done, 1)

            def take(name, g):
                c = ("q", "qp", "k", "kp").index(name)
                bank_of = {"q": 7, "qp": 6, "k": 7, "kp": 6}[name]
                table = const("cos" if c % 2 == 0 else "sin")
                dst = (rope_a if c % 2 == 0 else rope_b)[:, c // 2]
                dve.wait_ge(ready[name], g + 1)
                if not isinstance(g, int) or g >= 1:
                    dve.wait_ge(rope_summed, 2 * g - 1 + c // 2)
                v.scalar_tensor_tensor(out=dst, in0=bank(bank_of).rearrange("p (b t) -> p b t", b=GB),
                                       scalar=cst[:, bias_at + c:bias_at + c + 1],
                                       in1=table.rearrange("p (a t) -> p a t", a=1).to_broadcast([P, GB, TOKENS]),
                                       op0=ALU.add, op1=ALU.mult).then_inc(taken[name], 1)

            def negmax_of(n, b, s, smk_ready, late):
                dve.wait_ge(max_scored, n + 1)
                v.tensor_reduce(negmax[:, b % 2, :], bank(0, 2).rearrange("p (h t) -> p h t", h=HEADS),
                                AX.X, ALU.max, negate=True).then_inc(row_max, 1)
                dve.wait_ge(row_max, n + 1)
                if smk_ready is not None:
                    dve.wait_ge(taken["smk"], smk_ready)
                if late:
                    dve.wait_ge(scored, n - 1)
                wide = [t.rearrange("p (a h) -> p a h", a=1).to_broadcast([P, 4, HEADS])
                        for t in (smk_sb[:, s, b, :], negmax[:, b % 2, :])]
                v.scalar_tensor_tensor(out=negm[b % 2][:, :].rearrange("p (a n) -> p a n", a=4)[:, :, 0:HEADS],
                                       in0=wide[0], scalar=-1.0, in1=wide[1], op0=ALU.mult, op1=ALU.min
                                       ).then_inc(negm_done, 1)

            def split_pmk(n, b):
                dve.wait_ge(exp_done, n + 1)
                v.tensor_tensor(pmk_parts[:, b % 2, :], pmk_hid[:, b % 2, :], pmk[:, b % 2, :], ALU.subtract
                                ).then_inc(pmk_split, 1)

            def norm(n, b, s):
                dve.wait_ge(pv_done, n + 1)
                od = bank(4 + b % 2)
                v.reciprocal(rec[:, b % 2, :], od[:, 256:512]).then_inc(rec_done, 1)
                dve.wait_ge(rec_done, n + 1)
                v.tensor_tensor(attT[:, s, b].rearrange("p e t -> p (e t)"), od[:, 0:256], rec[:, b % 2, :],
                                ALU.mult).then_inc(norm_done, 1)

            def take_out(g):
                dve.wait_ge(ready["out"], g + 1)
                dve.wait_ge(h_biased, g + 1)
                v.tensor_tensor(grp(h, g), bank(6).rearrange("p (b n) -> p b n", b=GB), grp(h, g),
                                ALU.add).then_inc(taken["out"], 1)
                dve.wait_ge(taken["out"], g + 2)
                for b in range(GB):
                    ins = v.bn_stats(stats[:, bass.ds(g * GB + b, 1), :].rearrange("p a n -> p (a n)"),
                                     h[:, bass.ds(g * GB + b, 1), :].rearrange("p a n -> p (a n)"))
                ins.then_inc(stats_done, 1)

            make_xn(0, 0)
            for name in ("q", "qp", "k", "kp"):
                take(name, 0)
            make_xn(1, 1)
            negmax_of(0, 0, 0, 1, False)

            def dve_step(g, s):
                static = isinstance(g, int)
                first, last = static and g == 0, static and g == GROUPS - 1
                n = g * GB
                negmax_of(n + 1, 1, s, None, not first)
                split_pmk(n, 0)
                if not last:
                    take("q", g + 1)
                if not first:
                    norm(n - 1, GB - 1, 1 - s)
                if not last:
                    take("qp", g + 1)
                    take("k", g + 1)
                negmax_of(n + 2, 2, s, None, True)
                split_pmk(n + 1, 1)
                if not last:
                    take("kp", g + 1)
                norm(n, 0, s)
                negmax_of(n + 3, 3, s, None, True)
                split_pmk(n + 2, 2)
                if not first:
                    take_out(g - 1)
                norm(n + 1, 1, s)
                if not last:
                    negmax_of(n + 4, 0, 1 - s, g + 2, True)
                split_pmk(n + 3, 3)
                norm(n + 2, 2, s)

            def with_xn(g, s):
                dve_step(g, s)
                make_xn(g + 2, s)

            with_xn(0, 0)
            with dve.Fori(1, GROUPS - 4, 2) as g:
                with_xn(g, 1)
                with_xn(g + 1, 0)
            with_xn(GROUPS - 3, 1)
            dve_step(GROUPS - 2, 0)
            dve_step(GROUPS - 1, 1)
            norm(BATCH - 1, 3, 1)
            take_out(GROUPS - 1)

            for half in range(2):
                dve.wait_ge(mq_step, half + 1)
                link(v.tensor_reduce(mq[:, half, 0:1], bank(6 + half)[:, 0:P + 1], AX.X, ALU.max))
                v.tensor_scalar(mq[:, half, 1:2], mq[:, half, 0:1], -SCALE, None,
                                ALU.mult).then_inc(mq_max, 1)
            for half in range(2):
                dve.wait_ge(mq_exp, half + 1)
                link(v.reciprocal(mq[:, half, 3:4], mq[:, half, 2:3]))
                v.tensor_scalar(pmq[:, half, :], pmq[:, half, :], mq[:, half, 3:4], None,
                                ALU.mult).then_inc(mq_norm, 1)
            dve.wait_ge(mq_step, 3)
            v.tensor_copy(pmqT[:, :, :], bank(4)[:, 0:2 * P].rearrange("p (a n) -> p a n", a=2))
            v.tensor_copy(pmm[:, :, :],
                          bank(5)[0:1, 0:2 * P].rearrange("p (a n) -> p a n", a=2)).then_inc(mq_copied, 1)
            dve.wait_ge(mq_step, 4)
            link(v.tensor_tensor(mq_sel[:, :, :],
                                 bank(6)[:, 0:BATCH * HEADS].rearrange("p (b h) -> p b h", b=BATCH),
                                 const("headmask").rearrange("p (a h) -> p a h", a=1)
                                 .to_broadcast([P, BATCH, HEADS]), ALU.mult))
            v.tensor_reduce(attT_m[:, :], mq_sel[:, :, :], AX.X, ALU.add).then_inc(mq_att, 1)
            dve.wait_ge(mq_step, 5)
            link(v.tensor_tensor(h[0:BATCH, MT, :], bank(7)[0:BATCH, 0:HID], h[0:BATCH, MT, :], ALU.add))
            link(v.bn_stats(stats[:, MT, :], h[:, MT, :]))
            dve.wait_ge(stats_done, 2 * GROUPS)
            layernorm_scales()

            def x2(g, s):
                if not isinstance(g, int) or g >= 2:
                    dve.wait_ge(x2t_ready, g - 1)
                for b in range(GB):
                    ins = normalize(xn[:, s, b, :], g * GB + b)
                ins.then_inc(x2n_done, 1)

            def take_logits(g, s, n=GB):
                dve.wait_ge(logits_ready, g + 1)
                at, _ = COLS["bg"]
                v.tensor_tensor(logits[:, bass.ds(g * GB, n), :],
                                bank(2 + s)[:, 0:n * P].rearrange("p (b e) -> p b e", b=n)[:, :, 0:EXPERTS],
                                const("bg").rearrange("p (a e) -> p a e", a=1).to_broadcast([P, n, EXPERTS]),
                                ALU.add).then_inc(logits_taken, 1)

            x2(0, 0)
            x2(1, 1)
            take_logits(0, 0)
            with dve.Fori(1, GROUPS - 2, 2) as g:
                x2(g + 1, 0)
                take_logits(g, 1)
                x2(g + 2, 1)
                take_logits(g + 1, 0)
            dve.wait_ge(x2t_ready, GROUPS - 1)
            normalize(xn[:, 0, 0, :], MT).then_inc(x2n_done, 1)
            take_logits(GROUPS - 1, 1)
            take_logits(GROUPS, 0, 1)
            dve.wait_ge(logits_taken, GROUPS + 1)

            def wide(t):
                return t.rearrange("p (n a) -> p n a", a=1).to_broadcast([P, TILES, EXPERTS])

            rank = const("rank").rearrange("p (a e) -> p a e", a=1).to_broadcast([P, TILES, EXPERTS])

            def best(scores, top, pick, tmp):
                link(v.tensor_reduce(top, scores, AX.X, ALU.max))
                link(v.tensor_tensor(tmp, scores, wide(top), ALU.is_equal))
                link(v.tensor_tensor(tmp, tmp, rank, ALU.mult))
                link(v.tensor_reduce(gs[:, 7, :], tmp, AX.X, ALU.max))
                link(v.tensor_tensor(pick, tmp, wide(gs[:, 7, :]), ALU.is_equal))

            best(logits[:, :, :], gs[:, 0, :], gt[:, 0], gt[:, 2])
            link(v.scalar_tensor_tensor(out=gt[:, 3], in0=gt[:, 0], scalar=-3.0e38, in1=logits[:, :, :],
                                        op0=ALU.mult, op1=ALU.add))
            best(gt[:, 3], gs[:, 1, :], gt[:, 1], gt[:, 2])
            v.tensor_tensor(gs[:, 2, :], gs[:, 1, :], gs[:, 0, :], ALU.subtract).then_inc(gap_done, 1)
            dve.wait_ge(gap_exp, 1)
            link(v.tensor_scalar(gs[:, 4, :], gs[:, 3, :], 1.0, None, ALU.add))
            link(v.reciprocal(gs[:, 5, :], gs[:, 4, :]))
            link(v.tensor_tensor(gs[:, 6, :], gs[:, 5, :], gs[:, 3, :], ALU.mult))
            v.tensor_tensor(gt[:, 2], gt[:, 0], wide(gs[:, 5, :]), ALU.mult)
            link(v.tensor_tensor(gt[:, 3], gt[:, 1], wide(gs[:, 6, :]), ALU.mult))
            v.tensor_tensor(gate[:, :, :], gt[:, 2], gt[:, 3], ALU.add).then_inc(gate_done, 1)
            dve.wait_ge(gate_done, 1)

            def add_y(m, e, g, tiles, rows):
                dve.wait_ge(y_ready, m + 1)
                for b in range(tiles):
                    t = h[0:rows, bass.ds(g * GB + b, 1), :].rearrange("p a n -> p (a n)")
                    w = gate[0:rows, bass.ds(g * GB + b, 1), e]
                    ins = v.scalar_tensor_tensor(out=t, in0=bank(2 + e % 2)[0:rows, b * P:b * P + P],
                                                 scalar=w, in1=t, op0=ALU.mult, op1=ALU.add)
                ins.then_inc(y_taken, 1)
                dve.wait_ge(y_taken, m + 1)

            def add_experts(g, tiles, rows):
                for e in range(EXPERTS):
                    add_y(g * EXPERTS + e, e, g, tiles, rows)
                    if e == 3:
                        dve.wait_ge(b2_ready, g + 1)
                        t = h[0:rows, bass.ds(g * GB, tiles), :]
                        v.tensor_tensor(t, bank(4)[0:rows, 0:tiles * P].rearrange("p (b n) -> p b n", b=tiles),
                                        t, ALU.add).then_inc(b2_taken, 1)
                        dve.wait_ge(b2_taken, g + 1)

            with dve.Fori(0, GROUPS, 1) as g:
                add_experts(g, GB, P)
            add_experts(GROUPS, 1, BATCH)

        @block.tensor
        def _(pe):
            mm = nc.tensor.matmul
            pe.wait_ge(memsets_done, 1)
            pe.wait_ge(consts_in, 16)
            pe.wait_ge(weff_done, 1)
            for j in range(KCH):
                ins = mm(bank(2)[:, 0:HID], ones[:, :], cbw[:, j, :], start=(j == 0), stop=(j == KCH - 1))
            ins.then_inc(bias_sum, 1)
            pe.wait_ge(weff_done, 2)

            def tok(g, slot, landed):
                pe.wait_ge(x_in[slot], landed)
                pe.wait_ge(h_done, g + 1)
                for b in range(GB):
                    for j in range(KCH):
                        ins = mm(bank(slot % 2)[:, b * P:(b + 1) * P], x_sb[:, slot, j, b * P:(b + 1) * P],
                                 weff[:, j, :], start=(j == 0), stop=(j == KCH - 1))
                ins.then_inc(tok_done, 1)
            with pe.Fori(0, GROUPS - XSLOTS + 1, XSLOTS) as g:
                for slot in range(XSLOTS):
                    tok(g + slot, slot, g * (16 // XSLOTS) + 16)

            ident = const("ident")
            pe.wait_ge(setup_xn, 1)
            nc.tensor.transpose(bank(3)[:, 0:P], xn[:, 1, 0, :], ident).then_inc(setup_ready, 1)
            pe.wait_ge(setup_taken, 2)
            pe.wait_ge(weights_in, 32)
            mm(bank(3)[:, 0:1], wqkv_sb[:, 0, :], xnT_m[:, 0:1], start=True, stop=True)
            mm(bank(3)[:, 1:2], wqkv_sb[:, 2, :], xnT_m[:, 0:1], start=True, stop=True)
            mm(bank(3)[:, 128:256], xnT_m[:, 0:1].to_broadcast([P, P]), wqkv_sb[:, 4, :], start=True, stop=True)
            mm(bank(3)[:, 256:384], bv_wide[:, :], wo_sb[:, :], start=True, stop=True).then_inc(setup_ready, 1)

            def transposes(g, s):
                pe.wait_ge(xn_done, g + 1)
                if not isinstance(g, int) or g >= 1:
                    pe.wait_ge(taken["kp"], g)
                    pe.wait_ge(taken["out"], g - 1 if not isinstance(g, int) or g >= 2 else 1)
                for b in range(GB):
                    ins = nc.tensor.transpose(bank(6)[:, b * P:(b + 1) * P], xn[:, s, b, :], ident)
                ins.then_inc(ready["xnT"], 1)

            AFTER = {"q": "smk", "qp": "xnT", "k": "q", "kp": "qp", "v": "k", "smk": "v"}

            def project(name, g, s):
                if name != "q":
                    pe.wait_ge(taken[AFTER[name]], g + 1)
                else:
                    pe.wait_ge(taken["xnT"], g + 1)
                    if not isinstance(g, int) or g >= 1:
                        pe.wait_ge(taken["smk"], g)
                c = ("q", "qp", "k", "kp").index(name)
                mm(bank(7 if c % 2 == 0 else 6), wqkv_sb[:, c, :], xnT[:, s, :], start=True,
                   stop=True).then_inc(ready[name], 1)

            def project_v(g, s):
                pe.wait_ge(taken["k"], g + 1)
                for b in range(GB):
                    ins = mm(bank(7)[:, b * P:(b + 1) * P], xnT[:, s, b * P:(b + 1) * P], wqkv_sb[:, 4, :],
                             start=True, stop=True)
                ins.then_inc(ready["v"], 1)

            def marker_scores(g, s):
                pe.wait_ge(taken["v"], g + 1)
                pe.wait_ge(q_split, g + 1)
                for b in range(GB):
                    ins = mm(bank(7)[:, b * P:(b + 1) * P], q32[:, s, b, :], km_pad[:, :],
                             start=True, stop=True)
                ins.then_inc(ready["smk"], 1)

            def project_out(g, s, last=False):
                pe.wait_ge(norm_done, (g + 1) * GB)
                if not last:
                    pe.wait_ge(taken["kp"], g + 3)
                for b in range(GB):
                    for e in range(2):
                        ins = mm(bank(6)[:, b * P:(b + 1) * P], attT[:, s, b, e, :], wo_head[:, e, :],
                                 start=(e == 0), stop=(e == 1))
                ins.then_inc(ready["out"], 1)

            def score_max(n, b, s, landed):
                if landed is not None:
                    pe.wait_ge(q_stacked[s], landed[0])
                    pe.wait_ge(k_stacked[s], landed[1])
                if not (isinstance(n, int) and n == 0):
                    pe.wait_ge(negm_done, n)
                for r in range(HEADS // 2):
                    k = 1 + r * GB + b
                    for e in range(2):
                        pair = k_zeros[s][:, k:KB + 2:KB + 1 - k, :] if e == 0 else k_zeros[s][:, 0:k + 1:k, :]
                        ins = mm(bank(r // 2)[:, r % 2 * 2 * P:(r % 2 + 1) * 2 * P].rearrange(
                            "p (e t) -> p e t", e=2), q_stack[s][:, 2 * r + e, b, :], pair,
                            start=(e == 0), stop=(e == 1))
                ins.then_inc(max_scored, 1)

            idents = [ident_r[:, 1 - e:3 - e, :].rearrange("p a n -> p (a n)") for e in range(2)]

            def score(n, b, s, late):
                pe.wait_ge(negm_done, n + 1)
                if not (isinstance(n, int) and n == 0):
                    pe.wait_ge(exp_done, n)
                if late:
                    pe.wait_ge(norm_done, n - 1)
                nm = negm[b % 2]
                for r in range(HEADS // 2):
                    at = r % 2 * 2 * P
                    mm(bank(2 + r // 2)[:, at:at + 2 * P], k_stack[s][:, r, b, :],
                       q_stack[s][:, 2 * r:2 * r + 2, b, :], start=True, stop=False)
                    for e in range(2):
                        mm(bank(2 + r // 2)[:, at:at + 2 * P],
                           nm[:, 2 * r + e:2 * r + e + 1].to_broadcast([P, P]), idents[e],
                           start=False, stop=(e == 1))
                mk = bank(4 + b % 2)
                mm(mk[:, 256:512], nm[:, :], idents[0], start=True, stop=True)
                mm(mk[:, 256:384], km_pad[:, :], q32[:, s, b, :], start=False, stop=True,
                   skip_group_check=True).then_inc(scored, 1)

            def weigh(n, b, s):
                pe.wait_ge(exp_done, n + 1)
                pe.wait_ge(pmk_split, n + 1)
                od = bank(4 + b % 2)
                for part in range(2):
                    col = slice(part * 2 * P, (part + 1) * 2 * P)
                    mm(od[:, col].rearrange("p (e t) -> p e t", e=2), (vm_parts, one_parts)[part][:, :],
                       pmk_parts[:, b % 2:b % 2 + 1, :].to_broadcast([P, 2, TOKENS]), start=True, stop=False)
                    for r in range(HEADS // 2):
                        w = v_fix[:, s, b, 32 * r:32 * r + 32] if part == 0 else ones[:, 0:32]
                        ins = mm(od[32 * r:32 * r + 32, col], w,
                                 probs[:, b % 2, 2 * r:2 * r + 2, :].rearrange("p e t -> p (e t)"),
                                 start=False, stop=True)
                ins.then_inc(pv_done, 1)

            def landed(g, s):
                if isinstance(g, int):
                    return 16 * NQ * (g // 2 + 1), 16 * NK * (g // 2 + 1)
                return (g - s) * (8 * NQ) + 16 * NQ, (g - s) * (8 * NK) + 16 * NK

            pe.wait_ge(ident_r_done, 1)
            pe.wait_ge(marker_set, 1)
            transposes(0, 0)
            for name in ("q", "qp", "k", "kp"):
                project(name, 0, 0)
            project_v(0, 0)
            marker_scores(0, 0)
            score_max(0, 0, 0, landed(0, 0))

            def step(g, s):
                static = isinstance(g, int)
                first, last = static and g == 0, static and g == GROUPS - 1
                n = g * GB
                if not last:
                    transposes(g + 1, 1 - s)
                score(n, 0, s, not first)
                score_max(n + 1, 1, s, None)
                if not last:
                    project("q", g + 1, 1 - s)
                if not first:
                    weigh(n - 1, GB - 1, 1 - s)
                if not last:
                    project("qp", g + 1, 1 - s)
                    project("k", g + 1, 1 - s)
                score(n + 1, 1, s, not first)
                score_max(n + 2, 2, s, None)
                if not last:
                    project("kp", g + 1, 1 - s)
                weigh(n, 0, s)
                if not last:
                    project_v(g + 1, 1 - s)
                score(n + 2, 2, s, True)
                score_max(n + 3, 3, s, None)
                if not first:
                    project_out(g - 1, 1 - s, last)
                weigh(n + 1, 1, s)
                if not last:
                    marker_scores(g + 1, 1 - s)
                score(n + 3, 3, s, True)
                if not last:
                    score_max(n + 4, 0, 1 - s, landed(g + 1, 1 - s))
                weigh(n + 2, 2, s)

            groups(pe, step)
            weigh(BATCH - 1, 3, 1)
            pe.wait_ge(taken["out"], GROUPS)
            project_out(GROUPS - 1, 1, True)

            pe.wait_ge(taken["out"], GROUPS + 1)
            for half in range(2):
                for b in range(16):
                    mm(bank(6 + half)[:, 0:P], qm_shift[:, 120 - HEADS * b:248 - HEADS * b],
                       k_all[:, 16 * half + b, :], start=(b == 0), stop=(b == 15))
                mm(bank(6 + half)[:, P:P + 1], qm_tiled[:, :, :].rearrange("p a h -> p (a h)"), qm[:, 1:2],
                   start=True, stop=True).then_inc(mq_step, 1)
            pe.wait_ge(norm_done, BATCH)
            for half in range(2):
                pe.wait_ge(mq_norm, half + 1)
                nc.tensor.transpose(bank(4)[:, half * P:(half + 1) * P], pmq[:, half, 0:P], ident)
                ins = mm(bank(5)[0:1, half * P:(half + 1) * P], pmq[:, half, P:P + 1], ident,
                         start=True, stop=True)
            ins.then_inc(mq_step, 1)
            pe.wait_ge(mq_copied, 1)
            pe.wait_ge(v_kept, GROUPS)
            mm(bank(6)[:, 0:BATCH * HEADS], vm_row[:, :], pmm[:, :, :].rearrange("p a n -> p (a n)"),
               start=True, stop=False, skip_group_check=True)
            for b in range(BATCH):
                ins = mm(bank(6)[:, b * HEADS:(b + 1) * HEADS], v_all[:, b, :],
                         pmqT[:, :, :].rearrange("p a n -> p (a n)")[:, b * HEADS:(b + 1) * HEADS],
                         start=False, stop=(b == BATCH - 1), skip_group_check=True)
            ins.then_inc(mq_step, 1)
            pe.wait_ge(mq_att, 1)
            mm(bank(7)[0:BATCH, 0:HID], attT_m[:, :], wo_sb[:, :], start=True, stop=True).then_inc(mq_step, 1)

            def x2(g, s):
                pe.wait_ge(x2n_done, g + 1)
                if not isinstance(g, int) or g >= 2:
                    pe.wait_ge(x2t_taken, g - 1)
                for b in range(GB):
                    ins = nc.tensor.transpose(bank(s)[:, b * P:(b + 1) * P], xn[:, s, b, :], ident)
                ins.then_inc(x2t_ready, 1)

            wg_at, _ = COLS["wg"]

            def gate_logits(g, s, tiles=GB):
                pe.wait_ge(x2t_taken, g + 1)
                if not isinstance(g, int) or g >= 1:
                    pe.wait_ge(logits_taken, g)
                for b in range(tiles):
                    ins = mm(bank(2 + s)[:, b * P:(b + 1) * P], xnT[:, s, b * P:(b + 1) * P],
                             cst[:, wg_at:wg_at + P], start=True, stop=True)
                ins.then_inc(logits_ready, 1)

            x2(0, 0)
            x2(1, 1)
            gate_logits(0, 0)
            with pe.Fori(1, GROUPS - 2, 2) as g:
                x2(g + 1, 0)
                gate_logits(g, 1)
                x2(g + 2, 1)
                gate_logits(g + 1, 0)
            pe.wait_ge(x2n_done, GROUPS + 1)
            pe.wait_ge(x2t_taken, GROUPS - 1)
            nc.tensor.transpose(bank(0)[:, 0:P], xn[:, 0, 0, :], ident).then_inc(x2t_ready, 1)
            gate_logits(GROUPS - 1, 1)
            gate_logits(GROUPS, 0, 1)

            pe.wait_ge(ffn_in, 48)
            pe.wait_ge(x2_kept, GROUPS + 1)
            pe.wait_ge(logits_taken, GROUPS + 1)

            def hidden(n, e, g, cols, late):
                if late:
                    pe.wait_ge(gelu_done, n - 1)
                mm(bank(e % 2)[:, 0:cols], w1_sb[:, e, :], x2T[:, bass.ds(g * GT, cols)], start=True,
                   stop=True).then_inc(hid_ready, 1)

            def expert_out(n, e, tiles, rows, late):
                pe.wait_ge(gelu_done, n + 1)
                if late:
                    pe.wait_ge(y_taken, n - 1)
                for b in range(tiles):
                    ins = mm(bank(2 + e % 2)[0:rows, b * P:(b + 1) * P], hid[:, e % 2, b * P:b * P + rows],
                             w2_sb[:, e, :], start=True, stop=True)
                ins.then_inc(y_ready, 1)

            def gates_up(g, s, tiles, rows, late):
                if tiles == GB:
                    pe.wait_ge(wgrp_done, g + 1)
                if late:
                    pe.wait_ge(wT_taken, g)
                src = wgrp[:, s, :] if tiles == GB else gate[0:BATCH, MT, :]
                idn = ident if tiles == GB else cst[0:BATCH, COLS["ident"][0]:COLS["ident"][0] + BATCH]
                mm(bank(5)[0:tiles * EXPERTS, 0:rows], src, idn, start=True, stop=True).then_inc(wT_ready, 1)

            def second_bias(g, s, tiles, rows, late):
                pe.wait_ge(wT_taken, g + 1)
                if late:
                    pe.wait_ge(b2_taken, g)
                mm(bank(4)[0:rows, 0:tiles * P], wgrpT[:, 0:rows],
                   b2_sb[:, 0:tiles, :].rearrange("p b n -> p (b n)"), start=True,
                   stop=True).then_inc(b2_ready, 1)

            def experts(g, s, tiles, rows, cols, first, nexts):
                for e in range(EXPERTS):
                    n = g * EXPERTS + e
                    if e < EXPERTS - 1:
                        hidden(n + 1, e + 1, g, cols, not first or e >= 1)
                    elif nexts is not None:
                        hidden(n + 1, 0, g + 1, nexts, True)
                    expert_out(n, e, tiles, rows, not first or e >= 2)
                    if e == 0:
                        gates_up(g, s, tiles, rows, not first)
                    if e == 2:
                        second_bias(g, s, tiles, rows, not first)

            hidden(0, 0, 0, GT, False)
            experts(0, 0, GB, P, GT, True, GT)
            with pe.Fori(1, GROUPS - 2, 2) as g:
                experts(g, 1, GB, P, GT, False, GT)
                experts(g + 1, 0, GB, P, GT, False, GT)
            experts(GROUPS - 1, 1, GB, P, GT, False, BATCH)
            experts(GROUPS, 0, 1, BATCH, BATCH, False, None)


def columns():
    return COLS


def kernel(**inputs):
    from concourse import bacc
    from concourse.bass_utils import run_bass_kernel_spmd

    a = {n: np.asarray(t) for n, t in inputs.items()}
    f = np.float32

    x = a["x"].reshape(GROUPS, GB, TOKENS, KCH, P).transpose(0, 4, 3, 1, 2)
    conv = a["L0_tok_conv_w"].reshape(HID, MAX_CHANS, PER_CHAN, PATCH)[:, :CHANS]
    conv = conv.transpose(3, 1, 2, 0).reshape(KCH, P, PER_CHAN, HID).transpose(1, 0, 2, 3)

    def chan(t):
        return np.tile(t[:CHANS], (PATCH, 1)).reshape(KCH, P, PER_CHAN).transpose(1, 0, 2).reshape(P, -1)

    def rows(t):
        return np.broadcast_to(t, (P, t.shape[-1]))

    pos = np.arange(TOKENS, dtype=f)[:, None]
    freq = np.exp(-(f(2) * np.arange(HID // 2, dtype=f)[None] / f(HID)) * np.log(f(10000.0)))
    angle = pos * freq
    pe = np.stack([np.sin(angle), np.cos(angle)], -1).reshape(TOKENS, HID)
    half = HD // 2
    inv = f(1) / f(10000.0) ** (np.arange(0, HD, 2, dtype=f) / f(HD))
    angle = np.arange(1, TOKENS + 1, dtype=f)[None] * inv[:, None]
    cos, sin = np.cos(angle), np.sin(angle)
    sin[:half // 2] *= -1
    cos, sin = (np.tile(t, (P // half, 1)) for t in (cos, sin))
    head = np.arange(P)[:, None] // HD == np.arange(HEADS)[None]
    headrows = np.zeros((P, P), f)
    for block in range(4):
        headrows[32 * block:32 * block + HEADS] = head.T
    swap = np.arange(P) ^ (half // 2)

    w, b = a["L0_attn_qkv_w"].reshape(3, P, HID), a["L0_attn_qkv_b"].reshape(3, P)
    wqkv = np.stack([w[0], w[0][swap], w[1], w[1][swap], w[2]]).transpose(2, 0, 1)
    bias = np.stack([b[0], b[0][swap], b[1], b[1][swap], b[2]], 1)
    parts = {
        "pe": pe, "cos": cos, "sin": sin, "ident": np.eye(P, dtype=f), "headmask": head.astype(f),
        "headrows": headrows, "rank": rows(np.arange(EXPERTS, 0, -1, dtype=f)),
        "cw": chan(a["L0_tok_chan_w"]), "cb": chan(a["L0_tok_chan_b"]),
        "marker": rows(a["L0_tok_marker"]), "bias": bias, "ob": rows(a["L0_attn_out_b"]),
        "bg": rows(a["L0_ffn_bg"]), "wg": a["L0_ffn_Wg"], "b1": a["L0_ffn_b1"].T,
        "parity": np.stack([np.arange(P) // HD % 2 == e for e in range(2)], 1).astype(f),
        "low_key": (np.arange(P) // 64 == 1).astype(f)[:, None],
        "hide_high": np.where(np.arange(P) // 32 % 2 == 0, f(-1e30), f(0))[:, None],
    }
    b2bd = np.zeros((P, GB, HID), f)
    for t in range(GB):
        b2bd[t * EXPERTS:(t + 1) * EXPERTS, t] = a["L0_ffn_b2"]
    arrays = {
        "xt": x, "convw": conv, "consts": np.concatenate([parts[n] for n in COLS], 1).astype(f),
        "wqkv": wqkv, "wo": a["L0_attn_out_w"].T, "w1": a["L0_ffn_W1"].transpose(1, 0, 2),
        "w2": a["L0_ffn_W2"].transpose(1, 0, 2), "b2bd": b2bd,
    }
    arrays = {n: np.ascontiguousarray(t) for n, t in arrays.items()}
    nc = bacc.Bacc("TRN2", target_bir_lowering=False, num_devices=1)
    args = [nc.dram_tensor(n, t.shape, mybir.dt.from_np(t.dtype), kind="ExternalInput").ap()
            for n, t in arrays.items()]
    out = nc.dram_tensor("out", (BATCH, TOKENS + 1, HID), F32, kind="ExternalOutput").ap()
    audio_tower_kernel(nc, *args, out)
    r = run_bass_kernel_spmd(nc, [arrays], core_ids=[0])
    return r.results[0]["out"]
```

```python
from contextlib import ExitStack

import numpy as np

import concourse.bass as bass
from concourse import mybir

ALU = mybir.AluOpType
ACT = mybir.ActivationFunctionType
F32 = mybir.dt.float32
F32R = mybir.dt.float32r
AX = mybir.AxisListType

P = 128
BATCH, T_RAW, CHANS = 32, 1024, 48
PATCH, PER_CHAN, MAX_CHANS = 8, 8, 64
TOKENS = T_RAW // PATCH
HID = 128
HEADS, HD = 8, 16
EXPERTS = 8
KCH = PATCH * CHANS // P
GB = 4
GROUPS = BATCH // GB
GT = GB * TOKENS
TILES = BATCH + 1
MT = BATCH
EPS = 1e-5
SCALE = HD ** -0.5
XSLOTS = 4

COLS = {}


def _columns():
    at = 0
    for name, n in (("wg", EXPERTS), ("pe", HID), ("cos", TOKENS), ("sin", TOKENS), ("ident", P), ("headmask", HEADS),
                    ("headrows", P), ("rank", EXPERTS), ("cw", KCH * PER_CHAN), ("cb", KCH * PER_CHAN),
                    ("marker", HID), ("bias", 5), ("ob", HID), ("bg", EXPERTS),
                    ("b1", EXPERTS), ("parity", 2), ("low_key", 1), ("hide_high", 1),
                    ("row_parity", 2), ("low_row", 1)):
        COLS[name] = (at, n)
        at += n
    return at


NCOLS = _columns()


def audio_tower_kernel(nc, xt, convw, consts, wqkv, wo, w1, w2, b2bd, out):
    parts_dram = nc.dram_tensor("parts_dram", [GROUPS, 2, HEADS, 2, HD, GT], F32).ap()
    km_dram = nc.dram_tensor("km_dram", [HEADS, HD], F32).ap()
    ctx = ExitStack()
    with ctx:
        def sb(name, shape, dt=F32):
            return ctx.enter_context(nc.sbuf_tensor(name, shape, dt))

        def sem(name):
            return ctx.enter_context(nc.semaphore(name))

        cst = sb("cst", [P, NCOLS])

        def const(name):
            at, n = COLS[name]
            return cst[:, at:at + n]

        conv_sb = sb("conv_sb", [P, KCH, PER_CHAN, HID])
        weff = sb("weff", [P, KCH, HID])
        cbw = sb("cbw", [P, KCH, HID])
        ones = sb("ones", [P, P])
        pe_bias = sb("pe_bias", [P, HID])
        x_sb = sb("x_sb", [P, XSLOTS, KCH, GT])
        h = sb("h", [P, TILES, HID])
        stats = sb("stats", [P, TILES, 6])
        ln_tmp = sb("ln_tmp", [P, 6, TILES])
        rstd = sb("rstd", [P, TILES])
        shift = sb("shift", [P, TILES])
        wqkv_sb = sb("wqkv_sb", [P, 5, HID])
        wo_sb = sb("wo_sb", [P, HID])
        ident_r = sb("ident_r", [P, P], F32R)
        ones_head = sb("ones_head", [P, 2, 32])
        xn = sb("xn", [P, 2, GB, HID])
        xnT = sb("xnT", [P, 2, GT])
        xnT_m = sb("xnT_m", [P, 1])
        rope_a = sb("rope_a", [P, 2, GB, TOKENS])
        rope_b = sb("rope_b", [P, 2, GB, TOKENS])
        q32 = sb("q32", [P, GB, TOKENS])
        k_all = sb("k_all", [P, BATCH, TOKENS])
        v_all = sb("v_all", [P, BATCH, HID])
        split = sb("split", [P, 4, GT], F32R)
        q_stack = [sb(f"q_stack{s}", [P, HEADS, GB, TOKENS], F32R) for s in range(2)]
        k_stack = [sb(f"k_stack{s}", [P, HEADS // 2, GB, TOKENS], F32R) for s in range(2)]
        v_fix = sb("v_fix", [P, 2, GB, HID])
        smk_sb = sb("smk_sb", [P, BATCH, HEADS])
        negmax = sb("negmax", [P, 2, HEADS])
        negm = [sb(f"negm{s}", [P, P], F32R) for s in range(2)]
        probs = sb("probs", [P, 2, HEADS, TOKENS])
        pmk = sb("pmk", [P, 2, TOKENS])
        pmk_hid = sb("pmk_hid", [P, 2, TOKENS], F32R)
        pmk_parts = sb("pmk_parts", [P, 2, TOKENS], F32R)
        attT = sb("attT", [P, 2, GB, 2, TOKENS])
        wo_head = sb("wo_head", [P, 2, HID])
        obias = sb("obias", [P, HID])
        qm = sb("qm", [P, 2])
        km_pad = sb("km_pad", [P, P])
        km_rows = sb("km_rows", [P, HEADS // 2])
        km_hid = sb("km_hid", [P, HEADS // 2], F32R)
        km_parts = sb("km_parts", [P, HEADS // 2], F32R)
        km_stack = sb("km_stack", [P, HEADS // 2, P], F32R)
        qm_shift = sb("qm_shift", [P, 2 * 120 + HEADS])
        vm_heads, bv_wide = cbw[:, 0, :], cbw[:, 1, :]
        qm_tiled = cbw[:, 2, :].rearrange("p (a h) -> p a h", h=HEADS)
        vm_row = sb("vm_row", [1, HID])
        vm_hid = sb("vm_hid", [P, HID], F32R)
        vm_parts = sb("vm_parts", [P, HID], F32R)
        one_parts = sb("one_parts", [P, HID], F32R)
        mq = sb("mq", [P, 2, 4])
        attT_m = sb("attT_m", [P, BATCH])
        conv_flat = conv_sb[:, :, :, :].rearrange("p a b c -> p (a b c)")
        w1_sb = conv_flat[:, 0:EXPERTS * HID].rearrange("p (e n) -> p e n", e=EXPERTS)
        w2_sb = conv_flat[:, EXPERTS * HID:2 * EXPERTS * HID].rearrange("p (e n) -> p e n", e=EXPERTS)
        b2_sb = conv_flat[:, 2 * EXPERTS * HID:(2 * EXPERTS + GB) * HID].rearrange("p (b n) -> p b n", b=GB)
        rec = x_sb[:, XSLOTS - 1, 0, 0:2 * TOKENS].rearrange("p (s n) -> p s n", s=2)
        x_flat = x_sb[:, :, :, :].rearrange("p a b c -> p (a b c)")
        x2T = x_flat[:, 0:TILES * P]
        pmq = x_flat[:, 0:2 * (P + 1)].rearrange("p (a n) -> p a n", a=2)
        pmm = x_flat[0:1, 7 * P:9 * P].rearrange("p (a n) -> p a n", a=2)
        pmqT = x_flat[:, 3 * P:5 * P].rearrange("p (a n) -> p a n", a=2)
        mq_sel = x_flat[:, 5 * P:5 * P + BATCH * HEADS].rearrange("p (b h) -> p b h", b=BATCH)
        TE = TILES * EXPERTS
        at = TILES * P
        logits = x_flat[:, at:at + TE].rearrange("p (n e) -> p n e", n=TILES)
        gate = x_flat[:, at + TE:at + 2 * TE].rearrange("p (n e) -> p n e", n=TILES)
        gt = x_flat[:, at + 2 * TE:at + 6 * TE].rearrange("p (a n e) -> p a n e", a=4, n=TILES)
        gs = x_flat[:, at + 6 * TE:at + 7 * TE].rearrange("p (a n) -> p a n", a=8)
        hid = probs[:, :, :, :].rearrange("p a b c -> p a (b c)")[:, :, 0:GT]
        wgrp = pe_bias[:, 0:2 * GB * EXPERTS].rearrange("p (s n) -> p s n", s=2)
        wgrpT = sb("wgrpT", [P, P])

        banks = ctx.enter_context(nc.psum_tensor("banks", [P, 8, 512], F32))

        def bank(n, k=1):
            return banks[:, n:n + k, :].rearrange("p a b -> p (a b)")

        consts_in = sem("consts_in")
        conv_in = sem("conv_in")
        weights_in = sem("weights_in")
        ffn_in = sem("ffn_in")
        x_in = [sem(f"x_in{s}") for s in range(XSLOTS)]
        memsets_done = sem("memsets_done")
        pool_memsets = sem("pool_memsets")
        dve_chain = sem("dve_chain")
        pool_chain = sem("pool_chain")
        pool_held = sem("pool_held")
        sp_held = sem("sp_held")
        km_set = sem("km_set")
        km_out = sem("km_out")
        km_in = sem("km_in")
        km_stacked = sem("km_stacked")
        bias_sum = sem("bias_sum")
        setup_xn = sem("setup_xn")
        stats_done = sem("stats_done")
        rope_summed = sem("rope_summed")
        rope_high = sem("rope_high")
        row_max = sem("row_max")
        pe_bias_done = sem("pe_bias_done")
        weff_done = sem("weff_done")
        tok_done = sem("tok_done")
        h_done = sem("h_done")
        var_done = sem("var_done")
        std_done = sem("std_done")
        rstd_done = sem("rstd_done")
        xn_done = sem("xn_done")
        ready = {k: sem(f"{k}_ready") for k in ("xnT", "q", "qp", "k", "kp", "v", "smk", "out")}
        taken = {k: sem(f"{k}_taken") for k in ("xnT", "q", "qp", "k", "kp", "v", "smk", "out")}
        setup_ready = sem("setup_ready")
        setup_taken = sem("setup_taken")
        marker_set = sem("marker_set")
        ident_r_done = sem("ident_r_done")
        q_split = sem("q_split")
        k_split = sem("k_split")
        v_kept = sem("v_kept")
        pmk_split = sem("pmk_split")
        rec_done = sem("rec_done")
        h_biased = sem("h_biased")
        parts_out = [sem(f"parts_out{s}") for s in range(2)]
        q_stacked = [sem(f"q_stacked{s}") for s in range(2)]
        k_stacked = [sem(f"k_stacked{s}") for s in range(2)]
        max_scored = sem("max_scored")
        negm_done = sem("negm_done")
        scored = sem("scored")
        exp_done = sem("exp_done")
        pv_done = sem("pv_done")
        norm_done = sem("norm_done")
        mq_step = sem("mq_step")
        mq_max = sem("mq_max")
        mq_exp = sem("mq_exp")
        mq_norm = sem("mq_norm")
        mq_copied = sem("mq_copied")
        mq_att = sem("mq_att")
        x2n_done = sem("x2n_done")
        x2t_ready = sem("x2t_ready")
        x2t_taken = sem("x2t_taken")
        x2_kept = sem("x2_kept")
        logits_ready = sem("logits_ready")
        logits_taken = sem("logits_taken")
        gap_done = sem("gap_done")
        gap_exp = sem("gap_exp")
        gate_done = sem("gate_done")
        wgrp_done = sem("wgrp_done")
        wT_ready = sem("wT_ready")
        wT_taken = sem("wT_taken")
        b2_ready = sem("b2_ready")
        b2_taken = sem("b2_taken")
        hid_ready = sem("hid_ready")
        gelu_done = sem("gelu_done")
        y_ready = sem("y_ready")
        y_taken = sem("y_taken")
        stored = sem("stored")

        H = P // 2
        NQ, NK = 8, 4

        block = ctx.enter_context(nc.Block())

        def groups(eng, step):
            step(0, 0)
            with eng.Fori(1, GROUPS - 4, 2) as g:
                step(g, 1)
                step(g + 1, 0)
            for g in range(GROUPS - 3, GROUPS):
                step(g, g % 2)

        @block.sync
        def _(sp):
            sp.dma_start(cst[:, :], consts).then_inc(consts_in, 16)
            sp.dma_start(conv_sb[:, :, :, :], convw).then_inc(conv_in, 16)
            for g in range(XSLOTS):
                sp.dma_start(x_sb[:, g, :, :], xt[g]).then_inc(x_in[g], 16)
            sp.dma_start(wqkv_sb[:, :, :], wqkv).then_inc(weights_in, 16)
            sp.dma_start(wo_sb[:, :], wo).then_inc(weights_in, 16)
            for g in range(XSLOTS, GROUPS):
                sp.wait_ge(tok_done, g - XSLOTS + 1)
                sp.dma_start(x_sb[:, g - XSLOTS, :, :], xt[g]).then_inc(x_in[g - XSLOTS], 16)
            sp.wait_ge(weff_done, 2)
            sp.dma_start(w1_sb[:, :, :], w1).then_inc(ffn_in, 16)
            sp.dma_start(w2_sb[:, :, :], w2).then_inc(ffn_in, 16)
            sp.dma_start(b2_sb[:, :, :], b2bd).then_inc(ffn_in, 16)
            sp.wait_ge(pool_memsets, 2)

            def put(which, g):
                for part in range(2):
                    dst = parts_dram[bass.ds(g, 1), which].rearrange("g h a d n -> g a h d n")[0, part]
                    sp.dma_start(dst, split[:, 2 * which + part, :].bitcast(F32)).then_inc(parts_out[which], 16)

            def stack_q(g, s):
                for e in range(2):
                    for j in range(4):
                        row = P // 2 * e + HD * j
                        src = parts_dram[bass.ds(g, 1), 0].rearrange(
                            "g (r e) a d n -> g e a d r n", e=2)[0, e, j // 2]
                        dst = q_stack[s][row:row + HD, e:HEADS:2, :, :].rearrange("p r b t -> p r (b t)")
                        sp.dma_start(dst.bitcast(F32), src).then_inc(q_stacked[s], 16)

            def stack_k(g, s):
                for e in range(2):
                    src = parts_dram[bass.ds(g, 1), 1].rearrange("g (r e) a d n -> g e (a d) r n", e=2)[0, e]
                    for j in range(2):
                        row = P // 2 * e + 2 * HD * j
                        dst = k_stack[s][row:row + 2 * HD, :, :, :].rearrange("p r b t -> p r (b t)")
                        sp.dma_start(dst.bitcast(F32), src).then_inc(k_stacked[s], 16)

            def hold(signal, value):
                sp.wait_ge(signal, value)
                if not isinstance(value, int):
                    sp.sem_inc(sp_held, 1)

            def put_both(g):
                hold(q_split, g + 1)
                put(0, g)
                hold(k_split, g + 1)
                put(1, g)

            def stack_both(g, s, late):
                if late:
                    hold(scored, (g - 1) * GB)
                hold(parts_out[0], (g + 1) * 32)
                stack_q(g, s)
                hold(parts_out[1], (g + 1) * 32)
                stack_k(g, s)

            sp.wait_ge(km_set, 1)
            sp.dma_start(km_dram, qm[:, 1:2]).then_inc(km_out, 16)
            put_both(0)
            stack_both(0, 0, False)
            sp.wait_ge(km_out, 16)
            for e in range(2):
                for j in range(4):
                    row = P // 2 * e + HD * j
                    sp.dma_start(km_rows[row:row + HD, :],
                                 km_dram.rearrange("(r e) d -> e d r", e=2)[e],
                                 allow_slow_non_contiguous=True).then_inc(km_in, 16)
            put_both(1)
            stack_both(1, 1, False)
            put_both(2)

            def ahead(g, s):
                stack_both(g, s, True)
                put_both(g + 1)
            with sp.Fori(2, GROUPS - 3, 2) as g:
                ahead(g, 0)
                ahead(g + 1, 1)
            ahead(GROUPS - 2, 0)
            stack_both(GROUPS - 1, 1, True)

            def store(g):
                sp.wait_ge(y_taken, (g + 1) * EXPERTS)
                sp.dma_start(out[bass.ds(g * GB, GB), 1:TOKENS + 1, :].rearrange("b t c -> t b c"),
                             h[:, bass.ds(g * GB, GB), :]).then_inc(stored, 16)
            with sp.Fori(0, GROUPS, 1) as g:
                store(g)
            sp.wait_ge(y_taken, (GROUPS + 1) * EXPERTS)
            sp.dma_start(out[:, 0, :], h[0:BATCH, MT, :]).then_inc(stored, 16)
            sp.wait_ge(stored, 16 * (GROUPS + 1))

        @block.gpsimd
        def _(pool):
            def hold(signal, value):
                pool.wait_ge(signal, value)
                if not isinstance(value, int):
                    pool.sem_inc(pool_held, 1)

            for s in range(2):
                pool.memset(q_stack[s][:, :, :, :].bitcast(F32), 0.0).then_inc(pool_memsets, 1)
            def stage_a(g, s, first):
                hold(xn_done, g + 1)
                if first:
                    pool.wait_ge(marker_set, 1)
                pool.tensor_tensor(h[:, bass.ds(g * GB, GB), :], h[:, bass.ds(g * GB, GB), :],
                                   obias[:, :].rearrange("p (a n) -> p a n", a=1).to_broadcast([P, GB, HID]),
                                   ALU.add).then_inc(h_biased, 1)
                for which, halves in ((0, ("q", "qp")), (1, ("k", "kp"))):
                    x32 = q32[:, :, :] if which == 0 else k_all[:, bass.ds(g * GB, GB), :]
                    done = q_split if which == 0 else k_split
                    hi = split[:, 2 * which, :].rearrange("p (b t) -> p b t", b=GB)
                    lo = split[:, 2 * which + 1, :].rearrange("p (b t) -> p b t", b=GB)
                    hold(taken[halves[0]], g + 1)
                    hold(taken[halves[1]], g + 1)
                    if which == 0 and (not isinstance(g, int) or g >= 1):
                        hold(ready["smk"], g)
                    pool.tensor_tensor(x32, rope_a[:, which], rope_b[:, which],
                                       ALU.add).then_inc(rope_summed, 1)
                    hold(rope_summed, 2 * g + which + 1)
                    if not isinstance(g, int) or g >= 1:
                        hold(parts_out[which], g * 32)
                    pool.tensor_copy(hi, x32).then_inc(rope_high, 1)
                    hold(rope_high, 2 * g + which + 1)
                    pool.tensor_tensor(lo, x32, hi, ALU.subtract).then_inc(done, 1)
                if not isinstance(g, int) or g >= 1:
                    keep_v(g - 1, 1 - s)

            def keep_v(g, s):
                hold(taken["v"], g + 1)
                pool.tensor_copy(v_all[:, bass.ds(g * GB, GB), :], v_fix[:, s]).then_inc(v_kept, 1)

            stage_a(0, 0, True)
            stage_a(1, 1, False)
            with pool.Fori(2, GROUPS - 1, 2) as g:
                stage_a(g, 0, False)
                stage_a(g + 1, 1, False)
            keep_v(GROUPS - 1, 1)
            def keep(g, s):
                hold(x2t_taken, g + 1)
                pool.tensor_copy(x2T[:, bass.ds(g * GT, GT)], xnT[:, s, :]).then_inc(x2_kept, 1)
            with pool.Fori(0, GROUPS - 1, 2) as g:
                keep(g, 0)
                keep(g + 1, 1)
            pool.wait_ge(x2t_taken, GROUPS + 1)
            pool.tensor_copy(x2T[:, GROUPS * GT:], xnT[:, 0, 0:P]).then_inc(x2_kept, 1)
            pool.wait_ge(gate_done, 1)

            def regroup(g, s):
                if not isinstance(g, int):
                    hold(wT_ready, g - 1)
                pool.tensor_copy(wgrp[:, s, :].rearrange("p (b e) -> p b e", b=GB),
                                 gate[:, bass.ds(g * GB, GB), :]).then_inc(wgrp_done, 1)
            regroup(0, 0)
            regroup(1, 1)
            with pool.Fori(2, GROUPS - 1, 2) as g:
                regroup(g, 0)
                regroup(g + 1, 1)

        @block.scalar
        def _(act):
            act.wait_ge(consts_in, 16)
            nc.scalar.copy(ident_r[:, :], const("ident")).then_inc(ident_r_done, 1)

            def root(n):
                act.wait_ge(var_done, n)
                nc.scalar.activation(ln_tmp[:, 5, :], ln_tmp[:, 4, :], ACT.Sqrt).then_inc(std_done, 1)

            root(1)

            def take_xnT(g, s):
                act.wait_ge(ready["xnT"], g + 1)
                nc.scalar.copy(xnT[:, s, :], bank(6)).then_inc(taken["xnT"], 1)

            def take_v(g, s):
                act.wait_ge(ready["v"], g + 1)
                if not isinstance(g, int) or g >= 2:
                    act.wait_ge(v_kept, g - 1)
                nc.scalar.copy(v_fix[:, s], bank(7).rearrange("p (b n) -> p b n", b=GB)).then_inc(taken["v"], 1)

            def take_smk(g):
                act.wait_ge(ready["smk"], g + 1)
                nc.scalar.copy(smk_sb[:, bass.ds(g * GB, GB), :], bank(7).rearrange("p (b n) -> p b n", b=GB)[:, :, 0:HEADS]
                               ).then_inc(taken["smk"], 1)

            def exps(n, b, late):
                act.wait_ge(scored, n + 1)
                if late:
                    act.wait_ge(pv_done, n - 1)
                nc.scalar.activation(probs[:, b % 2].rearrange("p h t -> p (h t)"), bank(2, 2),
                                     ACT.Exp, scale=SCALE)
                mk = bank(4 + b % 2)[:, 384:512]
                nc.scalar.activation(pmk[:, b % 2, :], mk, ACT.Exp, scale=SCALE)
                at, _ = COLS["hide_high"]
                nc.scalar.activation(pmk_hid[:, b % 2, :], mk, ACT.Exp, bias=cst[:, at:at + 1],
                                     scale=SCALE).then_inc(exp_done, 1)

            def step(g, s):
                static = isinstance(g, int)
                for b in range(GB):
                    exps(g * GB + b, b, not static or g * GB + b >= 2)
                    if b == 0 and not (static and g + 2 >= GROUPS):
                        take_xnT(g + 2, s)
                    if b == 0 and not (static and g + 1 >= GROUPS):
                        take_v(g + 1, 1 - s)
                    if b == 3 and not (static and g + 2 >= GROUPS):
                        take_smk(g + 2)

            take_xnT(0, 0)
            take_smk(0)
            take_v(0, 0)
            take_xnT(1, 1)
            take_smk(1)
            groups(act, step)

            for half in range(2):
                act.wait_ge(mq_max, half + 1)
                nc.scalar.activation(pmq[:, half, :], bank(6 + half)[:, 0:P + 1], ACT.Exp,
                                     bias=mq[:, half, 1:2], scale=SCALE,
                                     accum_out=mq[:, half, 2:3]).then_inc(mq_exp, 1)
            root(2)

            def take_x2(g, s):
                act.wait_ge(x2t_ready, g + 1)
                if not isinstance(g, int) or g >= 2:
                    act.wait_ge(x2_kept, g - 1)
                    act.wait_ge(logits_ready, g - 1)
                nc.scalar.copy(xnT[:, s, :], bank(s)).then_inc(x2t_taken, 1)
            take_x2(0, 0)
            take_x2(1, 1)
            with act.Fori(2, GROUPS - 1, 2) as g:
                take_x2(g, 0)
                take_x2(g + 1, 1)
            act.wait_ge(x2t_ready, GROUPS + 1)
            act.wait_ge(x2_kept, GROUPS - 1)
            act.wait_ge(logits_ready, GROUPS - 1)
            nc.scalar.copy(xnT[:, 0, 0:P], bank(0)[:, 0:P]).then_inc(x2t_taken, 1)
            act.wait_ge(gap_done, 1)
            nc.scalar.activation(gs[:, 3, :], gs[:, 2, :], ACT.Exp).then_inc(gap_exp, 1)

            def gelu(n, e, cols, late):
                act.wait_ge(hid_ready, n + 1)
                if late:
                    act.wait_ge(y_ready, n - 1)
                at, _ = COLS["b1"]
                nc.scalar.activation(hid[:, e % 2, 0:cols], bank(e % 2)[:, 0:cols], ACT.Gelu,
                                     bias=cst[:, at + e:at + e + 1]).then_inc(gelu_done, 1)

            def experts(g, first=False):
                for e in range(EXPERTS):
                    gelu(g * EXPERTS + e, e, GT, not first or e >= 2)
                    if e == 1:
                        act.wait_ge(wT_ready, g + 1)
                        if not first:
                            act.wait_ge(b2_ready, g)
                        nc.scalar.copy(wgrpT[0:GB * EXPERTS, :],
                                       bank(5)[0:GB * EXPERTS, 0:P]).then_inc(wT_taken, 1)
            experts(0, True)
            with act.Fori(1, GROUPS, 1) as g:
                experts(g)
            for e in range(EXPERTS):
                gelu(GROUPS * EXPERTS + e, e, BATCH, True)
                if e == 1:
                    act.wait_ge(wT_ready, GROUPS + 1)
                    act.wait_ge(b2_ready, GROUPS)
                    nc.scalar.copy(wgrpT[0:EXPERTS, 0:BATCH],
                                   bank(5)[0:EXPERTS, 0:BATCH]).then_inc(wT_taken, 1)

        @block.vector
        def _(dve):
            v = nc.vector
            links = [0]

            def link(ins):
                links[0] += 1
                ins.then_inc(dve_chain, 1)
                dve.wait_ge(dve_chain, links[0])

            v.memset(ones[:, :], 1.0).then_inc(h_done, 1)
            v.memset(km_pad[:, :], 0.0).then_inc(taken["out"], 1)
            v.memset(qm_shift[:, :], 0.0).then_inc(h_done, 1)
            v.memset(wgrpT[:, :], 0.0)
            v.memset(km_stack[:, :, :].bitcast(F32), 0.0)
            for s in range(2):
                v.memset(negm[s][:, :].bitcast(F32), 0.0)
            link(v.memset(ones_head[:, :, :], 0.0))
            for e in range(2):
                v.memset(ones_head[:, e, HD * e:HD * e + HD], 1.0)
            v.memset(h[:, MT, :], 0.0).then_inc(memsets_done, 1)
            dve.wait_ge(memsets_done, 1)
            dve.wait_ge(consts_in, 16)
            dve.wait_ge(conv_in, 16)
            for table, acc in (("cb", cbw), ("cw", weff)):
                at, _ = COLS[table]
                for d in range(PER_CHAN):
                    for j in range(KCH):
                        c = at + j * PER_CHAN + d
                        w = cst[:, c:c + 1]
                        if d == 0:
                            ins = v.tensor_scalar(acc[:, j, :], conv_sb[:, j, d, :], w, None, ALU.mult)
                        else:
                            ins = v.scalar_tensor_tensor(out=acc[:, j, :], in0=conv_sb[:, j, d, :], scalar=w,
                                                         in1=acc[:, j, :], op0=ALU.mult, op1=ALU.add)
                    if d < PER_CHAN - 1:
                        link(ins)
                ins.then_inc(weff_done, 1)
            dve.wait_ge(bias_sum, 1)
            v.tensor_tensor(pe_bias[:, :], bank(2)[:, 0:HID], const("pe"), ALU.add).then_inc(pe_bias_done, 1)
            dve.wait_ge(pe_bias_done, 1)
            at, _ = COLS["marker"]
            link(v.tensor_copy(h[0:BATCH, MT, :], cst[0:BATCH, at:at + HID]))
            link(v.bn_stats(stats[:, MT, :], h[:, MT, :]))

            def grp(t, g):
                return t[:, bass.ds(g * GB, GB), :]

            def tok(g, s):
                dve.wait_ge(tok_done, g + 1)
                v.tensor_tensor(grp(h, g), bank(s).rearrange("p (b n) -> p b n", b=GB),
                                pe_bias[:, :].rearrange("p (a n) -> p a n", a=1).to_broadcast([P, GB, HID]),
                                ALU.add).then_inc(h_done, 1)
                dve.wait_ge(h_done, g + 3)
                for b in range(GB):
                    ins = v.bn_stats(stats[:, bass.ds(g * GB + b, 1), :].rearrange("p a n -> p (a n)"),
                               h[:, bass.ds(g * GB + b, 1), :].rearrange("p a n -> p (a n)"))
                ins.then_inc(stats_done, 1)
            with dve.Fori(0, GROUPS - 1, 2) as g:
                tok(g, 0)
                tok(g + 1, 1)

            norms = [0]

            def layernorm_scales():
                me, se, mo, so = (stats[:, :, c] for c in (1, 2, 4, 5))
                t = [ln_tmp[:, c, :] for c in range(6)]
                v.tensor_tensor(t[0], me, mo, ALU.add)
                v.tensor_tensor(t[1], me, mo, ALU.subtract)
                link(v.tensor_tensor(t[2], se, so, ALU.add))
                link(v.tensor_tensor(t[3], t[1], t[1], ALU.mult))
                link(v.scalar_tensor_tensor(out=t[1], in0=t[3], scalar=float(HID) / 4, in1=t[2],
                                            op0=ALU.mult, op1=ALU.add))
                v.tensor_scalar(t[4], t[1], 1.0 / HID, EPS, ALU.mult, ALU.add).then_inc(var_done, 1)
                norms[0] += 1
                dve.wait_ge(std_done, norms[0])
                link(v.reciprocal(rstd[:, :], t[5]))
                link(v.scalar_tensor_tensor(out=shift[:, :], in0=t[0], scalar=-0.5, in1=rstd[:, :],
                                            op0=ALU.mult, op1=ALU.mult))

            dve.wait_ge(stats_done, GROUPS)
            layernorm_scales()

            def normalize(dst, n):
                return v.tensor_scalar(dst, h[:, bass.ds(n, 1), :].rearrange("p a n -> p (a n)"),
                                       rstd[:, bass.ds(n, 1)], shift[:, bass.ds(n, 1)], ALU.mult, ALU.add)

            normalize(xn[:, 1, 0, :], MT).then_inc(setup_xn, 1)
            dve.wait_ge(setup_ready, 1)
            v.tensor_copy(xnT_m[:, :], bank(3)[:, 0:1]).then_inc(setup_taken, 1)
            bias_at, _ = COLS["bias"]
            v.tensor_scalar(bv_wide[:, :], ones[:, :], cst[:, bias_at + 4:bias_at + 5], None,
                            ALU.mult).then_inc(setup_taken, 1)
            dve.wait_ge(setup_ready, 2)
            v.tensor_tensor(qm[:, 0:1], bank(3)[:, 0:1], cst[:, bias_at:bias_at + 1], ALU.add)
            v.tensor_tensor(qm[:, 1:2], bank(3)[:, 1:2], cst[:, bias_at + 2:bias_at + 3],
                            ALU.add).then_inc(km_set, 1)
            dve.wait_ge(km_set, 1)
            v.tensor_scalar(km_pad[:, :].rearrange("p (a n) -> p a n", a=4)[:, :, 0:HEADS],
                            const("headmask").rearrange("p (a h) -> p a h", a=1).to_broadcast([P, 4, HEADS]),
                            qm[:, 1:2], None, ALU.mult)
            v.tensor_scalar(qm_shift[:, 120:120 + HEADS], const("headmask"), qm[:, 0:1], None, ALU.mult)
            v.tensor_scalar(qm_tiled[:, :, :],
                            const("headmask").rearrange("p (a h) -> p a h", a=1).to_broadcast([P, 16, HEADS]),
                            qm[:, 0:1], None, ALU.mult)
            v.tensor_copy(vm_row[:, :], bank(3)[0:1, 128:256])
            at, _ = COLS["low_key"]
            low_key = cst[:, at:at + 1]
            link(v.tensor_tensor(vm_heads[:, :], bank(3)[:, 128:256], const("headrows"), ALU.mult))
            v.scalar_tensor_tensor(out=one_parts[:, :], in0=const("headrows"), scalar=low_key,
                                   in1=const("headrows"), op0=ALU.mult, op1=ALU.subtract)
            link(v.tensor_scalar(vm_hid[:, :], vm_heads[:, :], low_key, None, ALU.mult))
            v.tensor_tensor(vm_parts[:, :], vm_hid[:, :], vm_heads[:, :], ALU.subtract)
            at, _ = COLS["parity"]
            for e in range(2):
                v.tensor_scalar(wo_head[:, e, :], wo_sb[:, :], cst[:, at + e:at + e + 1], None, ALU.mult)
            v.tensor_tensor(obias[:, :], bank(3)[:, 256:384], const("ob"), ALU.add).then_inc(marker_set, 1)
            dve.wait_ge(marker_set, 1)
            v.tensor_tensor(h[0:BATCH, MT, :], h[0:BATCH, MT, :], obias[0:BATCH, :], ALU.add)

            def make_xn(g, s):
                if not isinstance(g, int) or g >= 2:
                    dve.wait_ge(ready["xnT"], g - 1)
                for b in range(GB):
                    ins = normalize(xn[:, s, b, :], g * GB + b)
                ins.then_inc(xn_done, 1)

            def take(name, g):
                c = ("q", "qp", "k", "kp").index(name)
                bank_of = {"q": 7, "qp": 6, "k": 7, "kp": 6}[name]
                table = const("cos" if c % 2 == 0 else "sin")
                dst = (rope_a if c % 2 == 0 else rope_b)[:, c // 2]
                dve.wait_ge(ready[name], g + 1)
                if not isinstance(g, int) or g >= 1:
                    dve.wait_ge(rope_summed, 2 * g - 1 + c // 2)
                v.scalar_tensor_tensor(out=dst, in0=bank(bank_of).rearrange("p (b t) -> p b t", b=GB),
                                       scalar=cst[:, bias_at + c:bias_at + c + 1],
                                       in1=table.rearrange("p (a t) -> p a t", a=1).to_broadcast([P, GB, TOKENS]),
                                       op0=ALU.add, op1=ALU.mult).then_inc(taken[name], 1)

            def negmax_of(n, b, s, smk_ready, late):
                dve.wait_ge(max_scored, n + 1)
                v.tensor_reduce(negmax[:, b % 2, :], bank(0, 2).rearrange("p (h t) -> p h t", h=HEADS),
                                AX.X, ALU.max, negate=True).then_inc(row_max, 1)
                dve.wait_ge(row_max, n + 1)
                if smk_ready is not None:
                    dve.wait_ge(taken["smk"], smk_ready)
                if late:
                    dve.wait_ge(scored, n - 1)
                wide = [t.rearrange("p (a h) -> p a h", a=1).to_broadcast([P, 4, HEADS])
                        for t in (smk_sb[:, bass.ds(n, 1), :].rearrange("p a h -> p (a h)"),
                                  negmax[:, b % 2, :])]
                v.scalar_tensor_tensor(out=negm[b % 2][:, :].rearrange("p (a n) -> p a n", a=4)[:, :, 0:HEADS],
                                       in0=wide[0], scalar=-1.0, in1=wide[1], op0=ALU.mult, op1=ALU.min
                                       ).then_inc(negm_done, 1)

            def split_pmk(n, b):
                dve.wait_ge(exp_done, n + 1)
                v.tensor_tensor(pmk_parts[:, b % 2, :], pmk_hid[:, b % 2, :], pmk[:, b % 2, :], ALU.subtract
                                ).then_inc(pmk_split, 1)

            def norm(n, b, s):
                dve.wait_ge(pv_done, n + 1)
                od = bank(4 + b % 2)
                v.reciprocal(rec[:, b % 2, :], od[:, 256:384]).then_inc(rec_done, 1)
                dve.wait_ge(rec_done, n + 1)
                v.tensor_tensor(attT[:, s, b], od[:, 0:256].rearrange("p (e t) -> p e t", e=2),
                                rec[:, b % 2:b % 2 + 1, :].to_broadcast([P, 2, TOKENS]),
                                ALU.mult).then_inc(norm_done, 1)

            def take_out(g):
                dve.wait_ge(ready["out"], g + 1)
                dve.wait_ge(h_biased, g + 1)
                v.tensor_tensor(grp(h, g), bank(6).rearrange("p (b n) -> p b n", b=GB), grp(h, g),
                                ALU.add).then_inc(taken["out"], 1)
                dve.wait_ge(taken["out"], g + 2)
                for b in range(GB):
                    ins = v.bn_stats(stats[:, bass.ds(g * GB + b, 1), :].rearrange("p a n -> p (a n)"),
                                     h[:, bass.ds(g * GB + b, 1), :].rearrange("p a n -> p (a n)"))
                ins.then_inc(stats_done, 1)

            def stack_km():
                dve.wait_ge(km_in, 8 * 16)
                low, _ = COLS["low_row"]
                at, _ = COLS["row_parity"]
                link(v.tensor_scalar(km_hid[:, :], km_rows[:, :], cst[:, low:low + 1], None, ALU.mult))
                link(v.tensor_tensor(km_parts[:, :], km_rows[:, :], km_hid[:, :], ALU.subtract))
                for r in range(HEADS // 2):
                    ins = v.tensor_scalar(
                        km_stack[:, r, :].rearrange("p (a n) -> p a n", a=4)[:, :, 2 * r:2 * r + 2],
                        cst[:, at:at + 2].rearrange("p (a e) -> p a e", a=1).to_broadcast([P, 4, 2]),
                        km_parts[:, r:r + 1].bitcast(F32), None, ALU.mult)
                ins.then_inc(km_stacked, 1)

            make_xn(0, 0)
            make_xn(1, 1)
            for name in ("q", "qp", "k", "kp"):
                take(name, 0)
            make_xn(2, 0)
            for name in ("q", "qp", "k", "kp"):
                take(name, 1)
            stack_km()
            negmax_of(0, 0, 0, 1, False)
            negmax_of(1, 1, 0, None, False)

            def dve_step(g, s):
                static = isinstance(g, int)
                first = static and g == 0
                ahead = not (static and g + 2 >= GROUPS)
                last = static and g == GROUPS - 1
                n = g * GB
                if not first:
                    norm(n - 1, GB - 1, 1 - s)
                split_pmk(n, 0)
                negmax_of(n + 2, 2, s, None, True)
                if not (static and g + 3 >= GROUPS):
                    make_xn(g + 3, 1 - s)
                norm(n, 0, s)
                split_pmk(n + 1, 1)
                negmax_of(n + 3, 3, s, None, True)
                if ahead:
                    take("q", g + 2)
                    take("qp", g + 2)
                norm(n + 1, 1, s)
                split_pmk(n + 2, 2)
                if not last:
                    negmax_of(n + 4, 0, 1 - s, g + 2, True)
                if ahead:
                    take("k", g + 2)
                    take("kp", g + 2)
                norm(n + 2, 2, s)
                split_pmk(n + 3, 3)
                if not last:
                    negmax_of(n + 5, 1, 1 - s, None, True)
                if not first:
                    take_out(g - 1)

            groups(dve, dve_step)
            norm(BATCH - 1, 3, 1)
            take_out(GROUPS - 1)

            for half in range(2):
                dve.wait_ge(mq_step, half + 1)
                link(v.tensor_reduce(mq[:, half, 0:1], bank(6 + half)[:, 0:P + 1], AX.X, ALU.max))
                v.tensor_scalar(mq[:, half, 1:2], mq[:, half, 0:1], -SCALE, None,
                                ALU.mult).then_inc(mq_max, 1)
            for half in range(2):
                dve.wait_ge(mq_exp, half + 1)
                link(v.reciprocal(mq[:, half, 3:4], mq[:, half, 2:3]))
                v.tensor_scalar(pmq[:, half, :], pmq[:, half, :], mq[:, half, 3:4], None,
                                ALU.mult).then_inc(mq_norm, 1)
            dve.wait_ge(mq_step, 3)
            v.tensor_copy(pmqT[:, :, :], bank(4)[:, 0:2 * P].rearrange("p (a n) -> p a n", a=2))
            v.tensor_copy(pmm[:, :, :],
                          bank(5)[0:1, 0:2 * P].rearrange("p (a n) -> p a n", a=2)).then_inc(mq_copied, 1)
            dve.wait_ge(mq_step, 4)
            link(v.tensor_tensor(mq_sel[:, :, :],
                                 bank(6)[:, 0:BATCH * HEADS].rearrange("p (b h) -> p b h", b=BATCH),
                                 const("headmask").rearrange("p (a h) -> p a h", a=1)
                                 .to_broadcast([P, BATCH, HEADS]), ALU.mult))
            v.tensor_reduce(attT_m[:, :], mq_sel[:, :, :], AX.X, ALU.add).then_inc(mq_att, 1)
            dve.wait_ge(mq_step, 5)
            link(v.tensor_tensor(h[0:BATCH, MT, :], bank(7)[0:BATCH, 0:HID], h[0:BATCH, MT, :], ALU.add))
            link(v.bn_stats(stats[:, MT, :], h[:, MT, :]))
            dve.wait_ge(stats_done, 2 * GROUPS)
            layernorm_scales()

            def x2(g, s):
                if not isinstance(g, int) or g >= 2:
                    dve.wait_ge(x2t_ready, g - 1)
                for b in range(GB):
                    ins = normalize(xn[:, s, b, :], g * GB + b)
                ins.then_inc(x2n_done, 1)

            def take_logits(g, s, n=GB):
                dve.wait_ge(logits_ready, g + 1)
                at, _ = COLS["bg"]
                v.tensor_tensor(logits[:, bass.ds(g * GB, n), :],
                                bank(2 + s)[:, 0:n * P].rearrange("p (b e) -> p b e", b=n)[:, :, 0:EXPERTS],
                                const("bg").rearrange("p (a e) -> p a e", a=1).to_broadcast([P, n, EXPERTS]),
                                ALU.add).then_inc(logits_taken, 1)

            x2(0, 0)
            x2(1, 1)
            take_logits(0, 0)
            with dve.Fori(1, GROUPS - 2, 2) as g:
                x2(g + 1, 0)
                take_logits(g, 1)
                x2(g + 2, 1)
                take_logits(g + 1, 0)
            dve.wait_ge(x2t_ready, GROUPS - 1)
            normalize(xn[:, 0, 0, :], MT).then_inc(x2n_done, 1)
            take_logits(GROUPS - 1, 1)
            take_logits(GROUPS, 0, 1)
            dve.wait_ge(logits_taken, GROUPS + 1)

            def wide(t):
                return t.rearrange("p (n a) -> p n a", a=1).to_broadcast([P, TILES, EXPERTS])

            rank = const("rank").rearrange("p (a e) -> p a e", a=1).to_broadcast([P, TILES, EXPERTS])

            def best(scores, top, pick, tmp):
                link(v.tensor_reduce(top, scores, AX.X, ALU.max))
                link(v.tensor_tensor(tmp, scores, wide(top), ALU.is_equal))
                link(v.tensor_tensor(tmp, tmp, rank, ALU.mult))
                link(v.tensor_reduce(gs[:, 7, :], tmp, AX.X, ALU.max))
                link(v.tensor_tensor(pick, tmp, wide(gs[:, 7, :]), ALU.is_equal))

            best(logits[:, :, :], gs[:, 0, :], gt[:, 0], gt[:, 2])
            link(v.scalar_tensor_tensor(out=gt[:, 3], in0=gt[:, 0], scalar=-3.0e38, in1=logits[:, :, :],
                                        op0=ALU.mult, op1=ALU.add))
            best(gt[:, 3], gs[:, 1, :], gt[:, 1], gt[:, 2])
            v.tensor_tensor(gs[:, 2, :], gs[:, 1, :], gs[:, 0, :], ALU.subtract).then_inc(gap_done, 1)
            dve.wait_ge(gap_exp, 1)
            link(v.tensor_scalar(gs[:, 4, :], gs[:, 3, :], 1.0, None, ALU.add))
            link(v.reciprocal(gs[:, 5, :], gs[:, 4, :]))
            link(v.tensor_tensor(gs[:, 6, :], gs[:, 5, :], gs[:, 3, :], ALU.mult))
            v.tensor_tensor(gt[:, 2], gt[:, 0], wide(gs[:, 5, :]), ALU.mult)
            link(v.tensor_tensor(gt[:, 3], gt[:, 1], wide(gs[:, 6, :]), ALU.mult))
            v.tensor_tensor(gate[:, :, :], gt[:, 2], gt[:, 3], ALU.add).then_inc(gate_done, 1)
            dve.wait_ge(gate_done, 1)

            def add_y(m, e, g, tiles, rows):
                dve.wait_ge(y_ready, m + 1)
                for b in range(tiles):
                    t = h[0:rows, bass.ds(g * GB + b, 1), :].rearrange("p a n -> p (a n)")
                    w = gate[0:rows, bass.ds(g * GB + b, 1), e]
                    ins = v.scalar_tensor_tensor(out=t, in0=bank(2 + e % 2)[0:rows, b * P:b * P + P],
                                                 scalar=w, in1=t, op0=ALU.mult, op1=ALU.add)
                ins.then_inc(y_taken, 1)
                dve.wait_ge(y_taken, m + 1)

            def add_experts(g, tiles, rows):
                for e in range(EXPERTS):
                    add_y(g * EXPERTS + e, e, g, tiles, rows)
                    if e == 3:
                        dve.wait_ge(b2_ready, g + 1)
                        t = h[0:rows, bass.ds(g * GB, tiles), :]
                        v.tensor_tensor(t, bank(4)[0:rows, 0:tiles * P].rearrange("p (b n) -> p b n", b=tiles),
                                        t, ALU.add).then_inc(b2_taken, 1)
                        dve.wait_ge(b2_taken, g + 1)

            with dve.Fori(0, GROUPS, 1) as g:
                add_experts(g, GB, P)
            add_experts(GROUPS, 1, BATCH)

        @block.tensor
        def _(pe):
            mm = nc.tensor.matmul
            pe.wait_ge(memsets_done, 1)
            pe.wait_ge(consts_in, 16)
            pe.wait_ge(weff_done, 1)
            for j in range(KCH):
                ins = mm(bank(2)[:, 0:HID], ones[:, :], cbw[:, j, :], start=(j == 0), stop=(j == KCH - 1))
            ins.then_inc(bias_sum, 1)
            pe.wait_ge(weff_done, 2)

            def tok(g, slot, landed):
                pe.wait_ge(x_in[slot], landed)
                pe.wait_ge(h_done, g + 1)
                for b in range(GB):
                    for j in range(KCH):
                        ins = mm(bank(slot % 2)[:, b * P:(b + 1) * P], x_sb[:, slot, j, b * P:(b + 1) * P],
                                 weff[:, j, :], start=(j == 0), stop=(j == KCH - 1))
                ins.then_inc(tok_done, 1)
            with pe.Fori(0, GROUPS - XSLOTS + 1, XSLOTS) as g:
                for slot in range(XSLOTS):
                    tok(g + slot, slot, g * (16 // XSLOTS) + 16)

            ident = const("ident")
            pe.wait_ge(setup_xn, 1)
            nc.tensor.transpose(bank(3)[:, 0:P], xn[:, 1, 0, :], ident).then_inc(setup_ready, 1)
            pe.wait_ge(setup_taken, 2)
            pe.wait_ge(weights_in, 32)
            mm(bank(3)[:, 0:1], wqkv_sb[:, 0, :], xnT_m[:, 0:1], start=True, stop=True)
            mm(bank(3)[:, 1:2], wqkv_sb[:, 2, :], xnT_m[:, 0:1], start=True, stop=True)
            mm(bank(3)[:, 128:256], xnT_m[:, 0:1].to_broadcast([P, P]), wqkv_sb[:, 4, :], start=True, stop=True)
            mm(bank(3)[:, 256:384], bv_wide[:, :], wo_sb[:, :], start=True, stop=True).then_inc(setup_ready, 1)

            def transposes(g, s):
                pe.wait_ge(xn_done, g + 1)
                if not isinstance(g, int) or g >= 1:
                    pe.wait_ge(taken["kp"], g)
                if not isinstance(g, int) or g >= 3:
                    pe.wait_ge(taken["out"], g - 2)
                for b in range(GB):
                    ins = nc.tensor.transpose(bank(6)[:, b * P:(b + 1) * P], xn[:, s, b, :], ident)
                ins.then_inc(ready["xnT"], 1)

            def project(name, g, s):
                if name in ("q", "qp"):
                    pe.wait_ge(taken["xnT"], g + 1)
                if name == "q" and (not isinstance(g, int) or g >= 1):
                    pe.wait_ge(taken["v"], g)
                if name in ("k", "kp"):
                    pe.wait_ge(taken[{"k": "q", "kp": "qp"}[name]], g + 1)
                c = ("q", "qp", "k", "kp").index(name)
                mm(bank(7 if c % 2 == 0 else 6), wqkv_sb[:, c, :], xnT[:, s, :], start=True,
                   stop=True).then_inc(ready[name], 1)

            def project_v(g, s):
                pe.wait_ge(taken["smk"], g + 1)
                for b in range(GB):
                    ins = mm(bank(7)[:, b * P:(b + 1) * P], xnT[:, s, b * P:(b + 1) * P], wqkv_sb[:, 4, :],
                             start=True, stop=True)
                ins.then_inc(ready["v"], 1)

            def marker_scores(g):
                pe.wait_ge(taken["k"], g + 1)
                pe.wait_ge(q_split, g + 1)
                for b in range(GB):
                    ins = mm(bank(7)[:, b * P:(b + 1) * P], q32[:, b, :], km_pad[:, :],
                             start=True, stop=True)
                ins.then_inc(ready["smk"], 1)

            def project_out(g, s, last=False):
                pe.wait_ge(norm_done, (g + 1) * GB)
                if not last:
                    pe.wait_ge(taken["kp"], g + 4)
                else:
                    pe.wait_ge(taken["out"], g + 1)
                for b in range(GB):
                    for e in range(2):
                        ins = mm(bank(6)[:, b * P:(b + 1) * P], attT[:, s, b, e, :], wo_head[:, e, :],
                                 start=(e == 0), stop=(e == 1))
                ins.then_inc(ready["out"], 1)

            def score_max(n, b, s, landed):
                if landed is not None:
                    pe.wait_ge(q_stacked[s], landed[0])
                    pe.wait_ge(k_stacked[s], landed[1])
                if not (isinstance(n, int) and n == 0):
                    pe.wait_ge(negm_done, n)
                for hd in range(HEADS):
                    ins = mm(bank(hd // 4)[:, hd % 4 * P:(hd % 4 + 1) * P], q_stack[s][:, hd, b, :],
                             k_stack[s][:, hd // 2, b, :], start=True, stop=True)
                ins.then_inc(max_scored, 1)

            def score(n, b, s):
                pe.wait_ge(negm_done, n + 1)
                if not (isinstance(n, int) and n == 0):
                    pe.wait_ge(exp_done, n)
                nm = negm[b % 2]
                for r in range(HEADS // 2):
                    at = r % 2 * 2 * P
                    mm(bank(2 + r // 2)[:, at:at + 2 * P], k_stack[s][:, r, b, :],
                       q_stack[s][:, 2 * r:2 * r + 2, b, :], start=True, stop=False)
                    for e in range(2):
                        mm(bank(2 + r // 2)[:, at + e * P:at + (e + 1) * P],
                           nm[:, 2 * r + e:2 * r + e + 1].to_broadcast([P, P]), ident_r[:, :],
                           start=False, stop=(e == 1))
                if not isinstance(n, int) or n >= 2:
                    pe.wait_ge(norm_done, n - 1)
                mk = bank(4 + b % 2)[:, 384:512]
                mm(mk, nm[:, :], ident_r[:, :], start=True, stop=False)
                for hd in range(HEADS):
                    ins = mm(mk, km_stack[:, hd // 2, :], q_stack[s][:, hd, b, :], start=False,
                             stop=(hd == HEADS - 1))
                ins.then_inc(scored, 1)

            def weigh(n, b, s):
                pe.wait_ge(exp_done, n + 1)
                pe.wait_ge(pmk_split, n + 1)
                od = bank(4 + b % 2)
                mm(od[:, 0:256].rearrange("p (e t) -> p e t", e=2), vm_parts[:, :],
                   pmk_parts[:, b % 2:b % 2 + 1, :].to_broadcast([P, 2, TOKENS]), start=True, stop=False)
                for r in range(HEADS // 2):
                    mm(od[32 * r:32 * r + 32, 0:256], v_fix[:, s, b, 32 * r:32 * r + 32],
                       probs[:, b % 2, 2 * r:2 * r + 2, :].rearrange("p e t -> p (e t)"),
                       start=False, stop=True)
                mm(od[:, 256:384], one_parts[:, :], pmk_parts[:, b % 2, :], start=True, stop=False)
                for e in range(2):
                    for r in range(HEADS // 2):
                        ins = mm(od[32 * r:32 * r + 32, 256:384], ones_head[:, e, :],
                                 probs[:, b % 2, 2 * r + e, :], start=False, stop=(e == 1))
                ins.then_inc(pv_done, 1)

            def landed(g, s):
                if isinstance(g, int):
                    return 16 * NQ * (g // 2 + 1), 16 * NK * (g // 2 + 1)
                return (g - s) * (8 * NQ) + 16 * NQ, (g - s) * (8 * NK) + 16 * NK

            pe.wait_ge(ident_r_done, 1)
            pe.wait_ge(marker_set, 1)
            for g in range(2):
                transposes(g, g)
                for name in ("q", "qp", "k", "kp"):
                    project(name, g, g)
                marker_scores(g)
                if g == 0:
                    project_v(0, 0)
            score_max(0, 0, 0, landed(0, 0))
            score_max(1, 1, 0, None)
            pe.wait_ge(km_stacked, 1)

            def step(g, s):
                static = isinstance(g, int)
                first = static and g == 0
                ahead = not (static and g + 2 >= GROUPS)
                last = static and g == GROUPS - 1
                n = g * GB
                score(n, 0, s)
                if not first:
                    weigh(n - 1, GB - 1, 1 - s)
                score_max(n + 2, 2, s, None)
                if ahead:
                    transposes(g + 2, s)
                if not last:
                    project_v(g + 1, 1 - s)
                score(n + 1, 1, s)
                weigh(n, 0, s)
                score_max(n + 3, 3, s, None)
                if ahead:
                    project("q", g + 2, s)
                    project("qp", g + 2, s)
                score(n + 2, 2, s)
                weigh(n + 1, 1, s)
                if not last:
                    score_max(n + 4, 0, 1 - s, landed(g + 1, 1 - s))
                if ahead:
                    project("k", g + 2, s)
                    project("kp", g + 2, s)
                score(n + 3, 3, s)
                weigh(n + 2, 2, s)
                if not last:
                    score_max(n + 5, 1, 1 - s, None)
                if not first:
                    project_out(g - 1, 1 - s, not ahead)
                if ahead:
                    marker_scores(g + 2)

            groups(pe, step)
            weigh(BATCH - 1, 3, 1)
            project_out(GROUPS - 1, 1, True)

            pe.wait_ge(taken["out"], GROUPS + 1)
            for half in range(2):
                for b in range(16):
                    mm(bank(6 + half)[:, 0:P], qm_shift[:, 120 - HEADS * b:248 - HEADS * b],
                       k_all[:, 16 * half + b, :], start=(b == 0), stop=(b == 15))
                mm(bank(6 + half)[:, P:P + 1], qm_tiled[:, :, :].rearrange("p a h -> p (a h)"), qm[:, 1:2],
                   start=True, stop=True).then_inc(mq_step, 1)
            pe.wait_ge(norm_done, BATCH)
            for half in range(2):
                pe.wait_ge(mq_norm, half + 1)
                nc.tensor.transpose(bank(4)[:, half * P:(half + 1) * P], pmq[:, half, 0:P], ident)
                ins = mm(bank(5)[0:1, half * P:(half + 1) * P], pmq[:, half, P:P + 1], ident,
                         start=True, stop=True)
            ins.then_inc(mq_step, 1)
            pe.wait_ge(mq_copied, 1)
            pe.wait_ge(v_kept, GROUPS)
            mm(bank(6)[:, 0:BATCH * HEADS], vm_row[:, :], pmm[:, :, :].rearrange("p a n -> p (a n)"),
               start=True, stop=False, skip_group_check=True)
            for b in range(BATCH):
                ins = mm(bank(6)[:, b * HEADS:(b + 1) * HEADS], v_all[:, b, :],
                         pmqT[:, :, :].rearrange("p a n -> p (a n)")[:, b * HEADS:(b + 1) * HEADS],
                         start=False, stop=(b == BATCH - 1), skip_group_check=True)
            ins.then_inc(mq_step, 1)
            pe.wait_ge(mq_att, 1)
            mm(bank(7)[0:BATCH, 0:HID], attT_m[:, :], wo_sb[:, :], start=True, stop=True).then_inc(mq_step, 1)

            def x2(g, s):
                pe.wait_ge(x2n_done, g + 1)
                if not isinstance(g, int) or g >= 2:
                    pe.wait_ge(x2t_taken, g - 1)
                for b in range(GB):
                    ins = nc.tensor.transpose(bank(s)[:, b * P:(b + 1) * P], xn[:, s, b, :], ident)
                ins.then_inc(x2t_ready, 1)

            wg_at, _ = COLS["wg"]

            def gate_logits(g, s, tiles=GB):
                pe.wait_ge(x2t_taken, g + 1)
                if not isinstance(g, int) or g >= 1:
                    pe.wait_ge(logits_taken, g)
                for b in range(tiles):
                    ins = mm(bank(2 + s)[:, b * P:(b + 1) * P], xnT[:, s, b * P:(b + 1) * P],
                             cst[:, wg_at:wg_at + P], start=True, stop=True)
                ins.then_inc(logits_ready, 1)

            x2(0, 0)
            x2(1, 1)
            gate_logits(0, 0)
            with pe.Fori(1, GROUPS - 2, 2) as g:
                x2(g + 1, 0)
                gate_logits(g, 1)
                x2(g + 2, 1)
                gate_logits(g + 1, 0)
            pe.wait_ge(x2n_done, GROUPS + 1)
            pe.wait_ge(x2t_taken, GROUPS - 1)
            nc.tensor.transpose(bank(0)[:, 0:P], xn[:, 0, 0, :], ident).then_inc(x2t_ready, 1)
            gate_logits(GROUPS - 1, 1)
            gate_logits(GROUPS, 0, 1)

            pe.wait_ge(ffn_in, 48)
            pe.wait_ge(x2_kept, GROUPS + 1)
            pe.wait_ge(logits_taken, GROUPS + 1)

            def hidden(n, e, g, cols, late):
                if late:
                    pe.wait_ge(gelu_done, n - 1)
                mm(bank(e % 2)[:, 0:cols], w1_sb[:, e, :], x2T[:, bass.ds(g * GT, cols)], start=True,
                   stop=True).then_inc(hid_ready, 1)

            def expert_out(n, e, tiles, rows, late):
                pe.wait_ge(gelu_done, n + 1)
                if late:
                    pe.wait_ge(y_taken, n - 1)
                for b in range(tiles):
                    ins = mm(bank(2 + e % 2)[0:rows, b * P:(b + 1) * P], hid[:, e % 2, b * P:b * P + rows],
                             w2_sb[:, e, :], start=True, stop=True)
                ins.then_inc(y_ready, 1)

            def gates_up(g, s, tiles, rows, late):
                if tiles == GB:
                    pe.wait_ge(wgrp_done, g + 1)
                if late:
                    pe.wait_ge(wT_taken, g)
                src = wgrp[:, s, :] if tiles == GB else gate[0:BATCH, MT, :]
                idn = ident if tiles == GB else cst[0:BATCH, COLS["ident"][0]:COLS["ident"][0] + BATCH]
                mm(bank(5)[0:tiles * EXPERTS, 0:rows], src, idn, start=True, stop=True).then_inc(wT_ready, 1)

            def second_bias(g, s, tiles, rows, late):
                pe.wait_ge(wT_taken, g + 1)
                if late:
                    pe.wait_ge(b2_taken, g)
                mm(bank(4)[0:rows, 0:tiles * P], wgrpT[:, 0:rows],
                   b2_sb[:, 0:tiles, :].rearrange("p b n -> p (b n)"), start=True,
                   stop=True).then_inc(b2_ready, 1)

            def experts(g, s, tiles, rows, cols, first, nexts):
                for e in range(EXPERTS):
                    n = g * EXPERTS + e
                    if e < EXPERTS - 1:
                        hidden(n + 1, e + 1, g, cols, not first or e >= 1)
                    elif nexts is not None:
                        hidden(n + 1, 0, g + 1, nexts, True)
                    expert_out(n, e, tiles, rows, not first or e >= 2)
                    if e == 0:
                        gates_up(g, s, tiles, rows, not first)
                    if e == 2:
                        second_bias(g, s, tiles, rows, not first)

            hidden(0, 0, 0, GT, False)
            experts(0, 0, GB, P, GT, True, GT)
            with pe.Fori(1, GROUPS - 2, 2) as g:
                experts(g, 1, GB, P, GT, False, GT)
                experts(g + 1, 0, GB, P, GT, False, GT)
            experts(GROUPS - 1, 1, GB, P, GT, False, BATCH)
            experts(GROUPS, 0, 1, BATCH, BATCH, False, None)


def columns():
    return COLS


def kernel(**inputs):
    from concourse import bacc
    from concourse.bass_utils import run_bass_kernel_spmd

    a = {n: np.asarray(t) for n, t in inputs.items()}
    f = np.float32

    x = a["x"].reshape(GROUPS, GB, TOKENS, KCH, P).transpose(0, 4, 3, 1, 2)
    conv = a["L0_tok_conv_w"].reshape(HID, MAX_CHANS, PER_CHAN, PATCH)[:, :CHANS]
    conv = conv.transpose(3, 1, 2, 0).reshape(KCH, P, PER_CHAN, HID).transpose(1, 0, 2, 3)

    def chan(t):
        return np.tile(t[:CHANS], (PATCH, 1)).reshape(KCH, P, PER_CHAN).transpose(1, 0, 2).reshape(P, -1)

    def rows(t):
        return np.broadcast_to(t, (P, t.shape[-1]))

    pos = np.arange(TOKENS, dtype=f)[:, None]
    freq = np.exp(-(f(2) * np.arange(HID // 2, dtype=f)[None] / f(HID)) * np.log(f(10000.0)))
    angle = pos * freq
    pe = np.stack([np.sin(angle), np.cos(angle)], -1).reshape(TOKENS, HID)
    half = HD // 2
    inv = f(1) / f(10000.0) ** (np.arange(0, HD, 2, dtype=f) / f(HD))
    angle = np.arange(1, TOKENS + 1, dtype=f)[None] * inv[:, None]
    cos, sin = np.cos(angle), np.sin(angle)
    sin[:half // 2] *= -1
    cos, sin = (np.tile(t, (P // half, 1)) for t in (cos, sin))
    head = np.arange(P)[:, None] // HD == np.arange(HEADS)[None]
    headrows = np.zeros((P, P), f)
    for block in range(4):
        headrows[32 * block:32 * block + HEADS] = head.T
    swap = np.arange(P) ^ (half // 2)

    w, b = a["L0_attn_qkv_w"].reshape(3, P, HID), a["L0_attn_qkv_b"].reshape(3, P)
    wqkv = np.stack([w[0], w[0][swap], w[1], w[1][swap], w[2]]).transpose(2, 0, 1)
    bias = np.stack([b[0], b[0][swap], b[1], b[1][swap], b[2]], 1)
    parts = {
        "pe": pe, "cos": cos, "sin": sin, "ident": np.eye(P, dtype=f), "headmask": head.astype(f),
        "headrows": headrows, "rank": rows(np.arange(EXPERTS, 0, -1, dtype=f)),
        "cw": chan(a["L0_tok_chan_w"]), "cb": chan(a["L0_tok_chan_b"]),
        "marker": rows(a["L0_tok_marker"]), "bias": bias, "ob": rows(a["L0_attn_out_b"]),
        "bg": rows(a["L0_ffn_bg"]), "wg": a["L0_ffn_Wg"], "b1": a["L0_ffn_b1"].T,
        "parity": np.stack([np.arange(P) // HD % 2 == e for e in range(2)], 1).astype(f),
        "row_parity": np.stack([np.arange(P) // (P // 2) == e for e in range(2)], 1).astype(f),
        "low_row": (np.arange(P) // HD % 2).astype(f)[:, None],
        "low_key": (np.arange(P) // 64 == 1).astype(f)[:, None],
        "hide_high": np.where(np.arange(P) // 32 % 2 == 0, f(-1e30), f(0))[:, None],
    }
    b2bd = np.zeros((P, GB, HID), f)
    for t in range(GB):
        b2bd[t * EXPERTS:(t + 1) * EXPERTS, t] = a["L0_ffn_b2"]
    arrays = {
        "xt": x, "convw": conv, "consts": np.concatenate([parts[n] for n in COLS], 1).astype(f),
        "wqkv": wqkv, "wo": a["L0_attn_out_w"].T, "w1": a["L0_ffn_W1"].transpose(1, 0, 2),
        "w2": a["L0_ffn_W2"].transpose(1, 0, 2), "b2bd": b2bd,
    }
    arrays = {n: np.ascontiguousarray(t) for n, t in arrays.items()}
    nc = bacc.Bacc("TRN2", target_bir_lowering=False, num_devices=1)
    args = [nc.dram_tensor(n, t.shape, mybir.dt.from_np(t.dtype), kind="ExternalInput").ap()
            for n, t in arrays.items()]
    out = nc.dram_tensor("out", (BATCH, TOKENS + 1, HID), F32, kind="ExternalOutput").ap()
    audio_tower_kernel(nc, *args, out)
    r = run_bass_kernel_spmd(nc, [arrays], core_ids=[0])
    return r.results[0]["out"]
```

```python
from contextlib import ExitStack

import numpy as np

import concourse.bass as bass
from concourse import mybir

ALU = mybir.AluOpType
ACT = mybir.ActivationFunctionType
F32 = mybir.dt.float32
F32R = mybir.dt.float32r
I32 = mybir.dt.int32
AX = mybir.AxisListType

P = 128
BATCH, T_RAW, CHANS = 32, 1024, 48
PATCH, PER_CHAN, MAX_CHANS = 8, 8, 64
TOKENS = T_RAW // PATCH
HID = 128
HEADS, HD = 8, 16
EXPERTS = 8
KCH = PATCH * CHANS // P
GB = 4
GROUPS = BATCH // GB
GT = GB * TOKENS
TILES = BATCH + 1
MT = BATCH
EPS = 1e-5
SCALE = HD ** -0.5
XSLOTS = 4
EARLY = 5

COLS = {}


def _columns():
    at = 0
    for name, n in (("wg", EXPERTS), ("pe", HID), ("cos", TOKENS), ("sin", TOKENS), ("ident", P), ("headmask", HEADS),
                    ("headrows", P), ("rank", EXPERTS), ("cw", KCH * PER_CHAN), ("cb", KCH * PER_CHAN),
                    ("marker", HID), ("bias", 5), ("ob", HID), ("bg", EXPERTS),
                    ("b1", EXPERTS), ("low_key", 1), ("low_prob", 1), ("hide_high", 1),
                    ("query_head", HID), ("query_batch", GB), ("query_row", 16)):
        COLS[name] = (at, n)
        at += n
    return at


NCOLS = _columns()


def audio_tower_kernel(nc, xt, convw, consts, wqkv, wo, w1, w2, b2bd, out):
    parts_dram = nc.dram_tensor("parts_dram", [GROUPS, 2, HEADS, 2, HD, GT], F32).ap()
    ctx = ExitStack()
    with ctx:
        def sb(name, shape, dt=F32):
            return ctx.enter_context(nc.sbuf_tensor(name, shape, dt))

        def sem(name):
            return ctx.enter_context(nc.semaphore(name))

        cst = sb("cst", [P, NCOLS])

        def const(name):
            at, n = COLS[name]
            return cst[:, at:at + n]

        conv_sb = sb("conv_sb", [P, KCH, PER_CHAN, HID])
        weff = sb("weff", [P, KCH, HID])
        ones = sb("ones", [P, P])
        pe_bias = sb("pe_bias", [P, HID])
        x_sb = sb("x_sb", [P, XSLOTS, KCH, GT])
        h = sb("h", [P, TILES, HID])
        stats = sb("stats", [P, TILES, 6])
        ln_tmp = sb("ln_tmp", [P, 5, TILES])
        rstd = sb("rstd", [P, TILES])
        shift = sb("shift", [P, TILES])
        wqkv_sb = sb("wqkv_sb", [P, 5, HID])
        wo_sb = sb("wo_sb", [P, HID])
        ident_r = sb("ident_r", [P, P], F32R)
        ones_head = sb("ones_head", [P, 2, 32])
        xn = sb("xn", [P, 2, GB, HID])
        xnT = sb("xnT", [P, 2, GT])
        xnT_m = sb("xnT_m", [P, 1])
        rope_a = sb("rope_a", [P, 2, GB, TOKENS])
        rope_b = sb("rope_b", [P, 2, GB, TOKENS])
        q32 = sb("q32", [P, GB, TOKENS])
        k_all = sb("k_all", [P, BATCH, TOKENS])
        v_all = sb("v_all", [P, BATCH, HID])
        split = sb("split", [P, 4, GT], F32R)
        q_stack = [sb(f"q_stack{s}", [P, HEADS, GB, TOKENS], F32R) for s in range(2)]
        k_stack = [sb(f"k_stack{s}", [P, HEADS // 2, GB, TOKENS], F32R) for s in range(2)]
        v_fix = sb("v_fix", [P, 2, 2, GB, HID])
        smk_sb = sb("smk_sb", [P, BATCH, HEADS])
        negmax = sb("negmax", [P, 2, HEADS])
        negm = [sb(f"negm{s}", [P, P], F32R) for s in range(2)]
        probs = sb("probs", [P, 2, HEADS, TOKENS])
        pmk = sb("pmk", [P, 2, TOKENS])
        pmk_hid = sb("pmk_hid", [P, 2, TOKENS], F32R)
        pmk_parts = sb("pmk_parts", [P, 2, TOKENS], F32R)
        rec = sb("rec", [P, 2, TOKENS])
        attT = sb("attT", [P, 2, GB, TOKENS])
        obias = sb("obias", [P, HID])
        qm = sb("qm", [P, 2])
        km_pad = sb("km_pad", [P, P])
        mk_row = sb("mk_row", [P, 2, GT])
        mk_less = sb("mk_less", [P, 2, TOKENS])
        qm_shift = sb("qm_shift", [P, 7 * HEADS])
        qm_tiled = sb("qm_tiled", [P, P // HEADS, HEADS])
        vm_rows = sb("vm_rows", [P, HID])
        vm_parts = sb("vm_parts", [P, HID], F32R)
        one_parts = sb("one_parts", [P, HID], F32R)
        gelu_ready = sb("gelu_ready", [P, 1])
        mq = sb("mq", [P, 2, 4])
        attT_m = sb("attT_m", [P, BATCH])
        vm_heads, vm_hid, bv_wide = mk_less[:, 0, :], pmk_hid[:, 0, :], rope_a[:, 0, 0, :]
        conv_flat = conv_sb[:, :, :, :].rearrange("p a b c -> p (a b c)")
        w1_sb = conv_flat[:, 0:EXPERTS * HID].rearrange("p (e n) -> p e n", e=EXPERTS)
        w2_sb = conv_flat[:, EXPERTS * HID:2 * EXPERTS * HID].rearrange("p (e n) -> p e n", e=EXPERTS)
        b2_sb = conv_flat[:, 2 * EXPERTS * HID:(2 * EXPERTS + GB) * HID].rearrange("p (b n) -> p b n", b=GB)
        b2_parts = split[:, 0, :].rearrange("p (b n) -> p b n", b=GB)
        x_flat = x_sb[:, :, :, :].rearrange("p a b c -> p (a b c)")
        x2T = x_flat[:, 0:TILES * P]
        ra, rb = (t[:, :, :, :].rearrange("p a b c -> p (a b c)") for t in (rope_a, rope_b))
        pmq = ra[:, 0:2 * (P + 1)].rearrange("p (a n) -> p a n", a=2)
        pmqT = rb[:, 0:2 * P].rearrange("p (a n) -> p a n", a=2)
        mq_sel = rb[:, 2 * P:4 * P].rearrange("p (a n) -> p a n", a=2)
        TE = TILES * EXPERTS
        at = TILES * P
        logits = x_flat[:, at:at + TE].rearrange("p (n e) -> p n e", n=TILES)
        gate = x_flat[:, at + TE:at + 2 * TE].rearrange("p (n e) -> p n e", n=TILES)
        gt = x_flat[:, at + 2 * TE:at + 6 * TE].rearrange("p (a n e) -> p a n e", a=4, n=TILES)
        gs = x_flat[:, at + 6 * TE:at + 7 * TE].rearrange("p (a n) -> p a n", a=8)
        hid = probs[:, :, :, :].rearrange("p a b c -> p a (b c)")[:, :, 0:GT]
        wgrp = pe_bias[:, :]
        wgrpT = sb("wgrpT", [P, P], F32R)

        banks = ctx.enter_context(nc.psum_tensor("banks", [P, 8, 512], F32))

        def bank(n, k=1):
            return banks[:, n:n + k, :].rearrange("p a b -> p (a b)")

        consts_in = sem("consts_in")
        conv_in = [sem(f"conv_in{n}") for n in range(PER_CHAN // 2)]
        weights_in = sem("weights_in")
        ffn_in = sem("ffn_in")
        x_in = [sem(f"x_in{s}") for s in range(XSLOTS)]
        memsets_done = sem("memsets_done")
        pool_memsets = sem("pool_memsets")
        dve_chain = sem("dve_chain")
        pool_held = sem("pool_held")
        sp_held = sem("sp_held")
        mk_shifted = sem("mk_shifted")
        probs_exp = sem("probs_exp")
        bias_sum = sem("bias_sum")
        setup_xn = sem("setup_xn")
        stats_done = sem("stats_done")
        rope_summed = sem("rope_summed")
        rope_high = sem("rope_high")
        row_max = sem("row_max")
        pe_bias_done = sem("pe_bias_done")
        weff_done = sem("weff_done")
        tok_done = sem("tok_done")
        h_done = sem("h_done")
        xn_done = sem("xn_done")
        ready = {k: sem(f"{k}_ready") for k in ("xnT", "q", "qp", "k", "kp", "v", "smk", "mk", "out")}
        taken = {k: sem(f"{k}_taken") for k in ("xnT", "q", "qp", "k", "kp", "v", "smk", "mk", "out")}
        setup_ready = sem("setup_ready")
        setup_taken = sem("setup_taken")
        marker_set = sem("marker_set")
        ident_r_done = sem("ident_r_done")
        q_split = sem("q_split")
        k_split = sem("k_split")
        v_kept = sem("v_kept")
        pmk_split = sem("pmk_split")
        rec_done = sem("rec_done")
        h_biased = sem("h_biased")
        parts_out = [sem(f"parts_out{s}") for s in range(2)]
        q_stacked = [sem(f"q_stacked{s}") for s in range(2)]
        k_stacked = [sem(f"k_stacked{s}") for s in range(2)]
        max_scored = sem("max_scored")
        negm_done = sem("negm_done")
        scored = sem("scored")
        exp_done = sem("exp_done")
        pv_done = sem("pv_done")
        norm_done = sem("norm_done")
        mq_step = sem("mq_step")
        mq_max = sem("mq_max")
        mq_exp = sem("mq_exp")
        mq_norm = sem("mq_norm")
        mq_copied = sem("mq_copied")
        mq_att = sem("mq_att")
        x2n_done = sem("x2n_done")
        x2t_ready = sem("x2t_ready")
        x2t_taken = sem("x2t_taken")
        x2_kept = sem("x2_kept")
        logits_ready = sem("logits_ready")
        logits_taken = sem("logits_taken")
        gap_done = sem("gap_done")
        gap_exp = sem("gap_exp")
        gate_done = sem("gate_done")
        wgrp_done = sem("wgrp_done")
        wT_ready = sem("wT_ready")
        wT_taken = sem("wT_taken")
        b2_ready = sem("b2_ready")
        b2_taken = sem("b2_taken")
        b2_split = sem("b2_split")
        gates_rounded = sem("gates_rounded")
        hid_ready = sem("hid_ready")
        gelu_done = sem("gelu_done")
        y_ready = sem("y_ready")
        y_taken = sem("y_taken")
        stored = sem("stored")

        NQ, NK = 8, 4

        block = ctx.enter_context(nc.Block())

        def groups(eng, step):
            step(0, 0)
            with eng.Fori(1, GROUPS - 4, 2) as g:
                step(g, 1)
                step(g + 1, 0)
            for g in range(GROUPS - 3, GROUPS):
                step(g, g % 2)

        def between(steps, g, e):
            if isinstance(g, int) and g < 3 and e % 2 == 1:
                step = steps.get(4 * g + e // 2 + 1)
                if step:
                    step()

        def ffn_groups(eng, experts):
            for g in range(3):
                experts(g)
            with eng.Fori(3, GROUPS - 1, 1) as g:
                experts(g)
            experts(GROUPS - 1)
            experts(GROUPS, BATCH)

        def part(n):
            return slice(0, EARLY * GB) if n == 0 else slice(EARLY * GB, TILES)

        @block.sync
        def _(sp):
            sp.dma_start(cst[:, :], consts).then_inc(consts_in, 16)
            for d in range(0, PER_CHAN, 2):
                sp.dma_start(conv_sb[:, :, d:d + 2, :], convw[:, :, d:d + 2, :]).then_inc(conv_in[d // 2], 16)
            for g in range(XSLOTS):
                sp.dma_start(x_sb[:, g, :, :], xt[g]).then_inc(x_in[g], 16)
            sp.dma_start(wqkv_sb[:, :, :], wqkv).then_inc(weights_in, 16)
            sp.dma_start(wo_sb[:, :], wo).then_inc(weights_in, 16)

            def x_again(g):
                sp.wait_ge(tok_done, g - XSLOTS + 1)
                sp.dma_start(x_sb[:, g - XSLOTS, :, :], xt[g]).then_inc(x_in[g - XSLOTS], 16)

            x_again(XSLOTS)
            x_again(XSLOTS + 1)
            x_again(XSLOTS + 2)
            sp.wait_ge(pool_memsets, 2)

            def put(which, g):
                for part in range(2):
                    dst = parts_dram[bass.ds(g, 1), which].rearrange("g h a d n -> g a h d n")[0, part]
                    sp.dma_start(dst, split[:, 2 * which + part, :].bitcast(F32)).then_inc(parts_out[which], 16)

            def stack_q(g, s):
                for e in range(2):
                    for j in range(4):
                        row = P // 2 * e + HD * j
                        src = parts_dram[bass.ds(g, 1), 0].rearrange(
                            "g (r e) a d n -> g e a d r n", e=2)[0, e, j // 2]
                        dst = q_stack[s][row:row + HD, e:HEADS:2, :, :].rearrange("p r b t -> p r (b t)")
                        sp.dma_start(dst.bitcast(F32), src).then_inc(q_stacked[s], 16)

            def stack_k(g, s):
                for e in range(2):
                    src = parts_dram[bass.ds(g, 1), 1].rearrange("g (r e) a d n -> g e (a d) r n", e=2)[0, e]
                    for j in range(2):
                        row = P // 2 * e + 2 * HD * j
                        dst = k_stack[s][row:row + 2 * HD, :, :, :].rearrange("p r b t -> p r (b t)")
                        sp.dma_start(dst.bitcast(F32), src).then_inc(k_stacked[s], 16)

            def hold(signal, value):
                sp.wait_ge(signal, value)
                if not isinstance(value, int):
                    sp.sem_inc(sp_held, 1)

            def put_both(g):
                hold(q_split, g + 1)
                put(0, g)
                hold(k_split, g + 1)
                put(1, g)

            def stack_both(g, s, late):
                if late:
                    hold(scored, (g - 1) * GB)
                hold(parts_out[0], (g + 1) * 32)
                stack_q(g, s)
                hold(parts_out[1], (g + 1) * 32)
                stack_k(g, s)

            x_again(XSLOTS + 3)
            put_both(0)
            stack_both(0, 0, False)
            put_both(1)
            stack_both(1, 1, False)
            sp.wait_ge(weff_done, 1)
            sp.wait_ge(bias_sum, 1)
            sp.dma_start(w1_sb[:, :, :], w1).then_inc(ffn_in, 16)
            sp.dma_start(w2_sb[:, :, :], w2).then_inc(ffn_in, 16)
            sp.dma_start(b2_sb[:, :, :], b2bd).then_inc(ffn_in, 16)
            put_both(2)

            def ahead(g, s):
                stack_both(g, s, True)
                put_both(g + 1)
            with sp.Fori(2, GROUPS - 3, 2) as g:
                ahead(g, 0)
                ahead(g + 1, 1)
            ahead(GROUPS - 2, 0)
            stack_both(GROUPS - 1, 1, True)

            def store(g):
                sp.wait_ge(y_taken, (g + 1) * EXPERTS)
                sp.dma_start(out[bass.ds(g * GB, GB), 1:TOKENS + 1, :].rearrange("b t c -> t b c"),
                             h[:, bass.ds(g * GB, GB), :]).then_inc(stored, 16)
            with sp.Fori(0, GROUPS, 1) as g:
                store(g)
            sp.wait_ge(y_taken, (GROUPS + 1) * EXPERTS)
            sp.dma_start(out[:, 0, :], h[0:BATCH, MT, :]).then_inc(stored, 16)
            sp.wait_ge(stored, 16 * (GROUPS + 1))

        @block.gpsimd
        def _(pool):
            def hold(signal, value):
                pool.wait_ge(signal, value)
                if not isinstance(value, int):
                    pool.sem_inc(pool_held, 1)

            for s in range(2):
                pool.memset(q_stack[s][:, :, :, :].bitcast(F32), 0.0).then_inc(pool_memsets, 1)
            pool.memset(v_fix[:, :, :, :, :], 0.0).then_inc(pool_memsets, 1)

            def stage_a(g, s, first):
                hold(xn_done, g + 1)
                if first:
                    pool.wait_ge(marker_set, 1)
                pool.tensor_tensor(h[:, bass.ds(g * GB, GB), :], h[:, bass.ds(g * GB, GB), :],
                                   obias[:, :].rearrange("p (a n) -> p a n", a=1).to_broadcast([P, GB, HID]),
                                   ALU.add).then_inc(h_biased, 1)
                for which, halves in ((0, ("q", "qp")), (1, ("k", "kp"))):
                    x32 = q32[:, :, :] if which == 0 else k_all[:, bass.ds(g * GB, GB), :]
                    done = q_split if which == 0 else k_split
                    hi = split[:, 2 * which, :].rearrange("p (b t) -> p b t", b=GB)
                    lo = split[:, 2 * which + 1, :].rearrange("p (b t) -> p b t", b=GB)
                    hold(taken[halves[0]], g + 1)
                    hold(taken[halves[1]], g + 1)
                    if which == 0 and (not isinstance(g, int) or g >= 1):
                        hold(ready["mk"], g)
                    pool.tensor_tensor(x32, rope_a[:, which], rope_b[:, which],
                                       ALU.add).then_inc(rope_summed, 1)
                    hold(rope_summed, 2 * g + which + 1)
                    if not isinstance(g, int) or g >= 1:
                        hold(parts_out[which], g * 32)
                    pool.tensor_copy(hi, x32).then_inc(rope_high, 1)
                    hold(rope_high, 2 * g + which + 1)
                    pool.tensor_tensor(lo, x32, hi, ALU.subtract).then_inc(done, 1)
                if not isinstance(g, int) or g >= 1:
                    keep_v(g - 1, 1 - s)

            def keep_v(g, s):
                hold(taken["v"], g + 1)
                pool.tensor_tensor(v_all[:, bass.ds(g * GB, GB), :], v_fix[:, s, 0], v_fix[:, s, 1],
                                   ALU.add).then_inc(v_kept, 1)

            stage_a(0, 0, True)
            stage_a(1, 1, False)
            with pool.Fori(2, GROUPS - 1, 2) as g:
                stage_a(g, 0, False)
                stage_a(g + 1, 1, False)
            keep_v(GROUPS - 1, 1)
            def keep(g, s):
                hold(x2t_taken, g + 1)
                pool.tensor_copy(x2T[:, bass.ds(g * GT, GT)], xnT[:, s, :]).then_inc(x2_kept, 1)
            def regroup(g, tiles=GB, rows=P):
                if not isinstance(g, int) or g >= 1:
                    hold(wT_ready, g)
                n = tiles * EXPERTS
                pool.tensor_copy(wgrp[0:rows, :].rearrange("p (c n) -> p c n", c=4)[:, :, 0:n],
                                 gate[0:rows, bass.ds(g * GB, tiles), :].rearrange("p (a b) e -> p a (b e)", a=1)
                                 .to_broadcast([rows, 4, n])).then_inc(wgrp_done, 1)

            with pool.Fori(0, EARLY - 2, 2) as g:
                keep(g, 0)
                keep(g + 1, 1)
            keep(EARLY - 1, 0)
            pool.wait_ge(gate_done, 1)
            regroup(0)
            regroup(1)
            for g in range(EARLY, GROUPS):
                keep(g, g % 2)
            regroup(2)
            regroup(3)
            pool.wait_ge(x2t_taken, GROUPS + 1)
            pool.tensor_copy(x2T[:, GROUPS * GT:], xnT[:, 0, 0:P]).then_inc(x2_kept, 1)
            regroup(4)
            pool.wait_ge(gate_done, 2)
            with pool.Fori(EARLY, GROUPS, 1) as g:
                regroup(g)
            regroup(GROUPS, 1, BATCH)

        @block.scalar
        def _(act):
            act.wait_ge(consts_in, 16)
            nc.scalar.copy(ident_r[:, :], const("ident")).then_inc(ident_r_done, 1)

            def take_x2(g):
                s = g % 2
                act.wait_ge(x2t_ready, g + 1)
                if g >= 2:
                    act.wait_ge(x2_kept, g - 1)
                    act.wait_ge(logits_ready, g - 1)
                nc.scalar.copy(xnT[:, s, :], bank(6)).then_inc(x2t_taken, 1)

            def take_xnT(g, s):
                act.wait_ge(ready["xnT"], g + 1)
                nc.scalar.copy(xnT[:, s, :], bank(6)).then_inc(taken["xnT"], 1)

            def take_v(g, s):
                act.wait_ge(ready["v"], g + 1)
                if not isinstance(g, int) or g >= 2:
                    act.wait_ge(v_kept, g - 1)
                for e in range(2):
                    dst, src = (t.rearrange("p (c e d) -> p e c d", e=2, d=HD)[:, e]
                                for t in (v_fix[:, s, e].rearrange("p b n -> p (b n)"), bank(7)))
                    ins = nc.scalar.copy(dst, src)
                ins.then_inc(taken["v"], 1)

            def take_mk(g, s):
                act.wait_ge(ready["mk"], g + 1)
                nc.scalar.copy(mk_row[:, s, :], bank(7)).then_inc(taken["mk"], 1)

            def take_smk(g):
                act.wait_ge(ready["smk"], g + 1)
                nc.scalar.copy(smk_sb[:, bass.ds(g * GB, GB), :], bank(7).rearrange("p (b n) -> p b n", b=GB)[:, :, 0:HEADS]
                               ).then_inc(taken["smk"], 1)

            def exps(n, b, late):
                act.wait_ge(scored, n + 1)
                if late:
                    act.wait_ge(pv_done, n - 1)
                nc.scalar.activation(probs[:, b % 2].rearrange("p h t -> p (h t)"), bank(2, 2),
                                     ACT.Exp, scale=SCALE).then_inc(probs_exp, 1)
                act.wait_ge(mk_shifted, n + 1)
                mk = mk_less[:, b % 2, :]
                nc.scalar.activation(pmk[:, b % 2, :], mk, ACT.Exp, scale=SCALE)
                at, _ = COLS["hide_high"]
                nc.scalar.activation(pmk_hid[:, b % 2, :], mk, ACT.Exp, bias=cst[:, at:at + 1],
                                     scale=SCALE).then_inc(exp_done, 1)

            def step(g, s):
                static = isinstance(g, int)
                for b in range(GB):
                    if b == 1 and not (static and g + 1 >= GROUPS):
                        take_v(g + 1, 1 - s)
                    exps(g * GB + b, b, not static or g * GB + b >= 2)
                    if b == 0 and not (static and (g == 0 or g + 1 >= GROUPS)):
                        take_mk(g + 1, 1 - s)
                    if b == 0 and not (static and (g == 0 or g + 2 >= GROUPS)):
                        take_xnT(g + 2, s)
                    if b == 3 and not (static and g + 2 >= GROUPS):
                        take_smk(g + 2)
                    if static and g == GROUPS - 2 and b in (1, 2):
                        take_x2(b - 1)
                    if static and g == GROUPS - 1 and b < 3:
                        take_x2(b + 2)

            take_xnT(0, 0)
            take_smk(0)
            take_xnT(1, 1)
            take_mk(0, 0)
            act.wait_ge(pool_memsets, 3)
            take_v(0, 0)
            take_smk(1)
            take_mk(1, 1)
            take_xnT(2, 0)
            groups(act, step)

            def gap_weight(n):
                act.wait_ge(gap_done, n + 1)
                t = part(n)
                nc.scalar.activation(gs[:, 3, t], gs[:, 2, t], ACT.Exp).then_inc(gap_exp, 1)
            gap_weight(0)

            def marker_softmax():
                act.wait_ge(mq_max, 2)
                for half in range(2):
                    nc.scalar.activation(pmq[:, half, :], bank(7)[:, 256 * half:256 * half + P + 1], ACT.Exp,
                                         bias=mq[:, half, 1:2], scale=SCALE,
                                         accum_out=mq[:, half, 2:3]).then_inc(mq_exp, 1)

            def take_last_x2():
                act.wait_ge(x2t_ready, GROUPS + 1)
                act.wait_ge(x2_kept, GROUPS - 1)
                act.wait_ge(logits_ready, GROUPS - 1)
                nc.scalar.copy(xnT[:, 0, 0:P], bank(6)[:, 0:P]).then_inc(x2t_taken, 1)

            marker_softmax()

            def last_gap_weight():
                gap_weight(1)
                at, _ = COLS["b1"]
                nc.scalar.activation(gelu_ready[:, :], cst[:, at:at + 1], ACT.Gelu)

            BETWEEN = {
                1: lambda: take_x2(5), 2: lambda: take_x2(6), 3: lambda: take_x2(7),
                9: take_last_x2, 12: last_gap_weight,
            }

            def gelu(n, e, cols, late):
                act.wait_ge(hid_ready, n + 1)
                if late:
                    act.wait_ge(y_ready, n - 1)
                else:
                    act.wait_ge(pv_done, BATCH)
                at, _ = COLS["b1"]
                nc.scalar.activation(hid[:, e % 2, 0:cols], bank(e % 2)[:, 0:cols], ACT.Gelu,
                                     bias=cst[:, at + e:at + e + 1]).then_inc(gelu_done, 1)

            def experts(g, cols=GT):
                static = isinstance(g, int)
                for e in range(EXPERTS):
                    gelu(g * EXPERTS + e, e, cols, not static or g >= 1 or e >= 2)
                    between(BETWEEN, g, e)
            ffn_groups(act, experts)

        @block.vector
        def _(dve):
            v = nc.vector
            links = [0]

            def link(ins):
                links[0] += 1
                ins.then_inc(dve_chain, 1)
                dve.wait_ge(dve_chain, links[0])

            def layernorm_guess(first, n):
                tiles = bass.ds(first, n)
                me, se, mo, so = (stats[:, tiles, c] for c in (1, 2, 4, 5))
                t = [ln_tmp[:, c, 0:n] for c in range(5)]
                v.tensor_tensor(t[0], me, mo, ALU.add)
                v.tensor_tensor(t[1], me, mo, ALU.subtract)
                link(v.tensor_tensor(t[2], se, so, ALU.add))
                link(v.tensor_tensor(t[3], t[1], t[1], ALU.mult))
                link(v.scalar_tensor_tensor(out=t[1], in0=t[3], scalar=float(HID) / 4, in1=t[2],
                                            op0=ALU.mult, op1=ALU.add))
                link(v.tensor_scalar(t[4], t[1], 1.0 / HID, EPS, ALU.mult, ALU.add))
                link(v.tensor_scalar(rstd[:, tiles].bitcast(I32), t[4].bitcast(I32), -0.5, float(0x5f3759df),
                                     ALU.mult, ALU.add))

            def layernorm_newton(first, n):
                tiles = bass.ds(first, n)
                t = [ln_tmp[:, c, 0:n] for c in range(5)]
                y = rstd[:, tiles]
                for _ in range(3):
                    link(v.tensor_tensor(t[1], y, y, ALU.mult))
                    link(v.scalar_tensor_tensor(out=t[2], in0=t[1], scalar=-0.5, in1=t[4],
                                                op0=ALU.mult, op1=ALU.mult))
                    link(v.scalar_tensor_tensor(out=y, in0=t[2], scalar=1.5, in1=y,
                                                op0=ALU.add, op1=ALU.mult))
                link(v.scalar_tensor_tensor(out=shift[:, tiles], in0=t[0], scalar=-0.5, in1=y,
                                            op0=ALU.mult, op1=ALU.mult))

            def layernorm_scales(first, n):
                layernorm_guess(first, n)
                layernorm_newton(first, n)

            def normalize(dst, n):
                return v.tensor_scalar(dst, h[:, bass.ds(n, 1), :].rearrange("p a n -> p (a n)"),
                                       rstd[:, bass.ds(n, 1)], shift[:, bass.ds(n, 1)], ALU.mult, ALU.add)

            v.memset(ones[:, :], 1.0).then_inc(h_done, 1)
            v.memset(km_pad[:, :], 0.0).then_inc(taken["out"], 1)
            v.memset(qm_shift[:, :], 0.0).then_inc(h_done, 1)
            for s in range(2):
                v.memset(negm[s][:, :].bitcast(F32), 0.0)
            link(v.memset(ones_head[:, :, :], 0.0))
            for e in range(2):
                v.memset(ones_head[:, e, HD * e:HD * e + HD], 1.0)
            v.memset(h[:, MT, :], 0.0).then_inc(memsets_done, 1)
            dve.wait_ge(memsets_done, 1)
            dve.wait_ge(consts_in, 16)
            at, _ = COLS["cw"]
            for d in range(PER_CHAN):
                if d % 2 == 0:
                    dve.wait_ge(conv_in[d // 2], 16)
                for j in range(KCH):
                    w = cst[:, at + j * PER_CHAN + d:at + j * PER_CHAN + d + 1]
                    if d == 0:
                        ins = v.tensor_scalar(weff[:, j, :], conv_sb[:, j, d, :], w, None, ALU.mult)
                    else:
                        ins = v.scalar_tensor_tensor(out=weff[:, j, :], in0=conv_sb[:, j, d, :], scalar=w,
                                                     in1=weff[:, j, :], op0=ALU.mult, op1=ALU.add)
                if d < PER_CHAN - 1:
                    link(ins)
            ins.then_inc(weff_done, 1)
            at, _ = COLS["marker"]
            link(v.tensor_copy(h[0:BATCH, MT, :], cst[0:BATCH, at:at + HID]))
            link(v.bn_stats(stats[:, MT, :], h[:, MT, :]))
            layernorm_scales(MT, 1)
            normalize(xn[:, 1, 0, :], MT).then_inc(setup_xn, 1)
            dve.wait_ge(bias_sum, 1)
            v.tensor_tensor(pe_bias[:, :], bank(2)[:, 0:HID], const("pe"), ALU.add).then_inc(pe_bias_done, 1)
            dve.wait_ge(pe_bias_done, 1)
            def grp(t, g):
                return t[:, bass.ds(g * GB, GB), :]

            def make_xn(g, s):
                if not isinstance(g, int) or g >= 2:
                    dve.wait_ge(ready["xnT"], g - 1)
                for b in range(GB):
                    ins = normalize(xn[:, s, b, :], g * GB + b)
                ins.then_inc(xn_done, 1)

            def tok(g, s):
                dve.wait_ge(tok_done, g + 1)
                v.tensor_tensor(grp(h, g), bank(s).rearrange("p (b n) -> p b n", b=GB),
                                pe_bias[:, :].rearrange("p (a n) -> p a n", a=1).to_broadcast([P, GB, HID]),
                                ALU.add).then_inc(h_done, 1)
                dve.wait_ge(h_done, g + 3)
                for b in range(GB):
                    ins = v.bn_stats(stats[:, bass.ds(g * GB + b, 1), :].rearrange("p a n -> p (a n)"),
                               h[:, bass.ds(g * GB + b, 1), :].rearrange("p a n -> p (a n)"))
                ins.then_inc(stats_done, 1)
            tok(0, 0)
            dve.wait_ge(setup_ready, 1)
            v.tensor_copy(xnT_m[:, :], bank(3)[:, 0:1]).then_inc(setup_taken, 1)
            bias_at, _ = COLS["bias"]
            v.tensor_scalar(bv_wide, ones[:, :], cst[:, bias_at + 4:bias_at + 5], None,
                            ALU.mult).then_inc(setup_taken, 1)
            tok(1, 1)
            dve.wait_ge(stats_done, 2)
            layernorm_scales(0, 2 * GB)
            make_xn(0, 0)
            dve.wait_ge(setup_ready, 2)
            v.tensor_tensor(qm[:, 0:1], bank(3)[:, 0:1], cst[:, bias_at:bias_at + 1], ALU.add)
            link(v.tensor_tensor(qm[:, 1:2], bank(3)[:, 1:2], cst[:, bias_at + 2:bias_at + 3], ALU.add))
            v.tensor_scalar(km_pad[:, :].rearrange("p (a n) -> p a n", a=4)[:, :, 0:HEADS],
                            const("headmask").rearrange("p (a h) -> p a h", a=1).to_broadcast([P, 4, HEADS]),
                            qm[:, 1:2], None, ALU.mult)
            v.tensor_scalar(qm_shift[:, 3 * HEADS:4 * HEADS], const("headmask"), qm[:, 0:1], None, ALU.mult)
            v.tensor_scalar(qm_tiled[:, :, :],
                            const("headmask").rearrange("p (a h) -> p a h", a=1).to_broadcast([P, 16, HEADS]),
                            qm[:, 0:1], None, ALU.mult)
            v.tensor_tensor(obias[:, :], bank(3)[:, 256:384], const("ob"), ALU.add).then_inc(marker_set, 1)
            dve.wait_ge(marker_set, 1)
            v.tensor_tensor(h[0:BATCH, MT, :], h[0:BATCH, MT, :], obias[0:BATCH, :], ALU.add)

            def marker_value():
                at, _ = COLS["low_key"]
                low_key = cst[:, at:at + 1]
                v.tensor_copy(vm_rows[:, :], bank(3)[:, 128:256])
                link(v.tensor_tensor(vm_heads, bank(3)[:, 128:256], const("headrows"), ALU.mult))
                v.scalar_tensor_tensor(out=one_parts[:, :], in0=const("headrows"), scalar=low_key,
                                       in1=const("headrows"), op0=ALU.mult, op1=ALU.subtract)
                link(v.tensor_scalar(vm_hid, vm_heads, low_key, None, ALU.mult))
                v.tensor_tensor(vm_parts[:, :], vm_hid, vm_heads, ALU.subtract).then_inc(marker_set, 1)

            def take(name, g):
                c = ("q", "qp", "k", "kp").index(name)
                bank_of = {"q": 7, "qp": 6, "k": 7, "kp": 6}[name]
                table = const("cos" if c % 2 == 0 else "sin")
                dst = (rope_a if c % 2 == 0 else rope_b)[:, c // 2]
                dve.wait_ge(ready[name], g + 1)
                if not isinstance(g, int) or g >= 1:
                    dve.wait_ge(rope_summed, 2 * g - 1 + c // 2)
                v.scalar_tensor_tensor(out=dst, in0=bank(bank_of).rearrange("p (b t) -> p b t", b=GB),
                                       scalar=cst[:, bias_at + c:bias_at + c + 1],
                                       in1=table.rearrange("p (a t) -> p a t", a=1).to_broadcast([P, GB, TOKENS]),
                                       op0=ALU.add, op1=ALU.mult).then_inc(taken[name], 1)

            def negmax_of(n, b, s, smk_ready, late):
                dve.wait_ge(max_scored, n + 1)
                v.tensor_reduce(negmax[:, b % 2, :], bank(0, 2).rearrange("p (h t) -> p h t", h=HEADS),
                                AX.X, ALU.max, negate=True).then_inc(row_max, 1)
                dve.wait_ge(row_max, n + 1)
                if smk_ready is not None:
                    dve.wait_ge(taken["smk"], smk_ready)
                if late:
                    dve.wait_ge(scored, n - 1)
                wide = [t.rearrange("p (a h) -> p a h", a=1).to_broadcast([P, 4, HEADS])
                        for t in (smk_sb[:, bass.ds(n, 1), :].rearrange("p a h -> p (a h)"),
                                  negmax[:, b % 2, :])]
                v.scalar_tensor_tensor(out=negm[b % 2][:, :].rearrange("p (a n) -> p a n", a=4)[:, :, 0:HEADS],
                                       in0=wide[0], scalar=-1.0, in1=wide[1], op0=ALU.mult, op1=ALU.min
                                       ).then_inc(negm_done, 1)

            def shift_mk(n, b, s, group=None):
                dve.wait_ge(scored, n + 1)
                if group is not None:
                    dve.wait_ge(taken["mk"], group + 1)
                if not isinstance(n, int) or n >= 2:
                    dve.wait_ge(exp_done, n - 1)
                v.tensor_tensor(mk_less[:, b % 2, :], bank(4 + b % 2)[:, 384:512],
                                mk_row[:, s, b * TOKENS:(b + 1) * TOKENS], ALU.add).then_inc(mk_shifted, 1)

            def split_pmk(n, b):
                dve.wait_ge(exp_done, n + 1)
                v.tensor_tensor(pmk_parts[:, b % 2, :], pmk_hid[:, b % 2, :], pmk[:, b % 2, :], ALU.subtract
                                ).then_inc(pmk_split, 1)

            def norm(n, b, s):
                dve.wait_ge(pv_done, n + 1)
                od = bank(4 + b % 2)
                v.reciprocal(rec[:, b % 2, :], od[:, 256:384]).then_inc(rec_done, 1)
                dve.wait_ge(rec_done, n + 1)
                v.tensor_tensor(attT[:, s, b], od[:, 0:TOKENS], rec[:, b % 2, :],
                                ALU.mult).then_inc(norm_done, 1)

            def take_out(g):
                dve.wait_ge(ready["out"], g + 1)
                dve.wait_ge(h_biased, g + 1)
                v.tensor_tensor(grp(h, g), bank(6).rearrange("p (b n) -> p b n", b=GB), grp(h, g),
                                ALU.add).then_inc(taken["out"], 1)
                dve.wait_ge(taken["out"], g + 2)
                for b in range(GB):
                    ins = v.bn_stats(stats[:, bass.ds(g * GB + b, 1), :].rearrange("p a n -> p (a n)"),
                                     h[:, bass.ds(g * GB + b, 1), :].rearrange("p a n -> p (a n)"))
                ins.then_inc(stats_done, 1)

            tok(2, 0)
            take("q", 0)
            take("qp", 0)
            make_xn(1, 1)
            tok(3, 1)
            take("k", 0)
            take("kp", 0)
            tok(4, 0)
            tok(5, 1)
            marker_value()
            dve.wait_ge(stats_done, GROUPS - 2)
            layernorm_scales(2 * GB, (GROUPS - 4) * GB)
            make_xn(2, 0)
            take("q", 1)
            take("qp", 1)
            tok(6, 0)
            take("k", 1)
            take("kp", 1)
            tok(7, 1)
            negmax_of(0, 0, 0, 1, False)
            dve.wait_ge(stats_done, GROUPS)
            layernorm_guess((GROUPS - 2) * GB, 2 * GB)
            negmax_of(1, 1, 0, None, False)

            def x2(g):
                s = g % 2
                if g >= 2:
                    dve.wait_ge(x2t_ready, g - 1)
                else:
                    dve.wait_ge(ready["xnT"], GROUPS)
                for b in range(GB):
                    ins = normalize(xn[:, s, b, :], g * GB + b)
                ins.then_inc(x2n_done, 1)

            def take_logits(g, n=GB):
                dve.wait_ge(logits_ready, g + 1)
                v.tensor_tensor(logits[:, g * GB:g * GB + n, :],
                                bank(7)[:, 0:n * P].rearrange("p (b e) -> p b e", b=n)[:, :, 0:EXPERTS],
                                const("bg").rearrange("p (a e) -> p a e", a=1).to_broadcast([P, n, EXPERTS]),
                                ALU.add).then_inc(logits_taken, 1)

            def wide(t):
                n = t.shape[-1]
                return t.rearrange("p (n a) -> p n a", a=1).to_broadcast([P, n, EXPERTS])

            def best(scores, top, pick, tmp, t):
                n = t.stop - t.start
                rank = const("rank").rearrange("p (a e) -> p a e", a=1).to_broadcast([P, n, EXPERTS])
                link(v.tensor_reduce(top, scores, AX.X, ALU.max))
                link(v.tensor_tensor(tmp, scores, wide(top), ALU.is_equal))
                link(v.tensor_tensor(tmp, tmp, rank, ALU.mult))
                link(v.tensor_reduce(gs[:, 7, t], tmp, AX.X, ALU.max))
                link(v.tensor_tensor(pick, tmp, wide(gs[:, 7, t]), ALU.is_equal))

            def first_best(n):
                t = part(n)
                dve.wait_ge(logits_taken, EARLY if n == 0 else GROUPS + 1)
                best(logits[:, t, :], gs[:, 0, t], gt[:, 0, t], gt[:, 2, t], t)

            def second_best(n):
                t = part(n)
                link(v.scalar_tensor_tensor(out=gt[:, 3, t], in0=gt[:, 0, t], scalar=-3.0e38,
                                            in1=logits[:, t, :], op0=ALU.mult, op1=ALU.add))
                best(gt[:, 3, t], gs[:, 1, t], gt[:, 1, t], gt[:, 2, t], t)
                v.tensor_tensor(gs[:, 2, t], gs[:, 1, t], gs[:, 0, t], ALU.subtract).then_inc(gap_done, 1)

            def gates_from_gap(n):
                t = part(n)
                dve.wait_ge(gap_exp, n + 1)
                link(v.tensor_scalar(gs[:, 4, t], gs[:, 3, t], 1.0, None, ALU.add))
                link(v.reciprocal(gs[:, 5, t], gs[:, 4, t]))
                link(v.tensor_tensor(gs[:, 6, t], gs[:, 5, t], gs[:, 3, t], ALU.mult))
                v.tensor_tensor(gt[:, 2, t], gt[:, 0, t], wide(gs[:, 5, t]), ALU.mult)
                link(v.tensor_tensor(gt[:, 3, t], gt[:, 1, t], wide(gs[:, 6, t]), ALU.mult))
                v.tensor_tensor(gate[:, t, :], gt[:, 2, t], gt[:, 3, t], ALU.add).then_inc(gate_done, 1)
                dve.wait_ge(gate_done, n + 1)

            def dve_step(g, s):
                static = isinstance(g, int)
                first = static and g == 0
                ahead = not (static and g + 2 >= GROUPS)
                last = static and g == GROUPS - 1
                n = g * GB
                shift_mk(n, 0, s, g)
                if not first:
                    norm(n - 1, GB - 1, 1 - s)
                split_pmk(n, 0)
                negmax_of(n + 2, 2, s, None, True)
                if not (static and g + 3 >= GROUPS):
                    make_xn(g + 3, 1 - s)
                if static and g == GROUPS - 2:
                    x2(0)
                if last:
                    dve.wait_ge(stats_done, GROUPS + g - 1)
                    layernorm_scales((g - 3) * GB, 2 * GB)
                shift_mk(n + 1, 1, s)
                norm(n, 0, s)
                split_pmk(n + 1, 1)
                negmax_of(n + 3, 3, s, None, True)
                if static and g == GROUPS - 3:
                    dve.wait_ge(stats_done, GROUPS + g - 1)
                    layernorm_guess(0, (g - 1) * GB)
                if ahead:
                    take("q", g + 2)
                    take("qp", g + 2)
                if static and g == GROUPS - 2:
                    x2(1)
                if last:
                    take_logits(2)
                    x2(4)
                shift_mk(n + 2, 2, s)
                norm(n + 1, 1, s)
                split_pmk(n + 2, 2)
                if not last:
                    negmax_of(n + 4, 0, 1 - s, g + 2, True)
                if last:
                    dve.wait_ge(ffn_in, 48)
                    dve.wait_ge(parts_out[0], GROUPS * 32)
                    at, _ = COLS["low_prob"]
                    link(v.tensor_scalar(b2_parts[:, :, :], b2_sb[:, :, :], cst[:, at:at + 1], None, ALU.mult))
                    v.tensor_tensor(b2_parts[:, :, :], b2_parts[:, :, :], b2_sb[:, :, :],
                                    ALU.subtract).then_inc(b2_split, 1)
                if first:
                    layernorm_newton((GROUPS - 2) * GB, 2 * GB)
                if static and g == GROUPS - 3:
                    layernorm_newton(0, (g - 1) * GB)
                if ahead:
                    take("k", g + 2)
                    take("kp", g + 2)
                if static and g == GROUPS - 2:
                    take_logits(0)
                    x2(2)
                if last:
                    take_logits(3)
                    x2(5)
                shift_mk(n + 3, 3, s)
                norm(n + 2, 2, s)
                split_pmk(n + 3, 3)
                if not last:
                    negmax_of(n + 5, 1, 1 - s, None, True)
                if not first:
                    take_out(g - 1)
                if static and g == GROUPS - 2:
                    take_logits(1)
                    x2(3)
                if last:
                    take_logits(4)

            groups(dve, dve_step)
            first_best(0)
            second_best(0)
            dve.wait_ge(mq_step, 2)
            for half in range(2):
                link(v.tensor_reduce(mq[:, half, 0:1], bank(7)[:, 256 * half:256 * half + P + 1], AX.X, ALU.max))
                v.tensor_scalar(mq[:, half, 1:2], mq[:, half, 0:1], -SCALE, None,
                                ALU.mult).then_inc(mq_max, 1)
            norm(BATCH - 1, 3, 1)
            gates_from_gap(0)
            take_out(GROUPS - 1)

            def last_scales():
                dve.wait_ge(stats_done, 2 * GROUPS)
                layernorm_scales((GROUPS - 2) * GB, 2 * GB)
                x2(6)

            def marker_norm():
                for half in range(2):
                    dve.wait_ge(mq_exp, half + 1)
                    link(v.reciprocal(mq[:, half, 3:4], mq[:, half, 2:3]))
                    v.tensor_scalar(pmq[:, half, :], pmq[:, half, :], mq[:, half, 3:4], None,
                                    ALU.mult).then_inc(mq_norm, 1)

            def marker_copy():
                dve.wait_ge(mq_step, 3)
                v.tensor_copy(pmqT[:, :, :],
                              bank(5)[:, 0:2 * P].rearrange("p (a n) -> p a n", a=2)).then_inc(mq_copied, 1)

            def marker_heads():
                dve.wait_ge(mq_step, 4)
                at, _ = COLS["query_batch"]
                for b in range(GB):
                    for half in range(2):
                        block = bank(6 + half)[:, b * P:(b + 1) * P]
                        w = cst[:, at + b:at + b + 1]
                        if b == 0:
                            ins = v.tensor_scalar(mq_sel[:, half, :], block, w, None, ALU.mult)
                        else:
                            ins = v.scalar_tensor_tensor(out=mq_sel[:, half, :], in0=block, scalar=w,
                                                         in1=mq_sel[:, half, :], op0=ALU.mult, op1=ALU.add)
                    link(ins)
                for half in range(2):
                    ins = v.scalar_tensor_tensor(out=mq_sel[:, half, :], in0=vm_rows[:, :],
                                                 scalar=pmq[:, half, P:P + 1], in1=mq_sel[:, half, :],
                                                 op0=ALU.mult, op1=ALU.add)
                link(ins)
                for half in range(2):
                    ins = v.tensor_tensor(mq_sel[:, half, :], mq_sel[:, half, :], const("query_head"), ALU.mult)
                ins.then_inc(mq_att, 1)

            def marker_att():
                dve.wait_ge(mq_step, 5)
                v.tensor_copy(attT_m[:, :], bank(6)[:, 0:BATCH]).then_inc(mq_att, 1)

            def marker_residual():
                dve.wait_ge(mq_step, 6)
                link(v.tensor_tensor(h[0:BATCH, MT, :], bank(7)[0:BATCH, 0:HID], h[0:BATCH, MT, :], ALU.add))
                link(v.bn_stats(stats[:, MT, :], h[:, MT, :]))
                layernorm_guess(MT, 1)

            def marker_x2():
                layernorm_newton(MT, 1)
                dve.wait_ge(x2t_ready, GROUPS - 1)
                normalize(xn[:, 0, 0, :], MT).then_inc(x2n_done, 1)

            BETWEEN = {
                1: last_scales, 2: lambda: (take_logits(5), x2(7)), 3: lambda: (take_logits(6), marker_norm()),
                4: lambda: (take_logits(7), marker_copy()), 5: marker_heads, 6: marker_att, 7: marker_residual,
                8: marker_x2, 10: lambda: (take_logits(GROUPS, 1), first_best(1)),
                11: lambda: second_best(1), 12: lambda: gates_from_gap(1),
            }

            def add_y(m, e, g, tiles, rows):
                dve.wait_ge(y_ready, m + 1)
                for b in range(tiles):
                    t = h[0:rows, bass.ds(g * GB + b, 1), :].rearrange("p a n -> p (a n)")
                    w = gate[0:rows, bass.ds(g * GB + b, 1), e]
                    ins = v.scalar_tensor_tensor(out=t, in0=bank(2 + e % 2)[0:rows, b * P:b * P + P],
                                                 scalar=w, in1=t, op0=ALU.mult, op1=ALU.add)
                ins.then_inc(y_taken, 1)
                dve.wait_ge(y_taken, m + 1)

            def split_gates(g, cols):
                dve.wait_ge(wT_ready, g + 1)
                at, _ = COLS["low_key"]
                v.tensor_scalar(pmk_hid[:, 0, 0:cols], bank(5)[:, 0:cols], cst[:, at:at + 1], None,
                                ALU.mult).then_inc(gates_rounded, 1)
                dve.wait_ge(gates_rounded, g + 1)
                if not isinstance(g, int) or g >= 1:
                    dve.wait_ge(b2_ready, g)
                v.tensor_tensor(wgrpT[:, 0:cols], pmk_hid[:, 0, 0:cols], bank(5)[:, 0:cols],
                                ALU.subtract).then_inc(wT_taken, 1)

            def add_experts(g, cols=GT):
                tiles, rows = (GB, P) if cols == GT else (1, BATCH)
                for e in range(EXPERTS):
                    add_y(g * EXPERTS + e, e, g, tiles, rows)
                    if e == 0:
                        split_gates(g, rows)
                    between(BETWEEN, g, e)
                    if e == 3:
                        dve.wait_ge(b2_ready, g + 1)
                        t = h[0:rows, bass.ds(g * GB, tiles), :]
                        v.tensor_tensor(t, bank(4)[0:rows, 0:tiles * P].rearrange("p (b n) -> p b n", b=tiles),
                                        t, ALU.add).then_inc(b2_taken, 1)
                        dve.wait_ge(b2_taken, g + 1)

            ffn_groups(dve, add_experts)

        @block.tensor
        def _(pe):
            mm = nc.tensor.matmul
            pe.wait_ge(memsets_done, 1)
            pe.wait_ge(consts_in, 16)
            ident = const("ident")
            ident_at, _ = COLS["ident"]
            at, _ = COLS["cb"]
            for d in range(PER_CHAN):
                if d % 2 == 0:
                    pe.wait_ge(conv_in[d // 2], 16)
                for j in range(KCH):
                    c = at + j * PER_CHAN + d
                    ins = mm(bank(2)[:, 0:HID], cst[:, c:c + 1].to_broadcast([P, P]), conv_sb[:, j, d, :],
                             start=(j == 0 and d == 0), stop=(j == KCH - 1 and d == PER_CHAN - 1))
            ins.then_inc(bias_sum, 1)
            pe.wait_ge(weff_done, 1)

            def tok(g, slot, landed):
                pe.wait_ge(x_in[slot], landed)
                pe.wait_ge(h_done, g + 1)
                for b in range(GB):
                    for j in range(KCH):
                        ins = mm(bank(slot % 2)[:, b * P:(b + 1) * P], x_sb[:, slot, j, b * P:(b + 1) * P],
                                 weff[:, j, :], start=(j == 0), stop=(j == KCH - 1))
                ins.then_inc(tok_done, 1)

            def tok_static(g):
                tok(g, g % XSLOTS, 16 * (g // XSLOTS + 1))

            tok_static(0)
            def setup():
                pe.wait_ge(setup_taken, 2)
                pe.wait_ge(weights_in, 32)
                mm(bank(3)[:, 0:1], wqkv_sb[:, 0, :], xnT_m[:, 0:1], start=True, stop=True)
                mm(bank(3)[:, 1:2], wqkv_sb[:, 2, :], xnT_m[:, 0:1], start=True, stop=True)
                mm(bank(3)[:, 128:256], xnT_m[:, 0:1].to_broadcast([P, P]), wqkv_sb[:, 4, :], start=True, stop=True)
                mm(bank(3)[:, 256:384], bv_wide, wo_sb[:, :], start=True, stop=True).then_inc(setup_ready, 1)

            def transposes(g, s):
                pe.wait_ge(xn_done, g + 1)
                if not isinstance(g, int) or g >= 1:
                    pe.wait_ge(taken["kp"], g)
                if not isinstance(g, int) or g >= 3:
                    pe.wait_ge(taken["out"], g - 2)
                for b in range(GB):
                    ins = nc.tensor.transpose(bank(6)[:, b * P:(b + 1) * P], xn[:, s, b, :], ident)
                ins.then_inc(ready["xnT"], 1)

            def project(name, g, s):
                if name in ("q", "qp"):
                    pe.wait_ge(taken["xnT"], g + 1)
                if name == "q" and (not isinstance(g, int) or g >= 1):
                    pe.wait_ge(taken["v"], g)
                if name in ("k", "kp"):
                    pe.wait_ge(taken[{"k": "q", "kp": "qp"}[name]], g + 1)
                c = ("q", "qp", "k", "kp").index(name)
                mm(bank(7 if c % 2 == 0 else 6), wqkv_sb[:, c, :], xnT[:, s, :], start=True,
                   stop=True).then_inc(ready[name], 1)

            def project_v(g, s):
                pe.wait_ge(taken["mk"], g + 1)
                for b in range(GB):
                    ins = mm(bank(7)[:, b * P:(b + 1) * P], xnT[:, s, b * P:(b + 1) * P], wqkv_sb[:, 4, :],
                             start=True, stop=True)
                ins.then_inc(ready["v"], 1)

            def marker_row(g):
                pe.wait_ge(taken["smk"], g + 1)
                pe.wait_ge(q_split, g + 1)
                mm(bank(7), km_pad[:, :], q32[:, :, :].rearrange("p b t -> p (b t)"), start=True,
                   stop=True).then_inc(ready["mk"], 1)

            def marker_scores(g):
                pe.wait_ge(taken["k"], g + 1)
                pe.wait_ge(q_split, g + 1)
                for b in range(GB):
                    ins = mm(bank(7)[:, b * P:(b + 1) * P], q32[:, b, :], km_pad[:, :],
                             start=True, stop=True)
                ins.then_inc(ready["smk"], 1)

            def project_out(g, s, x2_before=0):
                pe.wait_ge(norm_done, (g + 1) * GB)
                if isinstance(g, int) and g == GROUPS - 1:
                    pe.wait_ge(taken["out"], g + 1)
                elif x2_before:
                    pe.wait_ge(x2t_taken, x2_before)
                else:
                    pe.wait_ge(taken["kp"], g + 4)
                for b in range(GB):
                    ins = mm(bank(6)[:, b * P:(b + 1) * P], attT[:, s, b, :], wo_sb[:, :], start=True, stop=True)
                ins.then_inc(ready["out"], 1)

            def score_max(n, b, s, landed):
                if landed is not None:
                    pe.wait_ge(q_stacked[s], landed[0])
                    pe.wait_ge(k_stacked[s], landed[1])
                if not (isinstance(n, int) and n == 0):
                    pe.wait_ge(negm_done, n)
                for hd in range(HEADS):
                    ins = mm(bank(hd // 4)[:, hd % 4 * P:(hd % 4 + 1) * P], q_stack[s][:, hd, b, :],
                             k_stack[s][:, hd // 2, b, :], start=True, stop=True)
                ins.then_inc(max_scored, 1)

            def score(n, b, s):
                pe.wait_ge(negm_done, n + 1)
                if not (isinstance(n, int) and n == 0):
                    pe.wait_ge(probs_exp, n)
                nm = negm[b % 2]
                for r in range(HEADS // 2):
                    at = r % 2 * 2 * P
                    mm(bank(2 + r // 2)[:, at:at + 2 * P], k_stack[s][:, r, b, :],
                       q_stack[s][:, 2 * r:2 * r + 2, b, :], start=True, stop=False)
                    for e in range(2):
                        mm(bank(2 + r // 2)[:, at + e * P:at + (e + 1) * P],
                           nm[:, 2 * r + e:2 * r + e + 1].to_broadcast([P, P]), ident_r[:, :],
                           start=False, stop=(e == 1))
                if not isinstance(n, int) or n >= 2:
                    pe.wait_ge(norm_done, n - 1)
                mk = bank(4 + b % 2)[:, 384:512]
                mm(mk, nm[:, :], ident_r[:, :], start=True, stop=True).then_inc(scored, 1)

            def weigh(n, b, s):
                pe.wait_ge(exp_done, n + 1)
                pe.wait_ge(pmk_split, n + 1)
                od = bank(4 + b % 2)
                mm(od[:, 0:TOKENS], vm_parts[:, :], pmk_parts[:, b % 2, :], start=True, stop=False)
                for e in range(2):
                    for r in range(HEADS // 2):
                        mm(od[32 * r:32 * r + 32, 0:TOKENS], v_fix[:, s, e, b, 32 * r:32 * r + 32],
                           probs[:, b % 2, 2 * r + e, :], start=False, stop=(e == 1))
                mm(od[:, 256:384], one_parts[:, :], pmk_parts[:, b % 2, :], start=True, stop=False)
                for e in range(2):
                    for r in range(HEADS // 2):
                        ins = mm(od[32 * r:32 * r + 32, 256:384], ones_head[:, e, :],
                                 probs[:, b % 2, 2 * r + e, :], start=False, stop=(e == 1))
                ins.then_inc(pv_done, 1)

            def x2(g, before=None, count=None):
                s = g % 2
                pe.wait_ge(x2n_done, g + 1)
                if before is not None:
                    pe.wait_ge(before, count)
                else:
                    pe.wait_ge(x2t_taken, g)
                for b in range(GB):
                    ins = nc.tensor.transpose(bank(6)[:, b * P:(b + 1) * P], xn[:, s, b, :], ident)
                ins.then_inc(x2t_ready, 1)

            wg_at, _ = COLS["wg"]

            def gate_logits(g, before=None, tiles=GB):
                s = g % 2
                pe.wait_ge(x2t_taken, g + 1)
                if g == 0:
                    pe.wait_ge(taken["v"], GROUPS)
                else:
                    pe.wait_ge(logits_taken, g)
                if before is not None:
                    pe.wait_ge(*before)
                for b in range(tiles):
                    ins = mm(bank(7)[:, b * P:(b + 1) * P], xnT[:, s, b * P:(b + 1) * P],
                             cst[:, wg_at:wg_at + P], start=True, stop=True)
                ins.then_inc(logits_ready, 1)

            def landed(g, s):
                if isinstance(g, int):
                    return 16 * NQ * (g // 2 + 1), 16 * NK * (g // 2 + 1)
                return (g - s) * (8 * NQ) + 16 * NQ, (g - s) * (8 * NK) + 16 * NK

            pe.wait_ge(setup_xn, 1)
            nc.tensor.transpose(bank(3)[:, 0:P], xn[:, 1, 0, :], ident).then_inc(setup_ready, 1)
            tok_static(1)
            setup()
            tok_static(2)
            tok_static(3)
            transposes(0, 0)
            project("q", 0, 0)
            project("qp", 0, 0)
            tok_static(4)
            project("k", 0, 0)
            project("kp", 0, 0)
            tok_static(5)
            pe.wait_ge(marker_set, 1)
            marker_scores(0)
            transposes(1, 1)
            marker_row(0)
            tok_static(6)
            project_v(0, 0)
            for name in ("q", "qp", "k", "kp"):
                project(name, 1, 1)
            tok_static(7)
            pe.wait_ge(ident_r_done, 1)
            pe.wait_ge(h_done, GROUPS + 2)
            score_max(0, 0, 0, landed(0, 0))
            marker_scores(1)
            marker_row(1)
            transposes(2, 0)
            score_max(1, 1, 0, None)
            pe.wait_ge(marker_set, 2)

            def step(g, s):
                static = isinstance(g, int)
                first = static and g == 0
                ahead = not (static and g + 2 >= GROUPS)
                last = static and g == GROUPS - 1
                n = g * GB
                score(n, 0, s)
                if not (first or last):
                    marker_row(g + 1)
                if not first:
                    weigh(n - 1, GB - 1, 1 - s)
                score_max(n + 2, 2, s, None)
                if ahead and not first:
                    transposes(g + 2, s)
                if last:
                    x2(2, taken["out"], g)
                score(n + 1, 1, s)
                if not last:
                    project_v(g + 1, 1 - s)
                weigh(n, 0, s)
                score_max(n + 3, 3, s, None)
                if ahead:
                    project("q", g + 2, s)
                    project("qp", g + 2, s)
                elif not last:
                    x2(0, taken["out"], g)
                else:
                    gate_logits(2)
                    x2(3)
                score(n + 2, 2, s)
                weigh(n + 1, 1, s)
                if not last:
                    score_max(n + 4, 0, 1 - s, landed(g + 1, 1 - s))
                if ahead:
                    project("k", g + 2, s)
                    project("kp", g + 2, s)
                elif not last:
                    gate_logits(0)
                    x2(1)
                else:
                    gate_logits(3)
                    x2(4)
                score(n + 3, 3, s)
                weigh(n + 2, 2, s)
                if not last:
                    score_max(n + 5, 1, 1 - s, None)
                if not first:
                    project_out(g - 1, 1 - s, {GROUPS - 2: 2, GROUPS - 1: 5}[g] if not ahead else 0)
                if ahead:
                    marker_scores(g + 2)
                else:
                    gate_logits(1 if not last else 4)

            def hidden(n, e, g, cols, late):
                if late:
                    pe.wait_ge(gelu_done, n - 1)
                mm(bank(e % 2)[:, 0:cols], w1_sb[:, e, :], x2T[:, bass.ds(g * GT, cols)], start=True,
                   stop=True).then_inc(hid_ready, 1)

            groups(pe, step)
            pe.wait_ge(ffn_in, 48)
            pe.wait_ge(x2_kept, 1)
            hidden(0, 0, 0, GT, False)
            pe.wait_ge(logits_taken, EARLY)
            for half in range(2):
                at = 256 * half
                for i in range(4):
                    for t in range(4):
                        mm(bank(7)[32 * t:32 * t + 32, at:at + P], qm_shift[:, HEADS * (3 - i):HEADS * (3 - i) + 32],
                           k_all[:, 16 * half + 4 * t + i, :], start=(i == 0), stop=(i == 3))
                mm(bank(7)[:, at + P:at + P + 1], qm_tiled[:, :, :].rearrange("p a h -> p (a h)"), qm[:, 1:2],
                   start=True, stop=True).then_inc(mq_step, 1)

            weigh(BATCH - 1, 3, 1)
            hidden(1, 1, 0, GT, False)
            project_out(GROUPS - 1, 1)

            def marker_transposes():
                pe.wait_ge(wT_taken, 1)
                pe.wait_ge(mq_norm, 2)
                for half in range(2):
                    ins = nc.tensor.transpose(bank(5)[:, half * P:(half + 1) * P], pmq[:, half, 0:P], ident)
                ins.then_inc(mq_step, 1)

            def marker_values():
                pe.wait_ge(mq_copied, 1)
                pe.wait_ge(x2t_taken, GROUPS)
                pe.wait_ge(logits_taken, GROUPS)
                pe.wait_ge(v_kept, GROUPS)
                for g in range(GROUPS):
                    ins = mm(bank(6 + g // 4)[g % 4 * 32:g % 4 * 32 + 32, :],
                             pmqT[:, g // 4, g % 4 * 32:g % 4 * 32 + 32],
                             v_all[:, g * GB:(g + 1) * GB, :].rearrange("p b n -> p (b n)"), start=True, stop=True)
                ins.then_inc(mq_step, 1)

            def marker_sums():
                at, _ = COLS["query_row"]
                pe.wait_ge(mq_att, 1)
                for half in range(2):
                    ins = mm(bank(6)[:, 16 * half:16 * half + 16], mq_sel[:, half, :], cst[:, at:at + 16],
                             start=True, stop=True)
                ins.then_inc(mq_step, 1)

            def marker_out():
                pe.wait_ge(mq_att, 2)
                mm(bank(7)[0:BATCH, 0:HID], attT_m[:, :], wo_sb[:, :], start=True, stop=True).then_inc(mq_step, 1)

            def last_x2():
                pe.wait_ge(x2n_done, GROUPS + 1)
                nc.tensor.transpose(bank(6)[:, 0:P], xn[:, 0, 0, :], ident).then_inc(x2t_ready, 1)

            BETWEEN = {
                1: lambda: x2(5, taken["out"], GROUPS + 1), 2: lambda: (gate_logits(5, (mq_exp, 2)), x2(6)),
                3: lambda: (gate_logits(6), x2(7)), 4: lambda: (gate_logits(7), marker_transposes()),
                5: marker_values, 6: marker_sums, 7: marker_out, 9: last_x2,
                10: lambda: gate_logits(GROUPS, None, 1),
            }

            def expert_out(n, e, tiles, rows, late):
                pe.wait_ge(gelu_done, n + 1)
                if late:
                    pe.wait_ge(y_taken, n - 1)
                for b in range(tiles):
                    ins = mm(bank(2 + e % 2)[0:rows, b * P:(b + 1) * P], hid[:, e % 2, b * P:b * P + rows],
                             w2_sb[:, e, :], start=True, stop=True)
                ins.then_inc(y_ready, 1)

            def gates_up(g, tiles, rows, late):
                if isinstance(g, int) and g == 1:
                    pe.wait_ge(mq_copied, 1)
                pe.wait_ge(wgrp_done, g + 1)
                if late:
                    pe.wait_ge(wT_taken, g)
                mm(bank(5)[:, 0:rows], wgrp[0:rows, :], cst[0:rows, ident_at:ident_at + rows], start=True,
                   stop=True).then_inc(wT_ready, 1)

            def second_bias(g, tiles, rows, late):
                if not late:
                    pe.wait_ge(b2_split, 1)
                pe.wait_ge(wT_taken, g + 1)
                if late:
                    pe.wait_ge(b2_taken, g)
                mm(bank(4)[0:rows, 0:tiles * P], wgrpT[:, 0:rows],
                   b2_parts[:, 0:tiles, :].rearrange("p b n -> p (b n)"), start=True,
                   stop=True).then_inc(b2_ready, 1)

            def experts(g, cols=GT):
                tiles, rows = (GB, P) if cols == GT else (1, BATCH)
                first = isinstance(g, int) and g == 0
                for e in range(EXPERTS):
                    n = g * EXPERTS + e
                    if e < EXPERTS - 1 and not (first and e == 0):
                        hidden(n + 1, e + 1, g, cols, True)
                    elif e == EXPERTS - 1 and cols == GT:
                        pe.wait_ge(x2_kept, g + 2)
                        hidden(n + 1, 0, g + 1, BATCH if isinstance(g, int) and g == GROUPS - 1 else GT, True)
                    expert_out(n, e, tiles, rows, not first or e >= 2)
                    if e == 0:
                        gates_up(g, tiles, rows, not first)
                    if e == 2:
                        second_bias(g, tiles, rows, not first)
                    between(BETWEEN, g, e)

            ffn_groups(pe, experts)


def kernel(**inputs):
    from concourse import bacc
    from concourse.bass_utils import run_bass_kernel_spmd

    a = {n: np.asarray(t) for n, t in inputs.items()}
    f = np.float32

    x = a["x"].reshape(GROUPS, GB, TOKENS, KCH, P).transpose(0, 4, 3, 1, 2)
    conv = a["L0_tok_conv_w"].reshape(HID, MAX_CHANS, PER_CHAN, PATCH)[:, :CHANS]
    conv = conv.transpose(3, 1, 2, 0).reshape(KCH, P, PER_CHAN, HID).transpose(1, 0, 2, 3)

    def chan(t):
        return np.tile(t[:CHANS], (PATCH, 1)).reshape(KCH, P, PER_CHAN).transpose(1, 0, 2).reshape(P, -1)

    def rows(t):
        return np.broadcast_to(t, (P, t.shape[-1]))

    pos = np.arange(TOKENS, dtype=f)[:, None]
    freq = np.exp(-(f(2) * np.arange(HID // 2, dtype=f)[None] / f(HID)) * np.log(f(10000.0)))
    angle = pos * freq
    pe = np.stack([np.sin(angle), np.cos(angle)], -1).reshape(TOKENS, HID)
    half = HD // 2
    inv = f(1) / f(10000.0) ** (np.arange(0, HD, 2, dtype=f) / f(HD))
    angle = np.arange(1, TOKENS + 1, dtype=f)[None] * inv[:, None]
    cos, sin = np.cos(angle), np.sin(angle)
    sin[:half // 2] *= -1
    cos, sin = (np.tile(t, (P // half, 1)) for t in (cos, sin))
    head = np.arange(P)[:, None] // HD == np.arange(HEADS)[None]
    headrows = np.zeros((P, P), f)
    for block in range(4):
        headrows[32 * block:32 * block + HEADS] = head.T
    swap = np.arange(P) ^ (half // 2)

    w, b = a["L0_attn_qkv_w"].reshape(3, P, HID), a["L0_attn_qkv_b"].reshape(3, P)
    wqkv = np.stack([w[0], w[0][swap], w[1], w[1][swap], w[2]]).transpose(2, 0, 1)
    bias = np.stack([b[0], b[0][swap], b[1], b[1][swap], b[2]], 1)
    parts = {
        "pe": pe, "cos": cos, "sin": sin, "ident": np.eye(P, dtype=f), "headmask": head.astype(f),
        "headrows": headrows, "rank": rows(np.arange(EXPERTS, 0, -1, dtype=f)),
        "cw": chan(a["L0_tok_chan_w"]), "cb": chan(a["L0_tok_chan_b"]),
        "marker": rows(a["L0_tok_marker"]), "bias": bias, "ob": rows(a["L0_attn_out_b"]),
        "bg": rows(a["L0_ffn_bg"]), "wg": a["L0_ffn_Wg"], "b1": a["L0_ffn_b1"].T,
        "query_head": (np.arange(P)[:, None] % HEADS == np.arange(HID)[None] // HD).astype(f),
        "query_batch": (np.arange(P)[:, None] // HEADS % GB == np.arange(GB)[None]).astype(f),
        "query_row": (np.arange(P)[:, None] // HEADS == np.arange(16)[None]).astype(f),
        "low_key": (np.arange(P) // 64 == 1).astype(f)[:, None],
        "low_prob": (np.arange(P) // 32 % 2 == 1).astype(f)[:, None],
        "hide_high": np.where(np.arange(P) // 32 % 2 == 0, f(-1e30), f(0))[:, None],
    }
    b2bd = np.zeros((P, GB, HID), f)
    for t in range(P // EXPERTS):
        b2bd[t * EXPERTS:(t + 1) * EXPERTS, t % GB] = a["L0_ffn_b2"]
    arrays = {
        "xt": x, "convw": conv, "consts": np.concatenate([parts[n] for n in COLS], 1).astype(f),
        "wqkv": wqkv, "wo": a["L0_attn_out_w"].T, "w1": a["L0_ffn_W1"].transpose(1, 0, 2),
        "w2": a["L0_ffn_W2"].transpose(1, 0, 2), "b2bd": b2bd,
    }
    arrays = {n: np.ascontiguousarray(t) for n, t in arrays.items()}
    nc = bacc.Bacc("TRN2", target_bir_lowering=False, num_devices=1)
    args = [nc.dram_tensor(n, t.shape, mybir.dt.from_np(t.dtype), kind="ExternalInput").ap()
            for n, t in arrays.items()]
    out = nc.dram_tensor("out", (BATCH, TOKENS + 1, HID), F32, kind="ExternalOutput").ap()
    audio_tower_kernel(nc, *args, out)
    r = run_bass_kernel_spmd(nc, [arrays], core_ids=[0])
    return r.results[0]["out"]
```
